# Optimizing a Trainium2 kernel written in Bass

```python
import numpy as np
import jax
import jax.numpy as jnp

def _softmax(x, axis=-1):
    return jax.nn.softmax(x, axis=axis)

def _gelu(x):
    return jax.nn.gelu(x, approximate=True)

def _silu(x):
    return jax.nn.silu(x)

def _sigmoid(x):
    return jax.nn.sigmoid(x)

def _layernorm(x, axis=-1, eps=1e-05):
    m = jnp.mean(x, axis=axis, keepdims=True)
    v = jnp.var(x, axis=axis, keepdims=True)
    return (x - m) / jnp.sqrt(v + eps)

def _scatter_add(tgt, idx, src, axis=0):
    return tgt.at[idx].add(src)

def _segment_sum(src, seg, n):
    return jax.ops.segment_sum(src, seg, n)
kernel_name = 'mk_gnn_preln_d4_gnn_r64_4825a6'

def setup_inputs(seed: int=0):
    np.random.seed(seed)
    _w = jnp.asarray

    def _rec_inputs():
        import jax
        import jax.numpy as jnp
        _gk = jax.random.key(seed)
        x = -0.0005121 + 1.001 * jax.random.normal(jax.random.fold_in(_gk, 1), (50000, 64), jnp.float32)
        src = jax.random.randint(jax.random.fold_in(_gk, 2), (25000,), 0, 50000, jnp.int32)
        dst = jax.random.randint(jax.random.fold_in(_gk, 3), (25000,), 0, 50000, jnp.int32)
        _o = jnp.argsort(dst, stable=True)
        src = src[_o]
        dst = dst[_o]
        edge_attr_2 = jax.random.uniform(jax.random.fold_in(_gk, 12), (25000, 2), jnp.float32, 0.0, 1)
        edge_attr_8 = -4.12889e-05 + 1 * jax.random.normal(jax.random.fold_in(_gk, 13), (25000, 8), jnp.float32)
        edge_weight = jax.random.uniform(jax.random.fold_in(_gk, 15), (25000,), jnp.float32, 0.0, 0.999999)
        return (x, src, dst, edge_attr_2, edge_attr_8, edge_weight)
    x, src, dst, edge_attr_2, edge_attr_8, edge_weight = _rec_inputs()

    def _L0_gnn_setup():
        import jax, jax.numpy as jnp
        import numpy as np
        N = 50000
        E = 12500
        D_IN = 64
        D_OUT = 64
        P = 2
        M = 1
        EPS = 1e-10
        LN_EPS = 1e-05

        def _layer_norm(v):
            mu = jnp.mean(v, axis=-1, keepdims=True)
            var = jnp.var(v, axis=-1, keepdims=True)
            return (v - mu) * jax.lax.rsqrt(var + LN_EPS)
        key = jax.random.key(seed)
        ks = jax.random.split(key, 6)
        x = jax.random.normal(ks[0], (N, D_IN), dtype=jnp.float32)
        edge_index = jax.random.randint(ks[1], (2, E), 0, N, dtype=jnp.int64)
        s = 1.0 / np.sqrt(D_IN)
        W1 = jax.random.uniform(ks[2], (D_IN, D_OUT), jnp.float32, -s, s)
        b1 = jax.random.uniform(ks[3], (D_OUT,), jnp.float32, -s, s)
        W2 = jax.random.uniform(ks[4], (D_IN, D_OUT), jnp.float32, -s, s)
        b2 = jax.random.uniform(ks[5], (D_OUT,), jnp.float32, -s, s)
        return {'x': x, 'edge_index': edge_index, 'W1': W1, 'b1': b1, 'W2': W2, 'b2': b2}
    _L0_gnn_all = _L0_gnn_setup()
    _L0_gnn_in = {k: v for k, v in _L0_gnn_all.items() if k in ('W1', 'b1', 'W2', 'b2')}
    del _L0_gnn_all

    def _L1_gnn_setup():
        import jax, jax.numpy as jnp
        import numpy as np
        N_NODES = 50000
        N_EDGES = 12500
        D = 64
        N_BASIS = 8
        key = jax.random.key(seed)
        ks = jax.random.split(key, 16)
        inp = {'p': jax.random.normal(ks[0], (N_NODES, D), dtype=jnp.float32), 'idx_i': jax.random.randint(ks[1], (N_EDGES,), 0, N_NODES), 'idx_j': jax.random.randint(ks[2], (N_EDGES,), 0, N_NODES), 'basis': jax.random.normal(ks[3], (N_EDGES, N_BASIS), dtype=jnp.float32), 'pp_W1': jax.random.normal(ks[4], (D, D), dtype=jnp.float32) / np.sqrt(D), 'pp_b1': jnp.zeros((D,), dtype=jnp.float32), 'pp_W2': jax.random.normal(ks[5], (D, D), dtype=jnp.float32) / np.sqrt(D), 'pp_b2': jnp.zeros((D,), dtype=jnp.float32), 'pi_W1': jax.random.normal(ks[6], (2 * D, D), dtype=jnp.float32) / np.sqrt(2 * D), 'pi_b1': jnp.zeros((D,), dtype=jnp.float32), 'pi_W2': jax.random.normal(ks[7], (D, D), dtype=jnp.float32) / np.sqrt(D), 'pi_b2': jnp.zeros((D,), dtype=jnp.float32), 'pi_W3': jax.random.normal(ks[8], (D, D * N_BASIS), dtype=jnp.float32) / np.sqrt(D), 'ii_W1': jax.random.normal(ks[9], (D, D), dtype=jnp.float32) / np.sqrt(D), 'ii_b1': jnp.zeros((D,), dtype=jnp.float32), 'ii_W2': jax.random.normal(ks[10], (D, D), dtype=jnp.float32) / np.sqrt(D), 'ii_b2': jnp.zeros((D,), dtype=jnp.float32)}
        return inp
    _L1_gnn_all = _L1_gnn_setup()
    _L1_gnn_in = {k: v for k, v in _L1_gnn_all.items() if k in ('pp_W1', 'pp_b1', 'pp_W2', 'pp_b2', 'pi_W1', 'pi_b1', 'pi_W2', 'pi_b2', 'pi_W3', 'ii_W1', 'ii_b1', 'ii_W2', 'ii_b2')}
    del _L1_gnn_all

    def _L2_gnn_setup():
        import jax, jax.numpy as jnp
        import numpy as np
        N, E, D = (100000, 25000, 64)
        K_PROP = 10
        ALPHA = 0.1
        UNITS = [256, 64]

        def _gcn_norm(edge_index, edge_weight, num_nodes):
            loop = jnp.arange(num_nodes, dtype=edge_index.dtype)
            row = jnp.concatenate([edge_index[0], loop])
            col = jnp.concatenate([edge_index[1], loop])
            w = jnp.concatenate([edge_weight, jnp.ones((num_nodes,), edge_weight.dtype)])
            deg = jax.ops.segment_sum(w, row, num_segments=num_nodes)
            dinv = jax.lax.rsqrt(jnp.maximum(deg, 1e-12))
            return (row, col, dinv[row] * w * dinv[col])

        def _ssgc_propagate(x, row, col, w):
            n = x.shape[0]

            def step(carry, _):
                h, acc = carry
                h = jax.ops.segment_sum(w[:, None] * h[col], row, num_segments=n)
                return ((h, acc + h), None)
            (_, acc), _ = jax.lax.scan(step, (x, jnp.zeros_like(x)), None, length=K_PROP)
            return ALPHA * x + (1.0 - ALPHA) * acc / K_PROP
        key = jax.random.key(seed)
        ks = jax.random.split(key, 6)
        x = jax.random.normal(ks[0], (N, D), dtype=jnp.float32)
        edge_index = jax.random.randint(ks[1], (2, E), 0, N, dtype=jnp.int32)
        edge_weight = jax.random.uniform(ks[2], (E,), dtype=jnp.float32)
        W0 = jax.random.normal(ks[3], (D, UNITS[0]), dtype=jnp.float32) * (1.0 / np.sqrt(D))
        b0 = jnp.zeros((UNITS[0],), jnp.float32)
        W1 = jax.random.normal(ks[4], (UNITS[0], UNITS[1]), dtype=jnp.float32) * (1.0 / np.sqrt(UNITS[0]))
        b1 = jnp.zeros((UNITS[1],), jnp.float32)
        return {'x': x, 'edge_index': edge_index, 'edge_weight': edge_weight, 'W0': W0, 'b0': b0, 'W1': W1, 'b1': b1}
    _L2_gnn_all = _L2_gnn_setup()
    _L2_gnn_in = {k: v for k, v in _L2_gnn_all.items() if k in ('W0', 'b0', 'W1', 'b1')}
    del _L2_gnn_all

    def _L3_gnn_setup():
        import jax, jax.numpy as jnp
        import numpy as np
        K = 5

        def spline_conv(x, edge_index, pseudo, W, root, bias):
            N = x.shape[0]
            src, dst = (edge_index[0], edge_index[1])
            xk = jnp.einsum('ni,kio->nko', x, W)
            v = pseudo * (K - 1)
            bot = jnp.floor(v)
            frac = v - bot
            bot = bot.astype(jnp.int32)
            msg = jnp.zeros((src.shape[0], W.shape[2]), dtype=x.dtype)
            for s0 in (0, 1):
                for s1 in (0, 1):
                    b0 = frac[:, 0] if s0 else 1.0 - frac[:, 0]
                    b1 = frac[:, 1] if s1 else 1.0 - frac[:, 1]
                    basis = b0 * b1
                    idx = jnp.clip(bot[:, 0] + s0, 0, K - 1) + K * jnp.clip(bot[:, 1] + s1, 0, K - 1)
                    msg = msg + basis[:, None] * xk[src, idx]
            agg = jax.ops.segment_max(msg, dst, num_segments=N)
            agg = jnp.where(jnp.isfinite(agg), agg, jnp.zeros_like(agg))
            return agg + x @ root + bias
        key = jax.random.key(seed)
        ks = jax.random.split(key, 8)
        N, E, C = (50000, 25000, 64)
        Cin = C
        s = 1.0 / np.sqrt(25 * Cin)
        return {'x': jax.random.normal(ks[0], (N, C), dtype=jnp.float32), 'edge_index': jax.random.randint(ks[1], (2, E), 0, N, dtype=jnp.int32), 'edge_attr': jax.random.uniform(ks[2], (E, 2), dtype=jnp.float32), 'W1': jax.random.normal(ks[3], (25, C, C), dtype=jnp.float32) * s, 'root1': jax.random.normal(ks[4], (C, C), dtype=jnp.float32) / np.sqrt(C), 'bias1': jnp.zeros((C,), dtype=jnp.float32), 'W2': jax.random.normal(ks[5], (25, C, C), dtype=jnp.float32) * s, 'root2': jax.random.normal(ks[6], (C, C), dtype=jnp.float32) / np.sqrt(C), 'bias2': jnp.zeros((C,), dtype=jnp.float32)}
    _L3_gnn_all = _L3_gnn_setup()
    _L3_gnn_in = {k: v for k, v in _L3_gnn_all.items() if k in ('W1', 'root1', 'bias1', 'W2', 'root2', 'bias2')}
    del _L3_gnn_all
    return {'x': x, 'src': src, 'dst': dst, 'edge_attr_2': edge_attr_2, 'edge_attr_8': edge_attr_8, 'edge_weight': edge_weight, 'L0_gnn_W1': _L0_gnn_in['W1'], 'L0_gnn_b1': _L0_gnn_in['b1'], 'L0_gnn_W2': _L0_gnn_in['W2'], 'L0_gnn_b2': _L0_gnn_in['b2'], 'L1_gnn_pp_W1': _L1_gnn_in['pp_W1'], 'L1_gnn_pp_b1': _L1_gnn_in['pp_b1'], 'L1_gnn_pp_W2': _L1_gnn_in['pp_W2'], 'L1_gnn_pp_b2': _L1_gnn_in['pp_b2'], 'L1_gnn_pi_W1': _L1_gnn_in['pi_W1'], 'L1_gnn_pi_b1': _L1_gnn_in['pi_b1'], 'L1_gnn_pi_W2': _L1_gnn_in['pi_W2'], 'L1_gnn_pi_b2': _L1_gnn_in['pi_b2'], 'L1_gnn_pi_W3': _L1_gnn_in['pi_W3'], 'L1_gnn_ii_W1': _L1_gnn_in['ii_W1'], 'L1_gnn_ii_b1': _L1_gnn_in['ii_b1'], 'L1_gnn_ii_W2': _L1_gnn_in['ii_W2'], 'L1_gnn_ii_b2': _L1_gnn_in['ii_b2'], 'L2_gnn_W0': _L2_gnn_in['W0'], 'L2_gnn_b0': _L2_gnn_in['b0'], 'L2_gnn_W1': _L2_gnn_in['W1'], 'L2_gnn_b1': _L2_gnn_in['b1'], 'L3_gnn_W1': _L3_gnn_in['W1'], 'L3_gnn_root1': _L3_gnn_in['root1'], 'L3_gnn_bias1': _L3_gnn_in['bias1'], 'L3_gnn_W2': _L3_gnn_in['W2'], 'L3_gnn_root2': _L3_gnn_in['root2'], 'L3_gnn_bias2': _L3_gnn_in['bias2']}

def reference(x, src, dst, edge_attr_2, edge_attr_8, edge_weight, L0_gnn_W1, L0_gnn_b1, L0_gnn_W2, L0_gnn_b2, L1_gnn_pp_W1, L1_gnn_pp_b1, L1_gnn_pp_W2, L1_gnn_pp_b2, L1_gnn_pi_W1, L1_gnn_pi_b1, L1_gnn_pi_W2, L1_gnn_pi_b2, L1_gnn_pi_W3, L1_gnn_ii_W1, L1_gnn_ii_b1, L1_gnn_ii_W2, L1_gnn_ii_b2, L2_gnn_W0, L2_gnn_b0, L2_gnn_W1, L2_gnn_b1, L3_gnn_W1, L3_gnn_root1, L3_gnn_bias1, L3_gnn_W2, L3_gnn_root2, L3_gnn_bias2):
    import jax
    import jax.numpy as jnp

    def _L0_gnn_ref(x, edge_index, W1, b1, W2, b2):
        import jax, jax.numpy as jnp
        import numpy as np
        N = 50000
        E = 12500
        D_IN = 64
        D_OUT = 64
        P = 2
        M = 1
        EPS = 1e-10
        LN_EPS = 1e-05

        def _layer_norm(v):
            mu = jnp.mean(v, axis=-1, keepdims=True)
            var = jnp.var(v, axis=-1, keepdims=True)
            return (v - mu) * jax.lax.rsqrt(var + LN_EPS)
        V = x @ W1 + b1
        Q = jax.nn.relu(x @ W2 + b2)
        h = jnp.sum(_layer_norm(Q), axis=1, keepdims=True) ** P
        src, dst = (edge_index[0], edge_index[1])
        h_src = h[src]
        h_dst = h[dst]
        m = (jnp.max(h_src) - jnp.min(h_src)) * M
        attention = jnp.sum(jnp.cos(jnp.pi / (2.0 * m + EPS) * (h_src - h_dst)), axis=1)
        row_sum = jax.ops.segment_sum(attention, src, num_segments=N)
        norm_att = attention / row_sum[src] + EPS
        messages = norm_att[:, None] * V[dst]
        out = jax.ops.segment_sum(messages, src, num_segments=N)
        return out

    def _L1_gnn_ref(p, idx_i, idx_j, basis, pp_W1, pp_b1, pp_W2, pp_b2, pi_W1, pi_b1, pi_W2, pi_b2, pi_W3, ii_W1, ii_b1, ii_W2, ii_b2):
        import jax, jax.numpy as jnp
        import numpy as np
        N_NODES = 50000
        N_EDGES = 12500
        D = 64
        N_BASIS = 8
        p1 = jnp.tanh(p @ pp_W1 + pp_b1) @ pp_W2 + pp_b2
        inter = jnp.concatenate([p1[idx_i], p1[idx_j]], axis=-1)
        inter = inter @ pi_W1 + pi_b1
        inter = inter @ pi_W2 + pi_b2
        inter = inter @ pi_W3
        inter = inter.reshape(inter.shape[0], D, N_BASIS)
        i1 = jnp.einsum('ecb,eb->ec', inter, basis)
        i1 = jnp.tanh(i1 @ ii_W1 + ii_b1) @ ii_W2 + ii_b2
        out = jax.ops.segment_sum(i1, idx_j, num_segments=p1.shape[0])
        return out

    def _L2_gnn_ref(x, edge_index, edge_weight, W0, b0, W1, b1):
        import jax, jax.numpy as jnp
        import numpy as np
        N, E, D = (100000, 25000, 64)
        K_PROP = 10
        ALPHA = 0.1
        UNITS = [256, 64]

        def _gcn_norm(edge_index, edge_weight, num_nodes):
            loop = jnp.arange(num_nodes, dtype=edge_index.dtype)
            row = jnp.concatenate([edge_index[0], loop])
            col = jnp.concatenate([edge_index[1], loop])
            w = jnp.concatenate([edge_weight, jnp.ones((num_nodes,), edge_weight.dtype)])
            deg = jax.ops.segment_sum(w, row, num_segments=num_nodes)
            dinv = jax.lax.rsqrt(jnp.maximum(deg, 1e-12))
            return (row, col, dinv[row] * w * dinv[col])

        def _ssgc_propagate(x, row, col, w):
            n = x.shape[0]

            def step(carry, _):
                h, acc = carry
                h = jax.ops.segment_sum(w[:, None] * h[col], row, num_segments=n)
                return ((h, acc + h), None)
            (_, acc), _ = jax.lax.scan(step, (x, jnp.zeros_like(x)), None, length=K_PROP)
            return ALPHA * x + (1.0 - ALPHA) * acc / K_PROP
        row, col, w = _gcn_norm(edge_index, edge_weight, x.shape[0])
        h = _ssgc_propagate(x, row, col, w)
        h = jax.nn.relu(h @ W0 + b0)
        return h @ W1 + b1

    def _L3_gnn_ref(x, edge_index, edge_attr, W1, root1, bias1, W2, root2, bias2):
        import jax, jax.numpy as jnp
        import numpy as np
        K = 5

        def spline_conv(x, edge_index, pseudo, W, root, bias):
            N = x.shape[0]
            src, dst = (edge_index[0], edge_index[1])
            xk = jnp.einsum('ni,kio->nko', x, W)
            v = pseudo * (K - 1)
            bot = jnp.floor(v)
            frac = v - bot
            bot = bot.astype(jnp.int32)
            msg = jnp.zeros((src.shape[0], W.shape[2]), dtype=x.dtype)
            for s0 in (0, 1):
                for s1 in (0, 1):
                    b0 = frac[:, 0] if s0 else 1.0 - frac[:, 0]
                    b1 = frac[:, 1] if s1 else 1.0 - frac[:, 1]
                    basis = b0 * b1
                    idx = jnp.clip(bot[:, 0] + s0, 0, K - 1) + K * jnp.clip(bot[:, 1] + s1, 0, K - 1)
                    msg = msg + basis[:, None] * xk[src, idx]
            agg = jax.ops.segment_max(msg, dst, num_segments=N)
            agg = jnp.where(jnp.isfinite(agg), agg, jnp.zeros_like(agg))
            return agg + x @ root + bias
        h = jax.nn.relu(spline_conv(x, edge_index, edge_attr, W1, root1, bias1))
        out = spline_conv(h, edge_index, edge_attr, W2, root2, bias2)
        return out
    edge_index = jnp.stack([src, dst])
    h = jnp.maximum(_layernorm(x, axis=-1), 0.0)
    x = x + _L0_gnn_ref(h, edge_index, L0_gnn_W1, L0_gnn_b1, L0_gnn_W2, L0_gnn_b2)
    h = jnp.maximum(_layernorm(x, axis=-1), 0.0)
    x = x + _L1_gnn_ref(h, src, dst, edge_attr_8, L1_gnn_pp_W1, L1_gnn_pp_b1, L1_gnn_pp_W2, L1_gnn_pp_b2, L1_gnn_pi_W1, L1_gnn_pi_b1, L1_gnn_pi_W2, L1_gnn_pi_b2, L1_gnn_pi_W3, L1_gnn_ii_W1, L1_gnn_ii_b1, L1_gnn_ii_W2, L1_gnn_ii_b2)
    h = jnp.maximum(_layernorm(x, axis=-1), 0.0)
    x = x + _L2_gnn_ref(h, edge_index, edge_weight, L2_gnn_W0, L2_gnn_b0, L2_gnn_W1, L2_gnn_b1)
    h = jnp.maximum(_layernorm(x, axis=-1), 0.0)
    x = x + _L3_gnn_ref(h, edge_index, edge_attr_2, L3_gnn_W1, L3_gnn_root1, L3_gnn_bias1, L3_gnn_W2, L3_gnn_root2, L3_gnn_bias2)
    return x

_drawn_inputs = setup_inputs


def setup_inputs(seed=0):
    import zlib

    import numpy as np

    out = dict(_drawn_inputs(seed))
    spreads = {'L1_gnn_pp_b1': (0.0, 0.1),
     'L1_gnn_pp_b2': (0.0, 0.1),
     'L1_gnn_pi_b1': (0.0, 0.1),
     'L1_gnn_pi_b2': (0.0, 0.1),
     'L1_gnn_ii_b1': (0.0, 0.1),
     'L1_gnn_ii_b2': (0.0, 0.1),
     'L2_gnn_b0': (0.0, 0.1),
     'L2_gnn_b1': (0.0, 0.1),
     'L3_gnn_bias1': (0.0, 0.1),
     'L3_gnn_bias2': (0.0, 0.1)}
    factors = {}
    for name, (base, spread) in spreads.items():
        noise = np.random.default_rng([zlib.crc32(name.encode()), seed]).standard_normal(out[name].shape)
        drawn = base * np.exp(spread * noise) if base else spread * noise
        out[name] = jnp.asarray(drawn.astype(out[name].dtype))
    for name, factor in factors.items():
        out[name] = (out[name] * factor).astype(out[name].dtype)
    return out
```

```python
from contextlib import ExitStack, contextmanager

import numpy as np

import concourse.bass as bass
from concourse import mybir

P = 128
F32 = mybir.dt.float32
BF16 = mybir.dt.bfloat16
I32 = mybir.dt.int32
U8 = mybir.dt.uint8
RMAX = bass.bass_isa.ReduceOp.max
ALU = mybir.AluOpType
ACT = mybir.ActivationFunctionType
AX = mybir.AxisListType

N, D = 50000, 64
E = 25000
T = 196
SLOTS = P * T
CH = 14
NCH = T // CH
NIT = NCH // 2
REC = 16
NO_KEY = 65535
DIG = 256
FULL_P = E // T
TAIL = E - FULL_P * T


def wait_for(eng, sem, count):
    if not isinstance(count, int) or count > 0:
        eng.wait_ge(sem, count)


class Chain:

    def __init__(self, eng, sem, per=0):
        self.eng, self.sem, self.per, self.n, self.base = eng, sem, per, 0, 0

    def turn(self, i):
        assert self.n in (0, self.per), self.n
        self.base, self.n = i * self.per, 0

    def link(self, ins):
        ins.then_inc(self.sem, 1)
        self.n += 1
        self.eng.wait_ge(self.sem, self.base + self.n)


class Core:

    def __init__(self, nc, stack):
        self.nc, self.stack, self.phases = nc, stack, 0
        self.sems, self.sem_stack = [], stack.enter_context(ExitStack())

    def phase(self, name):
        self.phases += 1
        self.prefix = f"{name}{self.phases}_"

    def sb(self, name, shape, dt, stack=None):
        return (stack or self.stack).enter_context(self.nc.sbuf_tensor(self.prefix + name, shape, dt))

    def pb(self, name, shape, dt, stack=None):
        return (stack or self.stack).enter_context(self.nc.psum_tensor(self.prefix + name, shape, dt))

    def sem(self, name, stack=None):
        self.sems.append(self.sem_stack.enter_context(self.nc.semaphore(self.prefix + name)))
        return self.sems[-1]

    def recycle(self):
        with self.nc.Block() as block:
            @block.gpsimd
            def _(pool):
                pool.dma_reset()
                for s in self.sems:
                    pool.sem_clear(s)
        self.sem_stack.close()
        self.sems = []


def constants(k):
    nc = k.nc
    k.ident = k.sb("ident", [P, P], F32)
    k.identb = k.sb("identb", [P, P], BF16)
    k.onesb = k.sb("onesb", [P, P], BF16)
    k.ones = k.sb("ones", [P, P], F32)
    k.below = k.sb("below", [P, P], BF16)
    k.digits = k.sb("digits", [P, DIG], BF16)
    k.slot = k.sb("slot", [P, T], I32)
    with ExitStack() as st:
        digits_i = k.sb("digits_i", [P, DIG], I32, st)
        made = k.sem("const_made", st)
        block = st.enter_context(nc.Block())

        @block.gpsimd
        def _(pool):
            pool.memset(k.ident[:, :], 0.0).then_inc(made, 1)
            pool.memset(k.ones[:, :], 1.0).then_inc(made, 1)
            pool.memset(k.onesb[:, :], 1.0).then_inc(made, 1)
            pool.iota(digits_i[:, :], [[1, DIG]], base=0, channel_multiplier=0).then_inc(made, 1)
            pool.iota(k.slot[:, :], [[1, T]], base=0, channel_multiplier=T).then_inc(made, 1)
            pool.wait_ge(made, 5)
            pool.affine_select(out=k.ident[:, :], in_=k.ident[:, :], compare_op=ALU.not_equal, fill=1.0,
                               base=0, pattern=[[-1, P]], channel_multiplier=1).then_inc(made, 1)
            pool.affine_select(out=k.below[:, :], in_=k.onesb[:, :], compare_op=ALU.is_gt, fill=0.0,
                               base=0, pattern=[[1, P]], channel_multiplier=-1).then_inc(made, 1)
            pool.wait_ge(made, 7)
            pool.tensor_copy(k.identb[:, :], k.ident[:, :]).then_inc(made, 1)
            pool.tensor_copy(k.digits[:, :], digits_i[:, :]).then_inc(made, 1)
            pool.wait_ge(made, 9)


def load_records(k, keys, others, attrs, rec):
    nc = k.nc
    k.phase("load")
    with ExitStack() as st:
        words = 2 + sum(w for _, w in attrs)
        flat = k.sb("rec_in", [P, words * T], I32, st)
        cleared, landed, filed = (k.sem(x, st) for x in ("rec_cleared", "rec_landed", "rec_filed"))
        block = st.enter_context(nc.Block())
        parts = [(keys.rearrange("(e w) -> e w", w=1), 1), (others.rearrange("(e w) -> e w", w=1), 1), *attrs]

        @block.vector
        def _(dve):
            dve.memset(flat[:, 0:T], NO_KEY).then_inc(cleared, 1)
            dve.memset(flat[:, T:words * T], 0).then_inc(cleared, 1)
            dve.memset(rec[:, :, :], 0).then_inc(cleared, 1)
            dve.wait_ge(cleared, 3)
            dve.wait_ge(landed, 32 * len(parts))
            at = w0 = 0
            for _, w in parts:
                src = flat[:, at:at + w * T].rearrange("p (t w) -> p t w", w=w)
                dve.tensor_copy(rec[:, :, w0:w0 + w], src).then_inc(filed, 1)
                at, w0 = at + w * T, w0 + w
            dve.wait_ge(filed, len(parts))

        @block.sync
        def _(sp):
            sp.wait_ge(cleared, 2)
            at = 0
            for ap, w in parts:
                sp.dma_start(flat[0:FULL_P, at:at + w * T],
                             ap[0:FULL_P * T, :].rearrange("(p t) w -> p (t w)", t=T)).then_inc(landed, 16)
                sp.dma_start(flat[FULL_P:FULL_P + 1, at:at + w * TAIL],
                             ap[FULL_P * T:E, :].rearrange("(p t) w -> p (t w)", p=1)).then_inc(landed, 16)
                at += w * T
            sp.wait_ge(landed, 32 * len(parts))


def bound_register(pool, k, bound):
    none = pool.alloc_register(k.prefix + "none")
    limit = pool.alloc_register(k.prefix + "limit")
    pool.reg_mov(none, 0)
    return limit, lambda: pool.reg_add(limit, none, bound)


def scatter_rows(pool, k, idx_all, table, bound, stages, idx_stage, staged, sent, rows_made=None, rows_all=None):
    limit, set_limit = bound_register(pool, k, bound)
    with pool.Fori(0, NIT) as i:
        for s in range(2):
            c = 2 * i + s
            pool.wait_ge(sent[s], i * 16 * CH)
            pool.wait_ge(k.opened, 1)
            n = 1
            pool.tensor_copy(idx_stage[s][:, :], idx_all[:, bass.ds(c * CH, CH)]).then_inc(staged, 1)
            if rows_all is not None:
                pool.tensor_copy(stages[s][:, :, :], rows_all[:, bass.ds(c * CH, CH), :]).then_inc(staged, 1)
                n = 2
            pool.wait_ge(staged, (i * 2 + s + 1) * n)
            if rows_made is not None:
                pool.wait_ge(rows_made, c + 1)
            set_limit()
            for t in range(CH):
                pool.indirect_dma_start(
                    table, bass.IndirectOffsetOnAxis(ap=idx_stage[s][:, t:t + 1], axis=0),
                    stages[s][:, t, :], None, bounds_check=limit, oob_is_err=False).then_inc(sent[s], 16)
    for s in range(2):
        pool.wait_ge(sent[s], NIT * 16 * CH)


def gather_rows(pool, k, table, bound, idxs, stages, idx_stage, staged, landed, freed, per_turn, turn0=0, loop=None, ready=None):
    limit, set_limit = bound_register(pool, k, bound) if loop is None else loop
    with pool.Fori(0, NIT) as i:
        for s in range(2):
            c = 2 * i + s
            pool.wait_ge(freed[s], (turn0 + i) * per_turn)
            if ready is not None:
                pool.wait_ge(*ready)
            pool.wait_ge(k.opened, 1)
            for g, idx in enumerate(idxs):
                pool.tensor_copy(idx_stage[s][:, g, :], idx[:, bass.ds(c * CH, CH)]).then_inc(staged, 1)
            pool.wait_ge(staged, ((turn0 + i) * 2 + s + 1) * len(idxs))
            set_limit()
            for t in range(CH):
                for g in range(len(idxs)):
                    pool.indirect_dma_start(
                        stages[s][:, t, g, :], None, table,
                        bass.IndirectOffsetOnAxis(ap=idx_stage[s][:, g, t:t + 1], axis=0),
                        bounds_check=limit, oob_is_err=False).then_inc(landed[s], 16)


def sort_step(k, rank=None, scatter=None):
    nc = k.nc
    k.phase("sort")
    with ExitStack() as st:
        opened = k.opened = k.sem("sort_open", st)
        if scatter:
            stages = [k.sb(f"rec_stage{s}", [P, CH, REC], I32, st) for s in range(2)]
            idxs = [k.sb(f"rec_idx{s}", [P, CH], I32, st) for s in range(2)]
            staged = k.sem("rec_staged", st)
            sent = [k.sem(f"rec_sent{s}", st) for s in range(2)]
        if rank:
            rec, place, shift, source = rank
            dig_i = k.sb("dig_i", [P, T], I32, st)
            dig = k.sb("dig", [P, T], BF16, st)
            hot = k.sb("hot", [P, T + 1, DIG], BF16, st)
            cnt = k.sb("cnt", [P, DIG], BF16, st)
            tot = k.sb("tot", [P, DIG], F32, st)
            upto = k.sb("upto", [P, DIG], F32, st)
            start = k.sb("start", [P, DIG], F32, st)
            one = k.sb("one", [P, DIG], F32, st)
            prod = k.sb("prod", [P, 2, DIG], F32, st)
            rank_f = k.sb("rank_f", [P, T], F32, st)
            ps_cnt = k.pb("ps_cnt", [P, 512], F32, st)
            ps_tot = k.pb("ps_tot", [P, 512], F32, st)
            ps_x = [k.pb(f"ps_x{h}", [P, 512], F32, st) for h in range(2)]
            landed, dve_done, hot_made, counted, cnt_copied, totalled, start_made = (
                k.sem(x, st) for x in ("srt_landed", "srt_dve", "hot_made", "counted", "cnt_copied",
                                       "totalled", "start_made"))
            x_ready = [k.sem(f"x_ready{h}", st) for h in range(2)]
            x_read = [k.sem(f"x_read{h}", st) for h in range(2)]
            HOT = 28
        block = st.enter_context(nc.Block())

        @block.gpsimd
        def _(pool):
            if scatter:
                s_rec, s_rank, s_table = scatter
                pool.engine_nop().then_inc(opened, 1)
                scatter_rows(pool, k, s_rank, s_table, SLOTS - 1, stages, idxs, staged, sent, rows_all=s_rec)

        if not rank:
            return

        @block.sync
        def _(sp):
            if source is not None:
                sp.dma_start(rec[:, :, :].rearrange("p t w -> p (t w)"),
                             source.rearrange("(p t) w -> p (t w)", t=T)).then_inc(landed, 16)
                sp.wait_ge(landed, 16)

        @block.vector
        def _(dve):
            ch = Chain(dve, dve_done)
            if source is not None:
                dve.wait_ge(landed, 16)
            ch.link(dve.tensor_scalar(dig_i[:, :], rec[:, :, 0], shift, DIG - 1,
                                      ALU.logical_shift_right, ALU.bitwise_and))
            ch.link(dve.tensor_copy(dig[:, :], dig_i[:, :]))
            ch.link(dve.memset(hot[:, T, :], 0.0))
            ch.link(dve.memset(one[:, :], 1.0))
            for c in range(T // HOT):
                dve.tensor_tensor(
                    hot[:, c * HOT:(c + 1) * HOT, :],
                    dig[:, c * HOT:(c + 1) * HOT].rearrange("p (t o) -> p t o", o=1).to_broadcast([P, HOT, DIG]),
                    k.digits[:, :].rearrange("p (o d) -> p o d", o=1).to_broadcast([P, HOT, DIG]),
                    ALU.is_equal).then_inc(hot_made, 1)
            dve.wait_ge(counted, 1)
            dve.tensor_copy(cnt[:, :], ps_cnt[:, 0:DIG]).then_inc(cnt_copied, 1)
            dve.wait_ge(totalled, 1)
            ch.link(dve.tensor_copy(tot[:, :], ps_tot[:, 0:DIG]))
            ch.link(dve.tensor_tensor_scan(out=upto[:, :], data0=one[:, :], data1=tot[:, :], initial=0.0,
                                           op0=ALU.mult, op1=ALU.add))
            dve.tensor_tensor(start[:, :], upto[:, :], tot[:, :], ALU.subtract).then_inc(start_made, 1)
            with dve.Fori(0, T // 14) as i:
                for j in range(14):
                    h = j % 2
                    dve.wait_ge(x_ready[h], i * 7 + j // 2 + 1)
                    dve.scalar_tensor_tensor(
                        out=prod[:, h, :], in0=hot[:, bass.ds(i * 14 + j, 1), :].rearrange("p o d -> p (o d)"), scalar=1.0,
                        in1=ps_x[h][:, 0:DIG], op0=ALU.mult, op1=ALU.mult,
                        accum_out=rank_f[:, bass.ds(i * 14 + j, 1)]).then_inc(x_read[h], 1)
            dve.wait_ge(x_read[0], T // 2)
            dve.wait_ge(x_read[1], T // 2)
            ch.link(dve.tensor_copy(place[:, :], rank_f[:, :]))

        @block.tensor
        def _(pe):
            pe.wait_ge(hot_made, 1)
            pe.matmul(ps_cnt[:, 0:DIG], k.identb[:, :], hot[:, T, :], start=True, stop=True)
            with pe.Fori(0, T // HOT) as i:
                pe.wait_ge(hot_made, i + 1)
                for j in range(HOT):
                    pe.matmul(ps_cnt[:, 0:DIG], k.identb[:, :],
                              hot[:, bass.ds(i * HOT + j, 1), :].rearrange("p o d -> p (o d)"),
                              start=False, stop=True, skip_group_check=True)
            pe.matmul(ps_cnt[:, 0:DIG], k.identb[:, :], hot[:, T, :], start=False, stop=True,
                      skip_group_check=True).then_inc(counted, 1)
            pe.wait_ge(cnt_copied, 1)
            pe.matmul(ps_tot[:, 0:DIG], k.onesb[:, :], cnt[:, :], start=True, stop=True).then_inc(totalled, 1)
            pe.wait_ge(start_made, 1)
            for h in range(2):
                pe.matmul(ps_x[h][:, 0:DIG], k.ident[:, :], start[:, :], start=True, stop=False,
                          skip_group_check=True)
                last = pe.matmul(ps_x[h][:, 0:DIG], k.below[:, :], cnt[:, :], start=False, stop=h == 0,
                                 skip_group_check=True)
                if h:
                    last = pe.matmul(ps_x[h][:, 0:DIG], k.identb[:, :], hot[:, 0, :], start=False, stop=True,
                                     skip_group_check=True)
                last.then_inc(x_ready[h], 1)
            with pe.Fori(0, T // 14) as i:
                for j in range(14):
                    h = j % 2
                    pe.wait_ge(x_read[h], i * 7 + j // 2 + 1)
                    for q in range(2):
                        last = pe.matmul(ps_x[h][:, 0:DIG], k.identb[:, :],
                                         hot[:, bass.ds(i * 14 + (j + q), 1), :].rearrange("p o d -> p (o d)"),
                                         start=False, stop=True, skip_group_check=True)
                    last.then_inc(x_ready[h], 1)


def shift_columns(k, keyx, landed, sp):
    sp.dma_start(keyx[1:P, 0:1], keyx[0:P - 1, T:T + 1]).then_inc(landed, 16)
    sp.dma_start(keyx[0:P - 1, T + 1:T + 2], keyx[1:P, 1:2]).then_inc(landed, 16)


class Order:

    def __init__(self, k, name, attrs):
        k.phase(name)
        self.attrs = attrs
        self.key = k.sb("key", [P, T], I32)
        self.other = k.sb("other", [P, T], I32)
        self.last_row = k.sb("last_row", [P, T], I32)
        self.same = k.sb("same", [P, T], F32)
        self.cont = k.sb("cont", [P, T], F32)
        self.whole = k.sb("whole", [D + 1, P], F32)
        self.mask = k.sb("mask", [P, NCH, CH], BF16)
        self.val = {n: k.sb(n, [P, T, w], F32) for n, w in attrs}


def build_order(k, o, records):
    nc = k.nc
    k.phase("order")
    with ExitStack() as st:
        rec = k.sb("rec", [P, T, REC], I32, st)
        keyx = k.sb("keyx", [P, T + 2], F32, st)
        after = k.sb("after", [P, T], F32, st)
        tmp = k.sb("tmp", [P, T], F32, st)
        wide = k.sb("wide", [P, D + 1], F32, st)
        ps = k.pb("ps", [P, 512], F32, st)
        landed, shifted, key_made, done, wide_made, whole_made = (
            k.sem(x, st) for x in ("landed", "shifted", "key_made", "done", "wide_made", "whole_made"))
        block = st.enter_context(nc.Block())

        @block.sync
        def _(sp):
            sp.dma_start(rec[:, :, :].rearrange("p t w -> p (t w)"),
                         records.rearrange("(p t) w -> p (t w)", t=T)).then_inc(landed, 16)
            sp.wait_ge(landed, 16)
            sp.wait_ge(key_made, 1)
            shift_columns(k, keyx, shifted, sp)
            sp.wait_ge(shifted, 32)

        @block.tensor
        def _(pe):
            pe.wait_ge(wide_made, 1)
            pe.matmul(ps[0:D + 1, 0:P], wide[:, :], k.ident[:, :], start=True, stop=True).then_inc(whole_made, 1)

        @block.vector
        def _(dve):
            ch = Chain(dve, done)
            ch.link(dve.memset(keyx[:, :], -1.0))
            dve.wait_ge(landed, 16)
            dve.tensor_copy(keyx[:, 1:T + 1], rec[:, :, 0]).then_inc(key_made, 1)
            at = 2
            for name, w in o.attrs:
                ch.link(dve.tensor_copy(o.val[name][:, :, :], rec[:, :, at:at + w].bitcast(F32)))
                at += w
            ch.link(dve.tensor_scalar(o.key[:, :], rec[:, :, 0], float(N - 1), None, ALU.min))
            ch.link(dve.tensor_copy(o.other[:, :], rec[:, :, 1]))
            dve.wait_ge(key_made, 1)
            dve.wait_ge(shifted, 32)
            key = keyx[:, 1:T + 1]
            ch.link(dve.tensor_tensor(o.same[:, :], key, keyx[:, 0:T], ALU.is_equal))
            ch.link(dve.tensor_scalar(o.cont[:, :], key, keyx[:, 1:2], o.same[:, 0:1], ALU.is_equal, ALU.mult))
            ch.link(dve.memset(o.same[:, 0:1], 0.0))
            ch.link(dve.tensor_copy(o.mask[:, :, :], o.same[:, :].rearrange("p (c t) -> p c t", t=CH)))
            ch.link(dve.memset(o.mask[:, :, 0:1], 0.0))
            ch.link(dve.tensor_tensor(after[:, :], key, keyx[:, 2:T + 2], ALU.not_equal))
            ch.link(dve.scalar_tensor_tensor(out=tmp[:, :], in0=key, scalar=float(-NO_KEY), in1=after[:, :],
                                             op0=ALU.add, op1=ALU.mult))
            ch.link(dve.tensor_scalar(o.last_row[:, :], tmp[:, :], float(NO_KEY), None, ALU.add))
            ch.link(dve.memset(wide[:, :], 1.0))
            dve.tensor_scalar(wide[:, :], wide[:, :], o.cont[:, T - 1:T], None, ALU.mult).then_inc(wide_made, 1)
            dve.wait_ge(whole_made, 1)
            ch.link(dve.tensor_copy(o.whole[:, :], ps[0:D + 1, 0:P]))


def ln_buffers(k, st, tag, n):
    b = {x: k.sb(f"{tag}_{x}", [P, n], F32, st) for x in ("sum", "mean", "ssq", "var", "sd", "rstd")}
    b["sq"] = k.sb(f"{tag}_sq", [P, n, D], F32, st)
    b |= {x: k.sem(f"{tag}_{x}", st) for x in ("centred", "squared", "var_made", "sd_made")}
    b["n"] = n
    return b


def ln_vector(dve, ch, b, x, xc, y, call, floor, freed=None):
    n = b["n"]
    ch.link(dve.tensor_reduce(b["sum"][:, :], x, AX.X, ALU.add))
    ch.link(dve.tensor_scalar(b["mean"][:, :], b["sum"][:, :], 1.0 / D, None, ALU.mult))
    mean = b["mean"][:, :].rearrange("p (n o) -> p n o", o=1).to_broadcast([P, n, D])
    dve.tensor_tensor(xc, x, mean, ALU.subtract).then_inc(b["centred"], 1)
    dve.wait_ge(b["squared"], call + 1)
    ssq = dve.tensor_reduce(b["ssq"][:, :], b["sq"][:, :, :], AX.X, ALU.add)
    if freed is None:
        ch.link(ssq)
    else:
        ssq.then_inc(freed[0], 1)
        dve.wait_ge(*freed)
    dve.tensor_scalar(b["var"][:, :], b["ssq"][:, :], 1.0 / D, 1e-5, ALU.mult, ALU.add).then_inc(b["var_made"], 1)
    dve.wait_ge(b["sd_made"], call + 1)
    ch.link(dve.reciprocal(b["rstd"][:, :], b["sd"][:, :]))
    rstd = b["rstd"][:, :].rearrange("p (n o) -> p n o", o=1).to_broadcast([P, n, D])
    if floor is None:
        return dve.tensor_tensor(y, xc, rstd, ALU.mult)
    return dve.scalar_tensor_tensor(out=y, in0=xc, scalar=floor, in1=rstd, op0=ALU.max, op1=ALU.mult)


LN_LINKS = 4


def ln_scalar(act, b, xc, call, after_read=None):
    ln_square(act, b, xc, call)
    if after_read is not None:
        after_read()
    ln_root(act, b, call)


def ln_square(act, b, xc, call):
    act.wait_ge(b["centred"], call + 1)
    act.activation(b["sq"][:, :, :], xc, ACT.Square).then_inc(b["squared"], 1)


def ln_root(act, b, call):
    act.wait_ge(b["var_made"], call + 1)
    act.activation(b["sd"][:, :], b["var"][:, :], ACT.Sqrt).then_inc(b["sd_made"], 1)


def spread(ap, *shape):
    return ap.to_broadcast(list(shape))


BIG = 1.5e38
FMAX = 3.4028234663852886e38
PI = float(np.pi)


class Scan:

    def __init__(self, k, st, tag, o, f, largest=False, mask=None):
        self.own_mask = mask is None
        self.k, self.o, self.f, self.largest, self.tag = k, o, f, largest, tag
        self.mask = k.sb(f"{tag}_mask", [P, NCH, f, CH], BF16 if largest else U8, st) if mask is None else mask
        self.prev = k.sb(f"{tag}_prev", [P, P], F32, st)
        self.carry_t = k.sb(f"{tag}_carry_t", [P, P + 1], F32, st)
        self.carry = k.sb(f"{tag}_carry", [P, f], F32, st)
        if largest:
            self.wall = k.sb(f"{tag}_wall", [P, T], F32, st)
            self.far = k.sb(f"{tag}_far", [P, T], F32, st)
            self.chain = k.sb(f"{tag}_chain", [f, P], F32, st)
        self.turned, self.scanned, self.back = (k.sem(f"{tag}_{x}", st) for x in ("turned", "scanned", "back"))

    def prepare(self, dve, ch):
        o, f = self.o, self.f
        for_all = o.mask[:, :, :].rearrange("p c (o t) -> p c o t", o=1).to_broadcast([P, NCH, f, CH])
        zero = -BIG if self.largest else 0.0
        if self.own_mask:
            ch.link(dve.tensor_copy(self.mask[:, :, :, :], for_all))
        ch.link(dve.memset(self.carry_t[:, :], zero))
        ch.link(dve.memset(self.prev[:, :], zero))
        if self.largest:
            flat = self.mask[:, :, :, :].rearrange("p c f t -> p (c f t)")
            for out, x in ((flat, flat), (self.wall[:, :], o.same[:, :]), (self.far[:, :], o.cont[:, :]),
                           (self.chain[:, :], o.whole[0:f, :])):
                ch.link(dve.tensor_scalar(out, x, -1.0, BIG, ALU.add, ALU.mult))

    LINKS = 2

    def chunk(self, dve, ch, buf, c, run_made, turn=None):
        first = buf[:, :, 0]
        if self.largest:
            ch.link(dve.scalar_tensor_tensor(out=first, in0=self.prev[:, 0:self.f], scalar=self.wall[:, bass.ds(c * CH, 1)],
                                             in1=first, op0=ALU.add, op1=ALU.max))
        else:
            ch.link(dve.scalar_tensor_tensor(out=first, in0=self.prev[:, 0:self.f], scalar=self.o.same[:, bass.ds(c * CH, 1)],
                                             in1=first, op0=ALU.mult, op1=ALU.add))
        flat = buf.rearrange("p f t -> p (f t)")
        mask = self.mask[:, bass.ds(c, 1), 0:self.f, :].rearrange("p o f t -> p (o f t)")
        op0, op1 = (ALU.add, ALU.max) if self.largest else (ALU.mult, ALU.add)
        ch.link(dve.tensor_tensor_scan(out=flat, data0=mask, data1=flat, initial=0.0, op0=op0, op1=op1))
        dve.tensor_copy(self.prev[:, 0:self.f], buf[:, :, CH - 1]).then_inc(run_made, 1)
        dve.wait_ge(run_made, (c if turn is None else turn) + 1)

    def carries_vector(self, dve, ps, n=0):
        f = self.f
        dve.wait_ge(self.turned, n + 1)
        data0 = self.chain if self.largest else self.o.whole
        op0, op1 = (ALU.add, ALU.max) if self.largest else (ALU.mult, ALU.add)
        dve.tensor_tensor_scan(out=self.carry_t[0:f, 1:P + 1], data0=data0[0:f, :], data1=ps[0:f, 0:P],
                               initial=-BIG if self.largest else 0.0, op0=op0, op1=op1).then_inc(self.scanned, 1)
        dve.wait_ge(self.back, n + 1)
        return dve.tensor_copy(self.carry[:, :], ps[:, 256:256 + f])

    def carries_tensor(self, pe, ps, n=0):
        pe.transpose(ps[:, 0:P], self.prev[:, :], self.k.ident[:, :]).then_inc(self.turned, 1)
        pe.wait_ge(self.scanned, n + 1)
        pe.transpose(ps[:, 2 * P:3 * P], self.carry_t[:, 0:P], self.k.ident[:, :]).then_inc(self.back, 1)


def row(ap):
    return ap.rearrange("(o n) -> o n", o=1)


def col(ap):
    return ap.rearrange("(n o) -> n o", o=1)


def layer0(k, a, o, x1):
    nc = k.nc
    with ExitStack() as layer:
        k.phase("att")
        xs = k.sb("xs", [P, T, D], F32, layer)
        v = k.sb("v", [P, T, D], F32, layer)
        hs = k.sb("hs", [P, T, 2], F32, layer)
        att_rows(k, a, o, xs, v, hs)
        att = k.sb("att", [P, T], F32, layer)
        att_weights(k, a, o, hs, att)
        att_sums(k, o, xs, v, att, x1)


def att_rows(k, a, o, xs, v, hs):
    nc = k.nc
    k.phase("att_rows")
    G2 = 2 * CH
    GROUPS = CH // 2
    with ExitStack() as st:
        k.opened = k.sem("opened", st)
        gb = [k.sb(f"rows{s}", [P, CH, 2, D], F32, st) for s in range(2)]
        idx = [k.sb(f"idx{s}", [P, 2, CH], I32, st) for s in range(2)]
        wbd = k.sb("wbd", [P, 3 * D], F32, st)
        b2 = k.sb("b2", [P, 2 * D], F32, st)
        b1 = k.sb("b1", [P, D], F32, st)
        xc = k.sb("xc", [P, G2, D], F32, st)
        h = k.sb("h", [P, G2, D], F32, st)
        q = k.sb("q", [P, G2, D], F32, st)
        ht = k.sb("ht", [P, 2, 256], F32, st)
        hsum = k.sb("hsum", [P, G2], F32, st)
        ln1, ln2 = ln_buffers(k, st, "ln1", G2), ln_buffers(k, st, "ln2", G2)
        ps_t = [k.pb(f"ps_t{g}", [P, 512], F32, st) for g in range(2)]
        ps_y = [k.pb(f"ps_y{g}", [P, 512], F32, st) for g in range(2)]
        staged, w_clear, w_landed, chain, h_made, turned, ht_made, y_made, y_read, q_added, q_made = (
            k.sem(x, st) for x in ("staged", "w_clear", "w_landed", "chain", "h_made", "turned", "ht_made",
                                   "y_made", "y_read", "q_added", "q_made"))
        landed = [k.sem(f"landed{s}", st) for s in range(2)]
        freed = [k.sem(f"freed{s}", st) for s in range(2)]
        block = st.enter_context(nc.Block())

        @block.sync
        def _(sp):
            sp.wait_ge(w_clear, 1)
            for r, c, w in ((0, 0, "L0_gnn_W2"), (D, D, "L0_gnn_W2"), (D, 2 * D, "L0_gnn_W1")):
                sp.dma_start(wbd[r:r + D, c:c + D], a[w]).then_inc(w_landed, 16)
            for g in range(2):
                sp.dma_start(b2[:, g * D:(g + 1) * D], row(a["L0_gnn_b2"]).to_broadcast([P, D])).then_inc(w_landed, 16)
            sp.dma_start(b1[:, :], row(a["L0_gnn_b1"]).to_broadcast([P, D])).then_inc(w_landed, 16)
            sp.wait_ge(w_landed, 96)

        @block.gpsimd
        def _(pool):
            pool.engine_nop().then_inc(k.opened, 1)
            gather_rows(pool, k, a["x"], N - 1, [o.key, o.other], gb, idx, staged, landed, freed, 1)

        @block.scalar
        def _(act):
            with act.Fori(0, NIT) as i:
                for s in range(2):
                    c = 2 * i + s
                    ln_scalar(act, ln1, xc[:, :, :], c, lambda: act.activation(
                        xs[:, bass.ds(c * CH, CH), :], gb[s][:, :, 0, :], ACT.Copy).then_inc(freed[s], 1))
                    for g in range(GROUPS):
                        act.wait_ge(turned, c * GROUPS + g + 1)
                        if g >= 2:
                            act.wait_ge(y_made, c * GROUPS + g - 1)
                        act.activation(ht[:, g % 2, :], ps_t[g % 2][:, 0:256], ACT.Copy).then_inc(ht_made, 1)
                    act.wait_ge(q_added, c + 1)
                    act.activation(q[:, :, :], q[:, :, :], ACT.Relu).then_inc(q_made, 1)
                    ln_scalar(act, ln2, xc[:, :, :], c)

        @block.tensor
        def _(pe):
            pe.wait_ge(w_landed, 96)
            with pe.Fori(0, NCH) as c:
                pe.wait_ge(h_made, c + 1)
                for g in range(GROUPS + 1):
                    if g < GROUPS:
                        if g >= 2:
                            pe.wait_ge(ht_made, c * GROUPS + g - 1)
                        for j in range(2):
                            last = pe.transpose(ps_t[g % 2][:, j * P:(j + 1) * P],
                                                h[:, 2 * (2 * g + j):2 * (2 * g + j) + 2, :].rearrange("p n f -> p (n f)"),
                                                k.ident[:, :])
                        last.then_inc(turned, 1)
                    if g >= 1:
                        m = g - 1
                        pe.wait_ge(ht_made, c * GROUPS + m + 1)
                        if m >= 2:
                            pe.wait_ge(y_read, c * GROUPS + m - 1)
                        for j in range(2):
                            last = pe.matmul(ps_y[m % 2][:, j * 3 * D:(j + 1) * 3 * D], ht[:, m % 2, j * P:(j + 1) * P],
                                             wbd[:, :], start=True, stop=True)
                        last.then_inc(y_made, 1)

        @block.vector
        def _(dve):
            dve.memset(wbd[:, :], 0.0).then_inc(w_clear, 1)
            dve.wait_ge(w_landed, 96)
            ch = Chain(dve, chain, 2 * (2 * LN_LINKS + 2))
            with dve.Fori(0, NIT) as i:
                ch.turn(i)
                for s in range(2):
                    c = 2 * i + s
                    dve.wait_ge(landed[s], (i + 1) * 16 * G2)
                    dve.wait_ge(k.opened, 1)
                    ln_vector(dve, ch, ln1, gb[s][:, :, :, :].rearrange("p t g f -> p (t g) f"), xc[:, :, :],
                              h[:, :, :], c, 0.0).then_inc(h_made, 1)
                    for g in range(GROUPS):
                        dve.wait_ge(y_made, c * GROUPS + g + 1)
                        y = ps_y[g % 2][:, 0:6 * D].rearrange("p (t n) -> p t n", t=2)
                        q_in = dve.tensor_tensor(
                            q[:, 4 * g:4 * g + 4, :].rearrange("p (t g) f -> p t (g f)", t=2), y[:, :, 0:2 * D],
                            b2[:, :].rearrange("p (o n) -> p o n", o=1).to_broadcast([P, 2, 2 * D]), ALU.add)
                        if g == GROUPS - 1:
                            q_in.then_inc(q_added, 1)
                        dve.tensor_tensor(
                            v[:, bass.ds(c * CH + 2 * g, 2), :], y[:, :, 2 * D:3 * D],
                            b1[:, :].rearrange("p (o n) -> p o n", o=1).to_broadcast([P, 2, D]),
                            ALU.add).then_inc(y_read, 1)
                    dve.wait_ge(q_made, c + 1)
                    ch.link(ln_vector(dve, ch, ln2, q[:, :, :], xc[:, :, :], q[:, :, :], c, None))
                    ch.link(dve.tensor_reduce(hsum[:, :], q[:, :, :], AX.X, ALU.add))
                    dve.tensor_tensor(hs[:, bass.ds(c * CH, CH), :].rearrange("p t g -> p (t g)"), hsum[:, :],
                                      hsum[:, :], ALU.mult)


def att_weights(k, a, o, hs, att):
    nc = k.nc
    k.phase("att_weights")
    ROUND = 1.5 * 2.0 ** 23
    with ExitStack() as st:
        valid, low, x, y, diff, z = (k.sb(n, [P, T], F32, st) for n in ("valid", "low", "x", "y", "diff", "z"))
        ends = k.sb("ends", [P, 2], F32, st)
        ends_all = k.sb("ends_all", [P, 2], F32, st)
        sc = k.sb("sc", [P, 3], F32, st)
        chain, ends_made, all_made, arg_made, att_made = (
            k.sem(n, st) for n in ("chain", "ends_made", "all_made", "arg_made", "att_made"))
        block = st.enter_context(nc.Block())

        @block.vector
        def _(dve):
            ch = Chain(dve, chain)
            source, other = hs[:, :, 0], hs[:, :, 1]
            ch.link(dve.tensor_scalar(valid[:, :], k.slot[:, :], float(E), None, ALU.is_lt))
            ch.link(dve.tensor_scalar(low[:, :], valid[:, :], -1.0, BIG, ALU.add, ALU.mult))
            ch.link(dve.tensor_tensor(x[:, :], source, valid[:, :], ALU.mult))
            ch.link(dve.tensor_tensor(y[:, :], x[:, :], low[:, :], ALU.add))
            ch.link(dve.tensor_reduce(ends[:, 0:1], y[:, :], AX.X, ALU.max))
            ch.link(dve.tensor_tensor(y[:, :], low[:, :], x[:, :], ALU.subtract))
            dve.tensor_reduce(ends[:, 1:2], y[:, :], AX.X, ALU.max).then_inc(ends_made, 1)
            ch.link(dve.tensor_tensor(diff[:, :], source, other, ALU.subtract))
            dve.wait_ge(all_made, 1)
            ch.link(dve.tensor_tensor(sc[:, 0:1], ends_all[:, 0:1], ends_all[:, 1:2], ALU.add))
            ch.link(dve.tensor_scalar(sc[:, 1:2], sc[:, 0:1], 2.0, 1e-10, ALU.mult, ALU.add))
            ch.link(dve.reciprocal(sc[:, 2:3], sc[:, 1:2]))
            ch.link(dve.tensor_scalar(z[:, :], diff[:, :], sc[:, 2:3], 0.5, ALU.mult, ALU.mult))
            ch.link(dve.tensor_scalar(x[:, :], z[:, :], ROUND, None, ALU.add))
            ch.link(dve.tensor_scalar(y[:, :], x[:, :], -ROUND, None, ALU.add))
            ch.link(dve.tensor_tensor(x[:, :], z[:, :], y[:, :], ALU.subtract))
            ch.link(dve.scalar_tensor_tensor(out=y[:, :], in0=x[:, :], scalar=-1.0, in1=x[:, :], op0=ALU.mult,
                                             op1=ALU.max))
            dve.tensor_scalar(z[:, :], y[:, :], -2.0 * PI, 0.5 * PI, ALU.mult, ALU.add).then_inc(arg_made, 1)

        @block.gpsimd
        def _(pool):
            pool.wait_ge(ends_made, 1)
            pool.partition_all_reduce(ends_all[:, :], ends[:, :], P, RMAX).then_inc(all_made, 1)

        @block.scalar
        def _(act):
            act.wait_ge(arg_made, 1)
            act.activation(att[:, :], z[:, :], ACT.Sin).then_inc(att_made, 1)
            act.wait_ge(att_made, 1)


def chunk_cols(c):
    return bass.ds(c * CH, CH)


def att_sums(k, o, xs, v, att, x1):
    nc = k.nc
    k.phase("att_sums")
    F1 = D + 1
    with ExitStack() as st:
        k.opened = k.sem("opened", st)
        run = k.sb("run", [P, T, F1], F32, st)
        buf = k.sb("buf", [P, F1, CH], F32, st)
        buf2 = k.sb("buf2", [P, D, CH], F32, st)
        stages = [k.sb(f"stage{s}", [P, CH, D], F32, st) for s in range(2)]
        idx = [k.sb(f"idx{s}", [P, CH], I32, st) for s in range(2)]
        part = k.sb("part", [P, CH, D], F32, st)
        rs = k.sb("rs", [P, T], F32, st)
        rinv = k.sb("rinv", [P, T], F32, st)
        ps = [k.pb(f"ps{n}", [P, 512], F32, st) for n in range(2)]
        one = Scan(k, st, "one", o, F1)
        two = Scan(k, st, "two", o, D, mask=one.mask)
        staged, chain0, chain, chain2, chain3, rows_made, run1, run2, copied1, copied2 = (
            k.sem(n, st) for n in ("staged", "chain0", "chain", "chain2", "chain3", "rows_made", "run1", "run2",
                                   "copied1", "copied2"))
        sent = [k.sem(f"sent{s}", st) for s in range(2)]
        block = st.enter_context(nc.Block())

        @block.gpsimd
        def _(pool):
            pool.engine_nop().then_inc(k.opened, 1)
            scatter_rows(pool, k, o.last_row, x1, N - 1, stages, idx, staged, sent, rows_made)

        @block.tensor
        def _(pe):
            pe.wait_ge(run1, NCH)
            one.carries_tensor(pe, ps[0])
            pe.wait_ge(run2, NCH)
            two.carries_tensor(pe, ps[1])

        @block.scalar
        def _(act):
            with act.Fori(0, NCH) as c:
                act.wait_ge(run1, c + 1)
                act.wait_ge(k.opened, 1)
                act.activation(run[:, chunk_cols(c), :].rearrange("p t f -> p f t"), buf[:, :, :],
                               ACT.Copy).then_inc(copied1, 1)
                act.wait_ge(run2, c + 1)
                act.wait_ge(k.opened, 1)
                act.activation(v[:, chunk_cols(c), :].rearrange("p t f -> p f t"), buf2[:, :, :],
                               ACT.Copy).then_inc(copied2, 1)

        @block.vector
        def _(dve):
            ch = Chain(dve, chain0)
            one.prepare(dve, ch)
            two.prepare(dve, ch)
            ch = Chain(dve, chain, 3 + 2 * Scan.LINKS)
            with dve.Fori(0, NCH) as c:
                ch.turn(c)
                dve.wait_ge(copied1, c)
                vt = v[:, chunk_cols(c), :].rearrange("p t f -> p f t")
                at = att[:, chunk_cols(c)].rearrange("p (o t) -> p o t", o=1)
                ch.link(dve.tensor_tensor(buf[:, 0:D, :], vt, at.to_broadcast([P, D, CH]), ALU.mult))
                ch.link(dve.tensor_scalar(buf[:, D:F1, :], at, 1.0, None, ALU.mult))
                one.chunk(dve, ch, buf[:, :, :], c, run1)
                dve.wait_ge(copied2, c)
                dve.wait_ge(k.opened, 1)
                ch.link(dve.tensor_scalar(buf2[:, :, :], vt, 1.0, None, ALU.mult))
                two.chunk(dve, ch, buf2[:, :, :], c, run2)
            ch = Chain(dve, chain2)
            ch.link(one.carries_vector(dve, ps[0]))
            ch.link(two.carries_vector(dve, ps[1]))
            dve.wait_ge(copied1, NCH)
            dve.wait_ge(copied2, NCH)
            ch.link(dve.scalar_tensor_tensor(out=rs[:, :], in0=o.cont[:, :], scalar=one.carry[:, D:F1],
                                             in1=run[:, :, D], op0=ALU.mult, op1=ALU.add))
            ch.link(dve.reciprocal(rinv[:, :], rs[:, :]))
            ch = Chain(dve, chain3, 2 * 6)
            with dve.Fori(0, NIT) as i:
                ch.turn(i)
                for s in range(2):
                    c = 2 * i + s
                    stage = stages[s]
                    dve.wait_ge(sent[s], i * 16 * CH)
                    cont = spread(col_of(o.cont, c), P, CH, D)
                    ch.link(dve.tensor_tensor(part[:, :, :], cont, spread(across(one.carry, D), P, CH, D), ALU.mult))
                    ch.link(dve.tensor_tensor(part[:, :, :], part[:, :, :], run[:, chunk_cols(c), 0:D], ALU.add))
                    ch.link(dve.tensor_tensor(part[:, :, :], part[:, :, :], spread(col_of(rinv, c), P, CH, D), ALU.mult))
                    ch.link(dve.tensor_tensor(part[:, :, :], part[:, :, :], xs[:, chunk_cols(c), :], ALU.add))
                    ch.link(dve.tensor_tensor(stage[:, :, :], cont, spread(across(two.carry, D), P, CH, D), ALU.mult))
                    ch.link(dve.tensor_tensor(stage[:, :, :], stage[:, :, :], v[:, chunk_cols(c), :], ALU.add))
                    dve.scalar_tensor_tensor(out=stage[:, :, :], in0=stage[:, :, :], scalar=1e-10, in1=part[:, :, :],
                                             op0=ALU.mult, op1=ALU.add).then_inc(rows_made, 1)
                    dve.wait_ge(rows_made, c + 1)


def col_of(x, c):
    return x[:, chunk_cols(c)].rearrange("p (t o) -> p t o", o=1)


def across(x, n):
    return x[:, 0:n].rearrange("p (o f) -> p o f", o=1)


GROUPS = CH // 2


def pair_weights(k, a, w):
    nc = k.nc
    k.phase("pair_weights")
    NB = 8
    with ExitStack() as st:
        w2 = k.sb("w2", [P, P], F32, st)
        w2t = k.sb("w2t", [P, P], F32, st)
        pi1 = k.sb("pi1", [P, D], F32, st)
        pi1t = k.sb("pi1t", [D, P], F32, st)
        pi2 = k.sb("pi2", [D, D], F32, st)
        pi12 = k.sb("pi12", [P, D], F32, st)
        pi3 = k.sb("pi3", [D, D, NB], F32, st)
        pi3b = k.sb("pi3b", [D, NB, D], F32, st)
        pi3t = k.sb("pi3t", [D, NB, D], F32, st)
        ii1 = k.sb("ii1", [D, D], F32, st)
        b2 = k.sb("b2", [P, 1], F32, st)
        bs = k.sb("bs", [D, 3], F32, st)
        ps = [k.pb(f"ps{n}", [P, 512], F32, st) for n in range(4)]
        cleared, landed, pe_done, dve_done = (k.sem(n, st) for n in ("cleared", "landed", "pe_done", "dve_done"))
        block = st.enter_context(nc.Block())
        g = lambda n: a["L1_gnn_" + n]
        loads = []
        for q in range(2):
            h = slice(q * D, (q + 1) * D)
            loads += [(w.first[h, h], g("pp_W1")), (w2[h, h], g("pp_W2")), (w.last[h, h], g("ii_W2")),
                      (w.first_b[h, :], col(g("pp_b1"))), (b2[h, :], col(g("pp_b2"))),
                      (w.tanh_b[h, :], col(g("ii_b1"))),
                      (w.last_b[:, h], row(g("ii_b2")).to_broadcast([P, D]))]
        loads += [(pi1[:, :], g("pi_W1")), (pi2[:, :], g("pi_W2")), (ii1[:, :], g("ii_W1")),
                  (pi3[:, :, :].rearrange("p c b -> p (c b)"), g("pi_W3")),
                  (bs[:, 0:1], col(g("pi_b1"))), (bs[:, 1:2], col(g("pi_b2")))]

        @block.sync
        def _(sp):
            sp.wait_ge(cleared, 3)
            for to, src in loads:
                sp.dma_start(to, src).then_inc(landed, 16)
            sp.wait_ge(landed, 16 * len(loads))

        @block.tensor
        def _(pe):
            pe.wait_ge(landed, 16 * len(loads))
            pe.transpose(ps[0][0:D, 0:P], pi1[:, :], k.ident[:, :])
            pe.transpose(ps[0][:, P:2 * P], w2[:, :], k.ident[:, :])
            pe.matmul(ps[0][0:D, 300:301], pi1[:, :], b2[:, :], start=True, stop=True).then_inc(pe_done, 1)
            pe.wait_ge(dve_done, 1)
            for b in range(NB):
                last = pe.transpose(ps[1][0:D, b * D:(b + 1) * D], pi3b[:, b, :], k.ident[0:D, 0:D])
            last.then_inc(pe_done, 1)
            pe.wait_ge(dve_done, 2)
            pe.matmul(ps[2][:, 0:D], pi1t[:, :], pi2[:, :], start=True, stop=True)
            pe.matmul(ps[2][0:D, D:D + 1], pi2[:, :], bs[:, 2:3], start=True, stop=True).then_inc(pe_done, 1)
            pe.wait_ge(dve_done, 3)
            for b in range(NB):
                last = pe.matmul(ps[3][0:D, b * D:(b + 1) * D], pi3t[:, b, :], ii1[:, :], start=True, stop=True)
            last.then_inc(pe_done, 1)
            pe.wait_ge(dve_done, 4)
            pe.matmul(ps[2][:, 2 * D:3 * D], w2t[:, :], pi12[:, :], start=True, stop=True).then_inc(pe_done, 1)

        @block.vector
        def _(dve):
            for x in (w.first, w2, w.last):
                dve.memset(x[:, :], 0.0).then_inc(cleared, 1)
            dve.wait_ge(landed, 16 * len(loads))
            dve.tensor_copy(pi3b[:, :, :], pi3[:, :, :].rearrange("p c b -> p b c")).then_inc(dve_done, 1)
            dve.wait_ge(pe_done, 1)
            dve.tensor_copy(pi1t[:, :], ps[0][0:D, 0:P])
            dve.tensor_copy(w2t[:, :], ps[0][:, P:2 * P])
            dve.tensor_tensor(bs[:, 2:3], ps[0][0:D, 300:301], bs[:, 0:1], ALU.add).then_inc(dve_done, 1)
            dve.wait_ge(pe_done, 2)
            dve.tensor_copy(pi3t[:, :, :].rearrange("p b c -> p (b c)"), ps[1][0:D, :]).then_inc(dve_done, 1)
            dve.wait_ge(pe_done, 3)
            dve.tensor_tensor(w.middle_b[:, :], ps[2][0:D, D:D + 1], bs[:, 1:2], ALU.add)
            dve.tensor_copy(pi12[:, :], ps[2][:, 0:D]).then_inc(dve_done, 1)
            dve.wait_ge(pe_done, 4)
            dve.tensor_copy(w.basis[:, :], ps[3][0:D, :])
            dve.wait_ge(pe_done, 5)
            dve.tensor_copy(w.middle[:, :], ps[2][:, 2 * D:3 * D]).then_inc(dve_done, 1)
            dve.wait_ge(dve_done, 5)


class PairWeights:
    def __init__(self, k, st):
        self.first = k.sb("first", [P, P], F32, st)
        self.first_b = k.sb("first_b", [P, 1], F32, st)
        self.middle = k.sb("middle", [P, D], F32, st)
        self.middle_b = k.sb("middle_b", [D, 1], F32, st)
        self.basis = k.sb("basis", [D, 8 * D], F32, st)
        self.tanh_b = k.sb("tanh_b", [P, 1], F32, st)
        self.last = k.sb("last", [P, P], F32, st)
        self.last_b = k.sb("last_b", [P, P], F32, st)


def layer1(k, a, o, x1):
    nc = k.nc
    with ExitStack() as st:
        k.phase("pairs")
        w = PairWeights(k, st)
        xs = k.sb("xs", [P, T, D], F32, st)
        run = k.sb("run", [P, T, D], F32, st)
        scan = Scan(k, st, "sum", o, D)
        pair_weights(k, a, w)
        pair_rows(k, o, w, x1, xs, run, scan)
        send_rows(k, o, scan, run, x1, N - 1, o.last_row, add=xs)


def pair_rows(k, o, w, x1, xs, run, scan):
    nc = k.nc
    k.phase("pair_rows")
    G2 = 2 * CH
    with ExitStack() as st:
        k.opened = k.sem("opened", st)
        gb = [k.sb(f"rows{s}", [P, CH, 2, D], F32, st) for s in range(2)]
        idx = [k.sb(f"idx{s}", [P, 2, CH], I32, st) for s in range(2)]
        xc = k.sb("xc", [P, G2, D], F32, st)
        h = k.sb("h", [P, G2, D], F32, st)
        ht = k.sb("ht", [P, 2, 2 * P], F32, st)
        tt = k.sb("tt", [P, 2, 2 * P], F32, st)
        ut = k.sb("ut", [D, 2, 2 * P], F32, st)
        prod = k.sb("prod", [P, 2, 8, D], F32, st)
        i1 = k.sb("i1", [P, 2, 2, D], F32, st)
        th = k.sb("th", [P, 2, P], F32, st)
        buf = k.sb("buf", [P, D, CH], F32, st)
        ln1 = ln_buffers(k, st, "ln", G2)
        ps_t, ps_p, ps_u, ps_e, ps_o = (k.pb(n, [P, 512], F32, st) for n in ("ps_t", "ps_p", "ps_u", "ps_e", "ps_o"))
        ps_i = [k.pb(f"ps_i{j}", [P, 512], F32, st) for j in range(2)]
        (staged, chain, chain0, h_made, turned, ht_made, p_made, tt_made, u_made, ut_made, i_made, i_read, i1_made,
         e_made, th_made, o_made, o_read, run_made, copied) = (
            k.sem(x, st) for x in ("staged", "chain", "chain0", "h_made", "turned", "ht_made", "p_made", "tt_made",
                                   "u_made", "ut_made", "i_made", "i_read", "i1_made", "e_made", "th_made",
                                   "o_made", "o_read", "run_made", "copied"))
        landed = [k.sem(f"landed{s}", st) for s in range(2)]
        freed = [k.sem(f"freed{s}", st) for s in range(2)]
        block = st.enter_context(nc.Block())

        @block.gpsimd
        def _(pool):
            pool.engine_nop().then_inc(k.opened, 1)
            gather_rows(pool, k, x1, N - 1, [o.other, o.key], gb, idx, staged, landed, freed, 1)

        @block.scalar
        def _(act):
            with act.Fori(0, NIT) as i:
                for s in range(2):
                    c = 2 * i + s
                    n = c * GROUPS
                    ln_scalar(act, ln1, xc[:, :, :], c, lambda: act.activation(
                        xs[:, chunk_cols(c), :], gb[s][:, :, 1, :], ACT.Copy).then_inc(freed[s], 1))
                    for g in range(GROUPS + 4):
                        if g < GROUPS:
                            if g >= 2:
                                act.wait_ge(p_made, n + g - 1)
                            act.wait_ge(turned, n + g + 1)
                            act.activation(ht[:, g % 2, :], ps_t[:, 0:2 * P], ACT.Copy).then_inc(ht_made, 1)
                        m = g - 1
                        if 0 <= m < GROUPS:
                            if m >= 2:
                                act.wait_ge(u_made, n + m - 1)
                            act.wait_ge(p_made, n + m + 1)
                            act.activation(tt[:, m % 2, :], ps_p[:, 0:2 * P], ACT.Tanh,
                                           bias=w.first_b[:, :]).then_inc(tt_made, 1)
                        m = g - 2
                        if 0 <= m < GROUPS:
                            if m >= 2:
                                act.wait_ge(i_made, (n + m - 1) * 2)
                            act.wait_ge(u_made, n + m + 1)
                            act.activation(ut[:, m % 2, :], ps_u[0:D, 0:2 * P], ACT.Identity,
                                           bias=w.middle_b[:, :]).then_inc(ut_made, 1)
                        m = g - 4
                        if 0 <= m < GROUPS:
                            if m >= 2:
                                act.wait_ge(o_made, n + m - 1)
                            act.wait_ge(e_made, n + m + 1)
                            act.activation(th[:, m % 2, :], ps_e[:, 0:P], ACT.Tanh,
                                           bias=w.tanh_b[:, :]).then_inc(th_made, 1)
                    act.wait_ge(run_made, c + 1)
                    act.wait_ge(k.opened, 1)
                    act.activation(run[:, chunk_cols(c), :].rearrange("p t f -> p f t"), buf[:, :, :],
                                   ACT.Copy).then_inc(copied, 1)

        @block.tensor
        def _(pe):
            with pe.Fori(0, NCH) as c:
                n = c * GROUPS
                pe.wait_ge(h_made, c + 1)
                for g in range(GROUPS + 5):
                    if g < GROUPS:
                        pe.wait_ge(ht_made, n + g)
                        for j in range(2):
                            last = pe.transpose(ps_t[:, j * P:(j + 1) * P],
                                                h[:, 4 * g + 2 * j:4 * g + 2 * j + 2, :].rearrange("p n f -> p (n f)"),
                                                k.ident[:, :])
                        last.then_inc(turned, 1)
                    m = g - 1
                    if 0 <= m < GROUPS:
                        pe.wait_ge(tt_made, n + m)
                        pe.wait_ge(ht_made, n + m + 1)
                        pe.matmul(ps_p[:, 0:2 * P], w.first[:, :], ht[:, m % 2, :], start=True,
                                  stop=True).then_inc(p_made, 1)
                    m = g - 2
                    if 0 <= m < GROUPS:
                        pe.wait_ge(ut_made, n + m)
                        pe.wait_ge(tt_made, n + m + 1)
                        pe.matmul(ps_u[0:D, 0:2 * P], w.middle[:, :], tt[:, m % 2, :], start=True,
                                  stop=True).then_inc(u_made, 1)
                    m = g - 3
                    if 0 <= m < GROUPS:
                        pe.wait_ge(ut_made, n + m + 1)
                        for j in range(2):
                            if m >= 1:
                                pe.wait_ge(i_read, (n + m - 1) * 2 + j + 1)
                            pe.matmul(ps_i[j][:, :], ut[:, m % 2, j * P:(j + 1) * P], w.basis[:, :], start=True,
                                      stop=True).then_inc(i_made, 1)
                    m = g - 4
                    if 0 <= m < GROUPS:
                        pe.wait_ge(th_made, n + m)
                        pe.wait_ge(i1_made, n + m + 1)
                        pe.transpose(ps_e[:, 0:P], i1[:, m % 2, :, :].rearrange("p t f -> p (t f)"),
                                     k.ident[:, :]).then_inc(e_made, 1)
                    m = g - 5
                    if 0 <= m < GROUPS:
                        pe.wait_ge(o_read, n + m)
                        pe.wait_ge(th_made, n + m + 1)
                        pe.matmul(ps_o[:, 0:P], th[:, m % 2, :], w.last[:, :], start=True,
                                  stop=True).then_inc(o_made, 1)

        @block.vector
        def _(dve):
            ch0 = Chain(dve, chain0)
            scan.prepare(dve, ch0)
            ch = Chain(dve, chain, 2 * (LN_LINKS + Scan.LINKS))
            with dve.Fori(0, NIT) as i:
                ch.turn(i)
                for s in range(2):
                    c = 2 * i + s
                    n = c * GROUPS
                    dve.wait_ge(landed[s], (i + 1) * 16 * G2)
                    dve.wait_ge(k.opened, 1)
                    ln_vector(dve, ch, ln1, gb[s][:, :, :, :].rearrange("p t g f -> p (t g) f"), xc[:, :, :],
                              h[:, :, :], c, 0.0).then_inc(h_made, 1)
                    dve.wait_ge(copied, c)
                    for g in range(GROUPS + 2):
                        if g < GROUPS:
                            for j in range(2):
                                t = 2 * g + j
                                dve.wait_ge(i_made, (n + g) * 2 + j + 1)
                                factor = o.val["basis"][:, bass.ds(c * CH + t, 1), :].rearrange("p o (b f) -> p (o b) f", f=1)
                                dve.tensor_tensor(prod[:, j, :, :], ps_i[j][:, :].rearrange("p (b f) -> p b f", b=8),
                                                  factor.to_broadcast([P, 8, D]), ALU.mult).then_inc(i_read, 1)
                                dve.wait_ge(i_read, (n + g) * 2 + j + 1)
                                if g >= 2 and j == 0:
                                    dve.wait_ge(e_made, n + g - 1)
                                last = dve.tensor_reduce(i1[:, g % 2, j, :], prod[:, j, :, :].rearrange("p b f -> p f b"),
                                                         AX.X, ALU.add)
                                if j:
                                    last.then_inc(i1_made, 1)
                        m = g - 2
                        if 0 <= m < GROUPS:
                            dve.wait_ge(o_made, n + m + 1)
                            dve.tensor_tensor(buf[:, :, 2 * m:2 * m + 2].rearrange("p f t -> p t f"),
                                              ps_o[:, 0:P].rearrange("p (t f) -> p t f", t=2),
                                              w.last_b[:, :].rearrange("p (t f) -> p t f", t=2),
                                              ALU.add).then_inc(o_read, 1)
                    dve.wait_ge(o_read, n + GROUPS)
                    scan.chunk(dve, ch, buf[:, :, :], c, run_made)


def send_rows(k, o, scan, run, table, bound, rows, add=None):
    nc = k.nc
    k.phase("send")
    with ExitStack() as st:
        k.opened = k.sem("opened", st)
        stages = [k.sb(f"stage{s}", [P, CH, D], F32, st) for s in range(2)]
        idx = [k.sb(f"idx{s}", [P, CH], I32, st) for s in range(2)]
        part = k.sb("part", [P, CH, D], F32, st)
        if scan.largest:
            size = k.sb("size", [P, CH, D], F32, st)
            finite = k.sb("finite", [P, CH, D], I32, st)
        ps = k.pb("ps", [P, 512], F32, st)
        staged, chain0, chain, rows_made = (k.sem(n, st) for n in ("staged", "chain0", "chain", "rows_made"))
        sent = [k.sem(f"sent{s}", st) for s in range(2)]
        block = st.enter_context(nc.Block())

        @block.gpsimd
        def _(pool):
            pool.engine_nop().then_inc(k.opened, 1)
            scatter_rows(pool, k, rows, table, bound, stages, idx, staged, sent, rows_made)

        @block.tensor
        def _(pe):
            scan.carries_tensor(pe, ps)

        @block.vector
        def _(dve):
            ch = Chain(dve, chain0)
            ch.link(scan.carries_vector(dve, ps))
            ch = Chain(dve, chain, 2 * (1 + (add is not None) + 3 * scan.largest))
            with dve.Fori(0, NIT) as i:
                ch.turn(i)
                for s in range(2):
                    c = 2 * i + s
                    dve.wait_ge(sent[s], i * 16 * CH)
                    carry = spread(across(scan.carry, D), P, CH, D)
                    if scan.largest:
                        ch.link(dve.tensor_tensor(part[:, :, :], spread(col_of(scan.far, c), P, CH, D), carry, ALU.add))
                        join = ALU.max
                    else:
                        ch.link(dve.tensor_tensor(part[:, :, :], spread(col_of(o.cont, c), P, CH, D), carry, ALU.mult))
                        join = ALU.add
                    if add is not None:
                        ch.link(dve.tensor_tensor(part[:, :, :], part[:, :, :], add[:, chunk_cols(c), :], ALU.add))
                    if not scan.largest:
                        dve.tensor_tensor(stages[s][:, :, :], part[:, :, :], run[:, chunk_cols(c), :],
                                          join).then_inc(rows_made, 1)
                    else:
                        ch.link(dve.tensor_tensor(part[:, :, :], part[:, :, :], run[:, chunk_cols(c), :], join))
                        ch.link(dve.scalar_tensor_tensor(out=size[:, :, :], in0=part[:, :, :], scalar=-1.0,
                                                         in1=part[:, :, :], op0=ALU.mult, op1=ALU.max))
                        ch.link(dve.tensor_scalar(finite[:, :, :], size[:, :, :], FMAX, -1.0, ALU.is_le, ALU.mult))
                        dve.tensor_tensor(stages[s][:, :, :].bitcast(I32), finite[:, :, :], part[:, :, :].bitcast(I32),
                                          ALU.bitwise_and).then_inc(rows_made, 1)
                    dve.wait_ge(rows_made, c + 1)


def start_tables(k, x, x1, place_of, aggs):
    nc = k.nc
    k.phase("tables")
    Q = 125
    with ExitStack() as st:
        own = k.sb("own", [Q, N // Q], I32, st)
        zeros = k.sb("zeros", [P, 1000], F32, st)
        copied, made, zeroed = (k.sem(n, st) for n in ("copied", "made", "zeroed"))
        block = st.enter_context(nc.Block())

        @block.gpsimd
        def _(pool):
            pool.iota(own[:, :], [[1, N // Q]], base=0, channel_multiplier=N // Q).then_inc(made, 1)

        @block.vector
        def _(dve):
            dve.memset(zeros[:, :], 0.0).then_inc(zeroed, 1)

        @block.sync
        def _(sp):
            sp.dma_start(x1.rearrange("(a b) f -> a (b f)", a=16),
                         x.rearrange("(a b) f -> a (b f)", a=16)).then_inc(copied, 16)
            sp.wait_ge(made, 1)
            sp.dma_start(place_of.rearrange("(p j) o -> p (j o)", p=Q), own[:, :]).then_inc(copied, 16)
            sp.wait_ge(zeroed, 1)
            for agg in aggs:
                sp.dma_start(agg.rearrange("n f -> (n f)").rearrange("(p r w) -> p r w", p=P, w=1000),
                             zeros[:, :].rearrange("p (o w) -> p o w", o=1).to_broadcast([P, N * D // P // 1000, 1000])
                             ).then_inc(copied, 16)
            sp.wait_ge(copied, 16 * (2 + len(aggs)))


J = 25
PD = 125
NBLK = N // (PD * J)
assert NBLK * PD * J == N and NBLK % 2 == 0


def node_block(table, c):
    return table[bass.ds(c * (PD * J), PD * J), :].rearrange("(p j) f -> p (j f)", j=J)


def flat(x):
    return x.rearrange("p j f -> p (j f)")


def move_blocks(sp, loads, stores, loaded, read, made, stored, cleared):
    def load(c, s):
        for table, tiles in loads:
            sp.dma_start(flat(tiles[s][0:PD, 0:J, :]), node_block(table, c)).then_inc(loaded[s], 16)

    def store(c, so_far, s):
        sp.wait_ge(made, so_far)
        for table, tiles in stores:
            sp.dma_start(node_block(table, c), flat(tiles[s][0:PD, 0:J, :])).then_inc(stored[s], 16)

    sp.wait_ge(cleared, 2 * len(loads))
    for s in range(2):
        load(s, s)
    with sp.Fori(0, NBLK // 2 - 1) as i:
        for s in range(2):
            for sem, n in read:
                sp.wait_ge(sem, (2 * i + (s + 1)) * n)
            load(2 * i + s + 2, s)
            store(2 * i + s, 2 * i + (s + 1), s)
    for s in range(2):
        store(NBLK - 2 + s, NBLK - 1 + s, s)
    for s in range(2):
        sp.wait_ge(stored[s], NBLK // 2 * 16 * len(stores))


def clear_blocks(dve, tiles, cleared):
    for x in tiles:
        dve.memset(x[:, :, :], 0.0).then_inc(cleared, 1)


def norm_nodes(k, x, y):
    nc = k.nc
    k.phase("norm")
    with ExitStack() as st:
        xt = [k.sb(f"xt{s}", [P, J, D], F32, st) for s in range(2)]
        yt = [k.sb(f"yt{s}", [P, J, D], F32, st) for s in range(2)]
        xc = k.sb("xc", [P, J, D], F32, st)
        ln = ln_buffers(k, st, "ln", J)
        chain, made, cleared, x_read = (k.sem(n, st) for n in ("chain", "made", "cleared", "x_read"))
        loaded, stored = ([k.sem(f"{n}{s}", st) for s in range(2)] for n in ("loaded", "stored"))
        block = st.enter_context(nc.Block())

        @block.sync
        def _(sp):
            move_blocks(sp, [(x, xt)], [(y, yt)], loaded, [(x_read, 1)], made, stored, cleared)

        @block.scalar
        def _(act):
            with act.Fori(0, NBLK) as c:
                ln_scalar(act, ln, xc[:, :, :], c)

        @block.vector
        def _(dve):
            clear_blocks(dve, xt, cleared)
            ch = Chain(dve, chain, 2 * (LN_LINKS - 1))
            with dve.Fori(0, NBLK // 2) as i:
                ch.turn(i)
                for s in range(2):
                    c = 2 * i + s
                    dve.wait_ge(loaded[s], (i + 1) * 16)
                    dve.wait_ge(stored[s], i * 16)
                    ln_vector(dve, ch, ln, xt[s][:, :, :], xc[:, :, :], yt[s][:, :, :], c, 0.0,
                              freed=(x_read, c + 1)).then_inc(made, 1)


class Propagation:

    def __init__(self, k, st):
        k.phase("prop")
        self.other = k.sb("other", [P, T], I32, st)
        self.inv = k.sb("inv", [P, T], F32, st)
        self.root = k.sb("root", [P, T], F32, st)
        self.uproot = k.sb("uproot", [P, T], F32, st)
        self.cont_inv = k.sb("cont_inv", [P, T], F32, st)
        self.g = k.sb("g", [P, T, D], F32, st)
        self.total = k.sb("total", [P, T, D], F32, st)


def locate(k, o, pr, place_of):
    nc = k.nc
    k.phase("slots")
    with ExitStack() as st:
        k.opened = k.sem("opened", st)
        rows = k.sb("rows", [P, T, 1], I32, st)
        stages = [k.sb(f"stage{s}", [P, CH, 1], I32, st) for s in range(2)]
        idx = [k.sb(f"idx{s}", [P, CH], I32, st) for s in range(2)]
        staged, counted = k.sem("staged", st), k.sem("counted", st)
        sent = [k.sem(f"sent{s}", st) for s in range(2)]
        block = st.enter_context(nc.Block())

        @block.gpsimd
        def _(pool):
            pool.engine_nop().then_inc(k.opened, 1)
            pool.iota(rows[:, :, 0], [[1, T]], base=N, channel_multiplier=T).then_inc(counted, 1)
            pool.wait_ge(counted, 1)
            scatter_rows(pool, k, o.last_row, place_of, N - 1, stages, idx, staged, sent, rows_all=rows)

    k.phase("find")
    with ExitStack() as st:
        k.opened = k.sem("opened", st)
        stages = [k.sb(f"stage{s}", [P, CH, 1, 1], I32, st) for s in range(2)]
        idx = [k.sb(f"idx{s}", [P, 1, CH], I32, st) for s in range(2)]
        run = k.sb("run", [P, T], F32, st)
        deg = k.sb("deg", [P, T], F32, st)
        row_t = k.sb("row_t", [1, P + 1], F32, st)
        carry = k.sb("carry", [P, 1], F32, st)
        ps = [k.pb(f"ps{n}", [P, 512], F32, st) for n in range(2)]
        staged, chain, run_made, turned, scanned, back, root_made, rooted = (
            k.sem(n, st) for n in ("staged", "chain", "run_made", "turned", "scanned", "back", "root_made", "rooted"))
        landed = [k.sem(f"landed{s}", st) for s in range(2)]
        freed = [k.sem(f"freed{s}", st) for s in range(2)]
        block = st.enter_context(nc.Block())

        @block.gpsimd
        def _(pool):
            pool.engine_nop().then_inc(k.opened, 1)
            gather_rows(pool, k, place_of, N - 1, [o.other], stages, idx, staged, landed, freed, 1)

        @block.tensor
        def _(pe):
            pe.wait_ge(run_made, 1)
            pe.transpose(ps[0][0:1, 0:P], run[:, T - 1:T], k.ident[:, :]).then_inc(turned, 1)
            pe.wait_ge(scanned, 1)
            pe.transpose(ps[1][:, 0:1], row_t[:, 0:P], k.ident[0:1, 0:1]).then_inc(back, 1)

        @block.scalar
        def _(act):
            act.wait_ge(root_made, 1)
            act.activation(pr.root[:, :], deg[:, :], ACT.Sqrt).then_inc(rooted, 1)

        @block.vector
        def _(dve):
            ch = Chain(dve, chain)
            w = o.val["weight"][:, :, 0]
            ch.link(dve.memset(row_t[:, :], 0.0))
            dve.tensor_tensor_scan(out=run[:, :], data0=o.same[:, :], data1=w, initial=0.0, op0=ALU.mult,
                                   op1=ALU.add).then_inc(run_made, 1)
            dve.wait_ge(turned, 1)
            dve.tensor_tensor_scan(out=row_t[:, 1:P + 1], data0=o.whole[0:1, :], data1=ps[0][0:1, 0:P], initial=0.0,
                                   op0=ALU.mult, op1=ALU.add).then_inc(scanned, 1)
            dve.wait_ge(back, 1)
            ch.link(dve.tensor_copy(carry[:, :], ps[1][:, 0:1]))
            ch.link(dve.scalar_tensor_tensor(out=deg[:, :], in0=o.cont[:, :], scalar=carry[:, :], in1=run[:, :],
                                             op0=ALU.mult, op1=ALU.add))
            ch.link(dve.tensor_scalar(run[:, :], deg[:, :], 1.0, 1e-12, ALU.add, ALU.max))
            dve.tensor_copy(deg[:, :], run[:, :]).then_inc(root_made, 1)
            ch.link(dve.reciprocal(pr.inv[:, :], run[:, :]))
            ch.link(dve.tensor_tensor(pr.cont_inv[:, :], pr.inv[:, :], o.cont[:, :], ALU.mult))
            dve.wait_ge(rooted, 1)
            ch.link(dve.reciprocal(pr.uproot[:, :], pr.root[:, :]))
            with dve.Fori(0, NIT) as i:
                for s in range(2):
                    c = 2 * i + s
                    dve.wait_ge(landed[s], (i + 1) * 16 * CH)
                    dve.tensor_scalar(pr.other[:, chunk_cols(c)], stages[s][:, :, 0, 0], 0.0, None,
                                      ALU.add).then_inc(freed[s], 1)


PARTS = 7


def slot_rows(table, q):
    w = T // PARTS * D
    return table[N:N + SLOTS, :].rearrange("(p t) f -> p (t f)", t=T)[:, bass.ds(q * w, w)]


def slot_cols(q):
    return bass.ds(q * (T // PARTS), T // PARTS)


def propagate(k, o, pr, table, steps=10):
    nc = k.nc
    k.phase("prop_init")
    with ExitStack() as st:
        k.opened = k.sem("opened", st)
        gb = [k.sb(f"rows{s}", [P, CH, 1, D], F32, st) for s in range(2)]
        idx = [k.sb(f"idx{s}", [P, 1, CH], I32, st) for s in range(2)]
        staged, g_made = k.sem("staged", st), k.sem("g_made", st)
        landed = [k.sem(f"landed{s}", st) for s in range(2)]
        freed = [k.sem(f"freed{s}", st) for s in range(2)]
        block = st.enter_context(nc.Block())

        @block.gpsimd
        def _(pool):
            pool.engine_nop().then_inc(k.opened, 1)
            gather_rows(pool, k, table[0:N, :], N - 1, [o.key], gb, idx, staged, landed, freed, 1)

        @block.vector
        def _(dve):
            with dve.Fori(0, NIT) as i:
                for s in range(2):
                    c = 2 * i + s
                    dve.wait_ge(landed[s], (i + 1) * 16 * CH)
                    dve.tensor_tensor(pr.g[:, chunk_cols(c), :], gb[s][:, :, 0, :],
                                      spread(col_of(pr.uproot, c), P, CH, D), ALU.mult).then_inc(freed[s], 1)
            for s in range(2):
                dve.wait_ge(freed[s], NIT)
            dve.tensor_scalar(pr.total[:, :, :], pr.g[:, :, :], 0.1 / 0.09 - 1.0, None, ALU.mult).then_inc(g_made, 1)
            dve.wait_ge(g_made, 1)

    k.phase("prop_steps")
    with ExitStack() as st:
        k.opened = k.sem("opened", st)
        gb = [k.sb(f"rows{s}", [P, CH, 1, D], F32, st) for s in range(2)]
        idx = [k.sb(f"idx{s}", [P, 1, CH], I32, st) for s in range(2)]
        buf = k.sb("buf", [P, D, CH], F32, st)
        part = k.sb("part", [P, T // PARTS, D], F32, st)
        ps = k.pb("ps", [P, 512], F32, st)
        scan = Scan(k, st, "sum", o, D)
        staged, chain0, chain, carried, chain2, run_made, fixed, stored = (
            k.sem(n, st) for n in ("staged", "chain0", "chain", "carried", "chain2", "run_made", "fixed", "stored"))
        landed = [k.sem(f"landed{s}", st) for s in range(2)]
        freed = [k.sem(f"freed{s}", st) for s in range(2)]
        block = st.enter_context(nc.Block())

        @block.gpsimd
        def _(pool):
            pool.engine_nop().then_inc(k.opened, 1)
            loop = bound_register(pool, k, SLOTS + N - 1)
            with pool.Fori(0, steps) as step:
                gather_rows(pool, k, table, None, [pr.other], gb, idx, staged, landed, freed, 1,
                            turn0=step * NIT, loop=loop, ready=(stored, (step + 1) * 16 * PARTS))

        @block.sync
        def _(sp):
            with sp.Fori(0, PARTS) as q:
                sp.dma_start(slot_rows(table, q), flat(pr.g[:, slot_cols(q), :])).then_inc(stored, 16)
            with sp.Fori(0, steps - 1) as step:
                with sp.Fori(0, PARTS) as q:
                    sp.wait_ge(fixed, step * PARTS + q + 1)
                    sp.wait_ge(k.opened, 1)
                    sp.dma_start(slot_rows(table, q), flat(pr.g[:, slot_cols(q), :])).then_inc(stored, 16)
            sp.wait_ge(stored, steps * 16 * PARTS)

        @block.tensor
        def _(pe):
            with pe.Fori(0, steps) as step:
                pe.wait_ge(run_made, (step + 1) * NCH)
                scan.carries_tensor(pe, ps, step)

        @block.vector
        def _(dve):
            scan.prepare(dve, Chain(dve, chain0))
            ch = Chain(dve, chain, 2 * (3 + Scan.LINKS))
            ch2 = Chain(dve, chain2, 1)
            with dve.Fori(0, steps) as step:
                with dve.Fori(0, NIT) as i:
                    turn = step * NIT + i
                    ch.turn(turn)
                    for s in range(2):
                        c = 2 * i + s
                        g = pr.g[:, chunk_cols(c), :]
                        dve.wait_ge(stored, (step + 1) * 16 * PARTS)
                        ch.link(dve.tensor_tensor(pr.total[:, chunk_cols(c), :], pr.total[:, chunk_cols(c), :], g, ALU.add))
                        dve.wait_ge(landed[s], (turn + 1) * 16 * CH)
                        weight = o.val["weight"][:, chunk_cols(c), :].rearrange("p t o -> p o t")
                        dve.tensor_tensor(buf[:, :, :], gb[s][:, :, 0, :].rearrange("p t f -> p f t"),
                                          weight.to_broadcast([P, D, CH]), ALU.mult).then_inc(freed[s], 1)
                        dve.wait_ge(freed[s], turn + 1)
                        scan.chunk(dve, ch, buf[:, :, :], c, run_made, turn=step * NCH + c)
                        ch.link(dve.tensor_tensor(g, g, buf[:, :, :].rearrange("p f t -> p t f"), ALU.add))
                        ch.link(dve.tensor_tensor(g, g, spread(col_of(pr.inv, c), P, CH, D), ALU.mult))
                scan.carries_vector(dve, ps, step).then_inc(carried, 1)
                with dve.Fori(0, PARTS) as q:
                    ch2.turn(step * PARTS + q)
                    g = pr.g[:, slot_cols(q), :]
                    cont = pr.cont_inv[:, slot_cols(q)].rearrange("p (t o) -> p t o", o=1)
                    dve.wait_ge(carried, step + 1)
                    ch2.link(dve.tensor_tensor(part[:, :, :], spread(cont, P, T // PARTS, D),
                                               spread(across(scan.carry, D), P, T // PARTS, D), ALU.mult))
                    dve.tensor_tensor(g, g, part[:, :, :], ALU.add).then_inc(fixed, 1)
                    dve.wait_ge(fixed, step * PARTS + q + 1)

    k.phase("prop_send")
    with ExitStack() as st:
        k.opened = k.sem("opened", st)
        stages = [k.sb(f"stage{s}", [P, CH, D], F32, st) for s in range(2)]
        idx = [k.sb(f"idx{s}", [P, CH], I32, st) for s in range(2)]
        share = k.sb("share", [P, T], F32, st)
        staged, shared, chain, rows_made = (k.sem(n, st) for n in ("staged", "shared", "chain", "rows_made"))
        sent = [k.sem(f"sent{s}", st) for s in range(2)]
        block = st.enter_context(nc.Block())

        @block.gpsimd
        def _(pool):
            pool.engine_nop().then_inc(k.opened, 1)
            scatter_rows(pool, k, o.last_row, table[0:N, :], N - 1, stages, idx, staged, sent, rows_made)

        @block.vector
        def _(dve):
            Chain(dve, shared).link(dve.tensor_scalar(share[:, :], pr.root[:, :], 0.09, None, ALU.mult))
            ch = Chain(dve, chain, 2)
            with dve.Fori(0, NIT) as i:
                ch.turn(i)
                for s in range(2):
                    c = 2 * i + s
                    dve.wait_ge(sent[s], i * 16 * CH)
                    ch.link(dve.tensor_tensor(stages[s][:, :, :], pr.total[:, chunk_cols(c), :], pr.g[:, chunk_cols(c), :],
                                              ALU.add))
                    dve.tensor_tensor(stages[s][:, :, :], stages[s][:, :, :], spread(col_of(share, c), P, CH, D),
                                      ALU.mult).then_inc(rows_made, 1)


GJ = 4
NG = (J + 1 + GJ - 1) // GJ
assert NG % 2 == 1


def perceptron(k, a, p, x1, x3, h3):
    nc = k.nc
    k.phase("mlp")
    nodes = [min(GJ, J + 1 - g * GJ) for g in range(NG)]
    with ExitStack() as st:
        pt, xt, x3t, h3t = ([k.sb(f"{n}{s}", [P, J + 1, D], F32, st) for s in range(2)] for n in ("pt", "xt", "x3t", "h3t"))
        xc = k.sb("xc", [P, J + 1, D], F32, st)
        w0 = k.sb("w0", [P, 2, P], F32, st)
        b0 = k.sb("b0", [P, 2], F32, st)
        w1 = k.sb("w1", [P, 2, D], F32, st)
        b1 = k.sb("b1", [P, 1, D], F32, st)
        turned_p = k.sb("turned_p", [P, 2, 2 * P], F32, st)
        hidden = k.sb("hidden", [P, 2, 2, 2, 2 * P], F32, st)
        ln = ln_buffers(k, st, "ln", J + 1)
        ps_t = [k.pb(f"ps_t{n}", [P, 512], F32, st) for n in range(2)]
        ps_u = [k.pb(f"ps_u{n}", [P, 1024], F32, st) for n in range(2)]
        ps_o = [k.pb(f"ps_o{n}", [P, 512], F32, st) for n in range(2)]
        chain, made, cleared, turned, copied, x_biased, x3_made, w_landed, u_made, o_made = (
            k.sem(n, st) for n in ("chain", "made", "cleared", "turned", "copied", "x_biased", "x3_made", "w_landed",
                                   "u_made", "o_made"))
        loaded, stored, hidden_made = (
            [k.sem(f"{n}{s}", st) for s in range(2)] for n in ("loaded", "stored", "hidden_made"))
        block = st.enter_context(nc.Block())

        @block.sync
        def _(sp):
            for q in range(2):
                sp.dma_start(w0[q * D:(q + 1) * D, :, :].rearrange("p h n -> p (h n)"), a["L2_gnn_W0"]).then_inc(w_landed, 16)
            sp.dma_start(w1[:, :, :], a["L2_gnn_W1"].rearrange("(h p) f -> p h f", h=2)).then_inc(w_landed, 16)
            for h in range(2):
                sp.dma_start(b0[:, h:h + 1], col(a["L2_gnn_b0"])[h * P:(h + 1) * P, :]).then_inc(w_landed, 16)
            sp.dma_start(b1[:, 0, :], row(a["L2_gnn_b1"]).to_broadcast([P, D])).then_inc(w_landed, 16)
            sp.wait_ge(w_landed, 96)
            move_blocks(sp, [(p, pt), (x1, xt)], [(x3, x3t), (h3, h3t)], loaded, [(turned, NG), (x3_made, NG)],
                        made, stored, cleared)

        @block.tensor
        def _(pe):
            def turn_rows(n, g, s):
                ring = (s * NG + g) % 2
                wait_for(pe, copied, n + (g - 1))
                for q in range(nodes[g] // 2):
                    at = g * GJ + 2 * q
                    last = pe.transpose(ps_t[ring][:, q * P:(q + 1) * P], pt[s][:, at:at + 2, :].rearrange("p j f -> p (j f)"),
                                        k.ident[:, :])
                last.then_inc(turned, 1)

            def first(count, g, ring):
                pe.wait_ge(copied, count + 1)
                for h in range(2):
                    wait_for(pe, hidden_made[h], count - 1)
                w = nodes[g] // 2 * P
                for h in range(2):
                    for e in range(2):
                        rows, at = slice(e * D, (e + 1) * D), e * 512 + h * 2 * P
                        last = pe.matmul(ps_u[ring][:, at:at + w], w0[rows, h, :], turned_p[rows, ring, 0:w],
                                         start=True, stop=True)
                last.then_inc(u_made, 1)

            def second(count, g, ring):
                for h in range(2):
                    pe.wait_ge(hidden_made[h], count + 1)
                wait_for(pe, x3_made, count - 1)
                for q in range(nodes[g]):
                    for h in range(2):
                        last = pe.matmul(ps_o[ring][:, q * D:(q + 1) * D], hidden[:, ring, h, q % 2, q // 2 * P:(q // 2 + 1) * P],
                                         w1[:, h, :], start=h == 0, stop=h == 1)
                last.then_inc(o_made, 1)

            def turn(i):
                for s in range(2):
                    n = (2 * i + s) * NG
                    pe.wait_ge(loaded[s], (i + 1) * 32)
                    for g in range(NG):
                        turn_rows(n, g, s)
                        for stage, lag in ((first, 1), (second, 3)):
                            if not isinstance(i, int) or n + g >= lag:
                                stage(n + (g - lag), (g - lag) % NG, (s * NG + g + lag) % 2)

            pe.wait_ge(w_landed, 96)
            turn(0)
            with pe.Fori(1, NBLK // 2) as i:
                turn(i)
            end = NBLK * NG
            first(end - 1, NG - 1, 1)
            for lag in (3, 2, 1):
                second(end - lag, NG - lag, lag % 2)

        @block.scalar
        def _(act):
            def hide(count, g, ring):
                act.wait_ge(u_made, count + 1)
                wait_for(act, o_made, count - 1)
                w = nodes[g] // 2 * P
                for h in range(2):
                    act.activation(hidden[:, ring, h, :, 0:w],
                                   ps_u[ring][:, :].rearrange("p (e h n) -> p e h n", e=2, h=2)[:, :, h, 0:w], ACT.Relu,
                                   bias=b0[:, h:h + 1]).then_inc(hidden_made[h], 1)

            def turn(i):
                for s in range(2):
                    n = (2 * i + s) * NG
                    for g in range(NG):
                        ring = (s * NG + g) % 2
                        act.wait_ge(turned, n + g + 1)
                        wait_for(act, u_made, n + (g - 1))
                        w = nodes[g] // 2 * P
                        act.activation(turned_p[:, ring, 0:w], ps_t[ring][:, 0:w], ACT.Copy).then_inc(copied, 1)
                        if not isinstance(i, int) or n + g >= 1:
                            hide(n + (g - 1), (g - 1) % NG, 1 - ring)
                        if not isinstance(i, int) or 2 * i + s > 0:
                            if g == 3:
                                ln_square(act, ln, xc[:, :, :], 2 * i + (s - 1))
                            if g == 4:
                                ln_root(act, ln, 2 * i + (s - 1))

            turn(0)
            with act.Fori(1, NBLK // 2) as i:
                turn(i)
            hide(NBLK * NG - 1, NG - 1, 1)
            ln_scalar(act, ln, xc[:, :, :], NBLK - 1)

        @block.vector
        def _(dve):
            clear_blocks(dve, pt + xt, cleared)
            dve.wait_ge(w_landed, 96)
            ch = Chain(dve, chain, 2 * LN_LINKS)
            with dve.Fori(0, NBLK // 2) as i:
                ch.turn(i)
                for s in range(2):
                    c = 2 * i + s
                    n = c * NG
                    dve.wait_ge(loaded[s], (i + 1) * 32)
                    dve.tensor_tensor(xt[s][:, :, :], xt[s][:, :, :], spread(b1[:, :, :], P, J + 1, D),
                                      ALU.add).then_inc(x_biased, 1)
                    dve.wait_ge(x_biased, c + 1)
                    dve.wait_ge(stored[s], i * 32)
                    for g in range(NG):
                        dve.wait_ge(o_made, n + g + 1)
                        these = slice(g * GJ, g * GJ + nodes[g])
                        dve.tensor_tensor(x3t[s][:, these, :],
                                          ps_o[(s * NG + g) % 2][:, 0:nodes[g] * D].rearrange("p (j f) -> p j f", f=D),
                                          xt[s][:, these, :], ALU.add).then_inc(x3_made, 1)
                    dve.wait_ge(x3_made, n + NG)
                    ln_vector(dve, ch, ln, x3t[s][:, :, :], xc[:, :, :], h3t[s][:, :, :], c, 0.0).then_inc(made, 1)


def root_pass(k, h, root, bias, adds, y, relu):
    nc = k.nc
    k.phase("root")
    PAIRS = (J + 1) // 2
    GROUP = 4
    groups = [range(q, min(q + GROUP, PAIRS)) for q in range(0, PAIRS, GROUP)]
    NR = len(groups)
    assert NR % 2 == 0
    with ExitStack() as st:
        ht, yt = ([k.sb(f"{n}{s}", [P, J + 1, D], F32, st) for s in range(2)] for n in ("ht", "yt"))
        at = [[k.sb(f"add{q}_{s}", [P, J + 1, D], F32, st) for s in range(2)] for q in range(len(adds))]
        w = k.sb("w", [P, P], F32, st)
        b = k.sb("b", [P, 1, D], F32, st)
        turned_h = k.sb("turned_h", [P, 2, GROUP, P], F32, st)
        ps_t = [k.pb(f"ps_t{n}", [P, 512], F32, st) for n in range(2)]
        ps_y = [k.pb(f"ps_y{n}", [P, 512], F32, st) for n in range(2)]
        chain, made, cleared, w_clear, w_landed, turned, copied, y_made, y_read = (
            k.sem(n, st) for n in ("chain", "made", "cleared", "w_clear", "w_landed", "turned", "copied", "y_made",
                                   "y_read"))
        loaded, stored = ([k.sem(f"{n}{s}", st) for s in range(2)] for n in ("loaded", "stored"))
        block = st.enter_context(nc.Block())

        @block.sync
        def _(sp):
            sp.wait_ge(w_clear, 1)
            for q in range(2):
                sp.dma_start(w[q * D:(q + 1) * D, q * D:(q + 1) * D], root).then_inc(w_landed, 16)
            sp.dma_start(b[:, 0, :], row(bias).to_broadcast([P, D])).then_inc(w_landed, 16)
            sp.wait_ge(w_landed, 48)
            move_blocks(sp, [(h, ht), *zip(adds, at)], [(y, yt)], loaded, [(turned, NR), (y_read, NR)], made, stored,
                        cleared)

        @block.tensor
        def _(pe):
            def turn_rows(n, g, s):
                wait_for(pe, copied, n + (g - 1))
                for q, pair in enumerate(groups[g]):
                    last = pe.transpose(ps_t[g % 2][:, q * P:(q + 1) * P],
                                        ht[s][:, 2 * pair:2 * pair + 2, :].rearrange("p j f -> p (j f)"), k.ident[:, :])
                last.then_inc(turned, 1)

            def multiply(count, g):
                pe.wait_ge(copied, count + 1)
                wait_for(pe, y_read, count - 1)
                for q in range(len(groups[g])):
                    last = pe.matmul(ps_y[g % 2][:, q * P:(q + 1) * P], turned_h[:, g % 2, q, :], w[:, :],
                                     start=True, stop=True)
                last.then_inc(y_made, 1)

            def turn(i):
                for s in range(2):
                    n = (2 * i + s) * NR
                    pe.wait_ge(loaded[s], (i + 1) * 16 * (1 + len(adds)))
                    for g in range(NR):
                        turn_rows(n, g, s)
                        if not isinstance(i, int) or n + g > 0:
                            multiply(n + (g - 1), (g - 1) % NR)

            pe.wait_ge(w_landed, 48)
            turn(0)
            with pe.Fori(1, NBLK // 2) as i:
                turn(i)
            multiply(NBLK * NR - 1, NR - 1)

        @block.scalar
        def _(act):
            def copy(c):
                for g in range(NR):
                    act.wait_ge(turned, c * NR + g + 1)
                    wait_for(act, y_made, c * NR + (g - 1))
                    wide = len(groups[g]) * P
                    act.activation(turned_h[:, g % 2, 0:len(groups[g]), :].rearrange("p q n -> p (q n)"),
                                   ps_t[g % 2][:, 0:wide], ACT.Copy).then_inc(copied, 1)

            copy(0)
            with act.Fori(1, NBLK) as c:
                copy(c)

        @block.vector
        def _(dve):
            dve.memset(w[:, :], 0.0).then_inc(w_clear, 1)
            clear_blocks(dve, [x for xs in [ht, *at] for x in xs], cleared)
            dve.wait_ge(w_landed, 48)
            ch = Chain(dve, chain, 2 * len(adds))
            with dve.Fori(0, NBLK // 2) as i:
                ch.turn(i)
                for s in range(2):
                    c = 2 * i + s
                    n = c * NR
                    dve.wait_ge(loaded[s], (i + 1) * 16 * (1 + len(adds)))
                    base = at[0][s]
                    ch.link(dve.tensor_tensor(base[:, :, :], base[:, :, :], spread(b[:, :, :], P, J + 1, D), ALU.add))
                    for more in at[1:]:
                        ch.link(dve.tensor_tensor(base[:, :, :], base[:, :, :], more[s][:, :, :], ALU.add))
                    dve.wait_ge(stored[s], i * 16)
                    for g in range(NR):
                        dve.wait_ge(y_made, n + g + 1)
                        nodes = slice(2 * groups[g][0], 2 * groups[g][-1] + 2)
                        wide = len(groups[g]) * P
                        dve.tensor_tensor(yt[s][:, nodes, :], ps_y[g % 2][:, 0:wide].rearrange("p (j f) -> p j f", f=D),
                                          base[:, nodes, :], ALU.add).then_inc(y_read, 1)
                    dve.wait_ge(y_read, n + NR)
                    if relu:
                        dve.tensor_scalar(yt[s][:, :, :], yt[s][:, :, :], 0.0, None, ALU.max).then_inc(made, 1)
                    else:
                        dve.tensor_scalar(yt[s][:, 0:1, :], yt[s][:, 0:1, :], 1.0, None, ALU.mult).then_inc(made, 1)


K5 = 5


class Spline:

    def __init__(self, k, st, o):
        nc = k.nc
        k.phase("spline")
        self.knots = k.sb("knots", [P, T, 2, K5], F32, st)
        with ExitStack() as tmp:
            v = k.sb("v", [P, 2 * T], F32, tmp)
            x = k.sb("x", [P, 2 * T], F32, tmp)
            y = k.sb("y", [P, 2 * T], F32, tmp)
            chain = k.sem("chain", tmp)
            block = tmp.enter_context(nc.Block())

            @block.vector
            def _(dve):
                ch = Chain(dve, chain)
                pseudo = o.val["pseudo"][:, :, :].rearrange("p t d -> p (t d)")
                ch.link(dve.tensor_scalar(x[:, :], pseudo, float(K5 - 1), 0.0, ALU.mult, ALU.max))
                ch.link(dve.tensor_scalar(v[:, :], x[:, :], float(K5 - 1), None, ALU.min))
                for n in range(K5):
                    ch.link(dve.tensor_scalar(x[:, :], v[:, :], float(-n), None, ALU.add))
                    ch.link(dve.scalar_tensor_tensor(out=y[:, :], in0=x[:, :], scalar=-1.0, in1=x[:, :], op0=ALU.mult,
                                                     op1=ALU.max))
                    ch.link(dve.tensor_scalar(x[:, :], y[:, :], -1.0, 1.0, ALU.mult, ALU.add))
                    ch.link(dve.tensor_scalar(self.knots[:, :, :, n].rearrange("p t d -> p (t d)"), x[:, :], 0.0, None,
                                              ALU.max))


def conv(k, o, spline, h, weight, agg):
    with ExitStack() as st:
        k.phase("conv")
        run = k.sb("run", [P, T, D], F32, st)
        scan = Scan(k, st, "max", o, D, largest=True)
        conv_rows(k, o, spline, h, weight, run, scan)
        send_rows(k, o, scan, run, agg, N - 1, o.last_row)


def conv_rows(k, o, spline, h, weight, run, scan):
    nc = k.nc
    k.phase("conv_rows")
    W = K5 * D
    with ExitStack() as st:
        k.opened = k.sem("opened", st)
        gb = [k.sb(f"rows{s}", [P, CH, 1, D], F32, st) for s in range(2)]
        idx = [k.sb(f"idx{s}", [P, 1, CH], I32, st) for s in range(2)]
        w = k.sb("w", [P, 3, W], F32, st)
        z4 = [k.sb(f"z4_{s}", [P, CH, 4, D], F32, st) for s in range(2)]
        z1 = [k.sb(f"z1_{s}", [P, CH, D], F32, st) for s in range(2)]
        zt = k.sb("zt", [P, 2, K5 * P], F32, st)
        prod = k.sb("prod", [P, 2, K5, D], F32, st)
        buf = [k.sb(f"buf{s}", [P, D, CH], F32, st) for s in range(2)]
        ps_z = k.pb("ps_z", [P, 1024], F32, st)
        ps_m = [k.pb(f"ps_m{n}", [P, 1024], F32, st) for n in range(2)]
        staged, chain0, chain, w_landed, z4_made, turned, zt_made, m_made, m_read, reduced, run_made, copied = (
            k.sem(n, st) for n in ("staged", "chain0", "chain", "w_landed", "z4_made", "turned", "zt_made", "m_made",
                                   "m_read", "reduced", "run_made", "copied"))
        landed = [k.sem(f"landed{s}", st) for s in range(2)]
        z_made = [k.sem(f"z_made{s}", st) for s in range(2)]
        block = st.enter_context(nc.Block())

        @block.gpsimd
        def _(pool):
            pool.engine_nop().then_inc(k.opened, 1)
            gather_rows(pool, k, h, N - 1, [o.other], gb, idx, staged, landed, z_made, 1)

        @block.sync
        def _(sp):
            by_knot = weight.rearrange("(k1 k0) i o -> k0 i k1 o", k0=K5)
            for c, q, k0 in ((0, 0, 0), (0, 1, 1), (1, 0, 2), (1, 1, 3), (2, 0, 4), (2, 1, 4)):
                sp.dma_start(w[q * D:(q + 1) * D, c, :].rearrange("p (k o) -> p k o", k=K5),
                             by_knot[k0]).then_inc(w_landed, 16)
            sp.wait_ge(w_landed, 96)

        @block.tensor
        def _(pe):
            def turn_z(n, g, s):
                wait_for(pe, zt_made, n + g)
                for e in range(2):
                    for q in range(2):
                        pe.transpose(ps_z[:, (2 * e + q) * P:(2 * e + q + 1) * P],
                                     z4[s][:, 2 * g + e, 2 * q:2 * q + 2, :].rearrange("p n f -> p (n f)"), k.ident[:, :])
                pe.transpose(ps_z[:, 4 * P:5 * P], z1[s][:, 2 * g:2 * g + 2, :].rearrange("p t f -> p (t f)"),
                             k.ident[:, :]).then_inc(turned, 1)

            def multiply(pair, ring):
                pe.wait_ge(zt_made, pair + 1)
                wait_for(pe, m_read, pair - 1)
                to = [ps_m[ring][:, e * 512:e * 512 + W] for e in range(2)]
                for e in range(2):
                    for q in range(2):
                        pe.matmul(to[e], zt[:, ring, (2 * e + q) * P:(2 * e + q + 1) * P], w[:, q, :],
                                  start=q == 0, stop=False)
                for e in range(2):
                    rows = slice(e * D, (e + 1) * D)
                    last = pe.matmul(to[e], zt[rows, ring, 4 * P:5 * P], w[rows, 2, :], start=False, stop=True)
                last.then_inc(m_made, 1)

            def turn(i):
                for s in range(2):
                    n = (2 * i + s) * GROUPS
                    pe.wait_ge(z_made[s], i + 1)
                    for g in range(GROUPS):
                        turn_z(n, g, s)
                        if not isinstance(i, int) or n + g > 0:
                            multiply(n + g - 1, (s * GROUPS + g + 1) % 2)

            pe.wait_ge(w_landed, 96)
            turn(0)
            with pe.Fori(1, NIT) as i:
                turn(i)
            multiply(NCH * GROUPS - 1, 1)

        @block.scalar
        def _(act):
            def chunk(c, s, copies):
                for g in range(GROUPS):
                    act.wait_ge(turned, c * GROUPS + g + 1)
                    wait_for(act, m_made, c * GROUPS + (g - 1))
                    act.activation(zt[:, (s * GROUPS + g) % 2, :], ps_z[:, 0:K5 * P], ACT.Copy).then_inc(zt_made, 1)
                    if g == 3 and copies:
                        copy(c - 1, 1 - s)

            def copy(c, s):
                act.wait_ge(run_made, c + 1)
                act.wait_ge(k.opened, 1)
                act.activation(run[:, chunk_cols(c), :].rearrange("p t f -> p f t"), buf[s][:, :, :],
                               ACT.Copy).then_inc(copied, 1)

            chunk(0, 0, False)
            chunk(1, 1, True)
            with act.Fori(1, NIT) as i:
                for s in range(2):
                    chunk(2 * i + s, s, True)
            copy(NCH - 1, 1)

        @block.vector
        def _(dve):
            scan.prepare(dve, Chain(dve, chain0))
            ch = Chain(dve, chain, 2 * Scan.LINKS)

            def build(c, s, turn):
                dve.wait_ge(landed[s], turn * 16 * CH)
                dve.wait_ge(k.opened, 1)
                first = spline.knots[:, chunk_cols(c), 0, :]
                rows = gb[s][:, :, :, :]
                dve.tensor_tensor(z4[s][:, :, :, :],
                                  first[:, :, 0:4].rearrange("p t (n o) -> p t n o", o=1).to_broadcast([P, CH, 4, D]),
                                  rows.to_broadcast([P, CH, 4, D]), ALU.mult).then_inc(z4_made, 1)
                dve.wait_ge(z4_made, c + 1)
                dve.tensor_tensor(z1[s][:, :, :], first[:, :, 4:5].to_broadcast([P, CH, D]), rows[:, :, 0, :],
                                  ALU.mult).then_inc(z_made[s], 1)

            def take(c, s):
                for g in range(GROUPS):
                    n = c * GROUPS + g
                    dve.wait_ge(m_made, n + 1)
                    dve.wait_ge(reduced, n)
                    second = spline.knots[:, bass.ds(c * CH + 2 * g, 2), 1, :]
                    dve.tensor_tensor(prod[:, :, :, :],
                                      ps_m[(s * GROUPS + g) % 2][:, :].rearrange("p (e w) -> p e w", e=2)[:, :, 0:W].rearrange(
                                          "p e (n f) -> p e n f", f=D),
                                      second.rearrange("p t (n o) -> p t n o", o=1).to_broadcast([P, 2, K5, D]),
                                      ALU.mult).then_inc(m_read, 1)
                    dve.wait_ge(m_read, n + 1)
                    dve.tensor_reduce(buf[s][:, :, 2 * g:2 * g + 2].rearrange("p f t -> p t f"),
                                      prod[:, :, :, :].rearrange("p e n f -> p e f n"), AX.X,
                                      ALU.add).then_inc(reduced, 1)
                dve.wait_ge(reduced, (c + 1) * GROUPS)
                scan.chunk(dve, ch, buf[s][:, :, :], c, run_made)

            def step(c, s, i):
                dve.wait_ge(turned, c * GROUPS)
                build(c + 1, 1 - s, i + 1 + s)
                if s == 0:
                    dve.wait_ge(copied, c)
                else:
                    dve.wait_ge(copied, c)
                take(c, s)

            build(0, 0, 1)
            with dve.Fori(0, NIT - 1) as i:
                ch.turn(i)
                for s in range(2):
                    step(2 * i + s, s, i)
            ch.turn(NIT - 1)
            step(NCH - 2, 0, NIT - 1)
            dve.wait_ge(copied, NCH - 1)
            take(NCH - 1, 1)


def gnn_kernel(nc, a, out):
    with ExitStack() as stack:
        k = Core(nc, stack)
        k.phase("all")
        constants(k)
        s, d = "src", "dst"
        k.rec_dram = {o: [nc.dram_tensor(f"rec_{o}{i}", (SLOTS, REC), I32, kind="Internal").ap() for i in range(2)]
                      for o in (s, d)}
        with ExitStack() as st:
            rec = {o: k.sb(f"rec_{o}", [P, T, REC], I32, st) for o in (s, d)}
            place = {o: k.sb(f"place_{o}", [P, T], I32, st) for o in (s, d)}
            load_records(k, a[s], a[d], [(a["edge_weight"].bitcast(I32).rearrange("(e w) -> e w", w=1), 1)], rec[s])
            load_records(k, a[d], a[s], [(a["edge_attr_2"].bitcast(I32), 2), (a["edge_attr_8"].bitcast(I32), 8)],
                         rec[d])
            sort_step(k, (rec[s], place[s], 0, None))
            sort_step(k, (rec[d], place[d], 0, None), (rec[s], place[s], k.rec_dram[s][0]))
            sort_step(k, (rec[s], place[s], 8, k.rec_dram[s][0]), (rec[d], place[d], k.rec_dram[d][0]))
            sort_step(k, (rec[d], place[d], 8, k.rec_dram[d][0]), (rec[s], place[s], k.rec_dram[s][1]))
            sort_step(k, None, (rec[d], place[d], k.rec_dram[d][1]))
        by_src = Order(k, "by_src", [("weight", 1)])
        build_order(k, by_src, k.rec_dram[s][1])
        x1 = nc.dram_tensor("x1", (N, D), F32, kind="Internal").ap()
        place_of = nc.dram_tensor("place_of", (N, 1), I32, kind="Internal").ap()
        table = nc.dram_tensor("table", (N + SLOTS, D), F32, kind="Internal").ap()
        agg = [nc.dram_tensor(f"agg{n}", (N, D), F32, kind="Internal").ap() for n in range(2)]
        start_tables(k, a["x"], x1, place_of, agg)
        layer0(k, a, by_src, x1)
        by_dst = Order(k, "by_dst", [("pseudo", 2), ("basis", 8)])
        build_order(k, by_dst, k.rec_dram[d][1])
        k.recycle()
        layer1(k, a, by_dst, x1)
        norm_nodes(k, x1, table[0:N, :])
        k.recycle()
        with ExitStack() as st:
            pr = Propagation(k, st)
            locate(k, by_src, pr, place_of)
            propagate(k, by_src, pr, table)
        k.recycle()
        x3, h3, h4 = (nc.dram_tensor(n, (N, D), F32, kind="Internal").ap() for n in ("x3", "h3", "h4"))
        perceptron(k, a, table[0:N, :], x1, x3, h3)
        spline = Spline(k, stack, by_dst)
        conv(k, by_dst, spline, h3, a["L3_gnn_W1"], agg[0])
        root_pass(k, h3, a["L3_gnn_root1"], a["L3_gnn_bias1"], [agg[0]], h4, True)
        k.recycle()
        conv(k, by_dst, spline, h4, a["L3_gnn_W2"], agg[1])
        root_pass(k, h4, a["L3_gnn_root2"], a["L3_gnn_bias2"], [x3, agg[1]], out, False)


def kernel(**inputs):
    import concourse.bacc as bacc
    from concourse.bass_utils import run_bass_kernel_spmd

    nc = bacc.Bacc("TRN2", target_bir_lowering=False, num_devices=1)
    arrays, args = {}, {}
    for name, value in inputs.items():
        value = np.ascontiguousarray(value)
        arrays[f"in_{name}_dram"] = value
        args[name] = nc.dram_tensor(f"in_{name}_dram", value.shape, mybir.dt.from_np(value.dtype),
                                    kind="ExternalInput").ap()
    out = nc.dram_tensor("out_0_dram", (N, D), F32, kind="ExternalOutput").ap()
    gnn_kernel(nc, args, out)
    return run_bass_kernel_spmd(nc, [arrays], core_ids=[0]).results[0]["out_0_dram"]
```

```python
from contextlib import ExitStack, contextmanager

import numpy as np

import concourse.bass as bass
from concourse import mybir

P = 128
F32 = mybir.dt.float32
BF16 = mybir.dt.bfloat16
I32 = mybir.dt.int32
U8 = mybir.dt.uint8
RMAX = bass.bass_isa.ReduceOp.max
ALU = mybir.AluOpType
ACT = mybir.ActivationFunctionType
AX = mybir.AxisListType

N, D = 50000, 64
E = 25000
T = 196
SLOTS = P * T
CH = 14
NCH = T // CH
NIT = NCH // 2
REC = 16
NO_KEY = 65535
DIG = 256
FULL_P = E // T
TAIL = E - FULL_P * T


def wait_for(eng, sem, count):
    if not isinstance(count, int) or count > 0:
        eng.wait_ge(sem, count)


class Chain:

    def __init__(self, eng, sem, per=0):
        self.eng, self.sem, self.per, self.n, self.base = eng, sem, per, 0, 0

    def turn(self, i):
        assert self.n in (0, self.per), self.n
        self.base, self.n = i * self.per, 0

    def link(self, ins):
        ins.then_inc(self.sem, 1)
        self.n += 1
        self.eng.wait_ge(self.sem, self.base + self.n)


class Core:

    def __init__(self, nc, stack):
        self.nc, self.stack, self.phases = nc, stack, 0
        self.sems, self.sem_stack = [], stack.enter_context(ExitStack())

    def phase(self, name):
        self.phases += 1
        self.prefix = f"{name}{self.phases}_"

    def sb(self, name, shape, dt, stack=None):
        return (stack or self.stack).enter_context(self.nc.sbuf_tensor(self.prefix + name, shape, dt))

    def pb(self, name, shape, dt, stack=None):
        return (stack or self.stack).enter_context(self.nc.psum_tensor(self.prefix + name, shape, dt))

    def sem(self, name, stack=None):
        self.sems.append(self.sem_stack.enter_context(self.nc.semaphore(self.prefix + name)))
        return self.sems[-1]

    def recycle(self):
        with self.nc.Block() as block:
            @block.gpsimd
            def _(pool):
                pool.dma_reset()
                for s in self.sems:
                    pool.sem_clear(s)
        self.sem_stack.close()
        self.sems = []


def constants(k):
    nc = k.nc
    k.ident = k.sb("ident", [P, P], F32)
    k.identb = k.sb("identb", [P, P], BF16)
    k.onesb = k.sb("onesb", [P, P], BF16)
    k.ones = k.sb("ones", [P, P], F32)
    k.below = k.sb("below", [P, P], BF16)
    k.digits = k.sb("digits", [P, DIG], BF16)
    k.slot = k.sb("slot", [P, T], I32)
    with ExitStack() as st:
        digits_i = k.sb("digits_i", [P, DIG], I32, st)
        made = k.sem("const_made", st)
        block = st.enter_context(nc.Block())

        @block.gpsimd
        def _(pool):
            pool.memset(k.ident[:, :], 0.0).then_inc(made, 1)
            pool.memset(k.ones[:, :], 1.0).then_inc(made, 1)
            pool.memset(k.onesb[:, :], 1.0).then_inc(made, 1)
            pool.iota(digits_i[:, :], [[1, DIG]], base=0, channel_multiplier=0).then_inc(made, 1)
            pool.iota(k.slot[:, :], [[1, T]], base=0, channel_multiplier=T).then_inc(made, 1)
            pool.wait_ge(made, 5)
            pool.affine_select(out=k.ident[:, :], in_=k.ident[:, :], compare_op=ALU.not_equal, fill=1.0,
                               base=0, pattern=[[-1, P]], channel_multiplier=1).then_inc(made, 1)
            pool.affine_select(out=k.below[:, :], in_=k.onesb[:, :], compare_op=ALU.is_gt, fill=0.0,
                               base=0, pattern=[[1, P]], channel_multiplier=-1).then_inc(made, 1)
            pool.wait_ge(made, 7)
            pool.tensor_copy(k.identb[:, :], k.ident[:, :]).then_inc(made, 1)
            pool.tensor_copy(k.digits[:, :], digits_i[:, :]).then_inc(made, 1)
            pool.wait_ge(made, 9)


def load_records(k, keys, others, attrs, rec):
    nc = k.nc
    k.phase("load")
    with ExitStack() as st:
        words = 2 + sum(w for _, w in attrs)
        flat = k.sb("rec_in", [P, words * T], I32, st)
        cleared, landed, filed = (k.sem(x, st) for x in ("rec_cleared", "rec_landed", "rec_filed"))
        block = st.enter_context(nc.Block())
        parts = [(keys.rearrange("(e w) -> e w", w=1), 1), (others.rearrange("(e w) -> e w", w=1), 1), *attrs]

        @block.vector
        def _(dve):
            dve.memset(flat[:, 0:T], NO_KEY).then_inc(cleared, 1)
            dve.memset(flat[:, T:words * T], 0).then_inc(cleared, 1)
            dve.memset(rec[:, :, :], 0).then_inc(cleared, 1)
            dve.wait_ge(cleared, 3)
            dve.wait_ge(landed, 32 * len(parts))
            at = w0 = 0
            for _, w in parts:
                src = flat[:, at:at + w * T].rearrange("p (t w) -> p t w", w=w)
                dve.tensor_copy(rec[:, :, w0:w0 + w], src).then_inc(filed, 1)
                at, w0 = at + w * T, w0 + w
            dve.wait_ge(filed, len(parts))

        @block.sync
        def _(sp):
            sp.wait_ge(cleared, 2)
            at = 0
            for ap, w in parts:
                sp.dma_start(flat[0:FULL_P, at:at + w * T],
                             ap[0:FULL_P * T, :].rearrange("(p t) w -> p (t w)", t=T)).then_inc(landed, 16)
                sp.dma_start(flat[FULL_P:FULL_P + 1, at:at + w * TAIL],
                             ap[FULL_P * T:E, :].rearrange("(p t) w -> p (t w)", p=1)).then_inc(landed, 16)
                at += w * T
            sp.wait_ge(landed, 32 * len(parts))


def bound_register(pool, k, bound):
    none = pool.alloc_register(k.prefix + "none")
    limit = pool.alloc_register(k.prefix + "limit")
    pool.reg_mov(none, 0)
    return limit, lambda: pool.reg_add(limit, none, bound)


def scatter_rows(pool, k, idx_all, table, bound, stages, idx_stage, staged, sent, rows_made=None, rows_all=None):
    limit, set_limit = bound_register(pool, k, bound)
    def turn(i):
        for s in range(2):
            c = 2 * i + s
            wait_for(pool, sent[s], i * 16 * CH)
            pool.wait_ge(k.opened, 1)
            n = 1
            pool.tensor_copy(idx_stage[s][:, :], idx_all[:, bass.ds(c * CH, CH)]).then_inc(staged, 1)
            if rows_all is not None:
                pool.tensor_copy(stages[s][:, :, :], rows_all[:, bass.ds(c * CH, CH), :]).then_inc(staged, 1)
                n = 2
            pool.wait_ge(staged, (i * 2 + s + 1) * n)
            if rows_made is not None:
                pool.wait_ge(rows_made, c + 1)
            set_limit()
            for t in range(CH):
                pool.indirect_dma_start(
                    table, bass.IndirectOffsetOnAxis(ap=idx_stage[s][:, t:t + 1], axis=0),
                    stages[s][:, t, :], None, bounds_check=limit, oob_is_err=False).then_inc(sent[s], 16)

    turn(0)
    with pool.Fori(1, NIT) as i:
        turn(i)
    for s in range(2):
        pool.wait_ge(sent[s], NIT * 16 * CH)


def gather_rows(pool, k, table, bound, idxs, stages, idx_stage, staged, landed, freed, per_turn, turn0=0, limits=None, ready=None):
    limit, set_limit = bound_register(pool, k, bound) if limits is None else limits

    def turn(i):
        for s in range(2):
            c = 2 * i + s
            wait_for(pool, freed[s], (turn0 + i) * per_turn)
            if ready is not None:
                pool.wait_ge(*ready)
            pool.wait_ge(k.opened, 1)
            for g, idx in enumerate(idxs):
                pool.tensor_copy(idx_stage[s][:, g, :], idx[:, bass.ds(c * CH, CH)]).then_inc(staged, 1)
            pool.wait_ge(staged, ((turn0 + i) * 2 + s + 1) * len(idxs))
            set_limit()
            for t in range(CH):
                for g in range(len(idxs)):
                    pool.indirect_dma_start(
                        stages[s][:, t, g, :], None, table,
                        bass.IndirectOffsetOnAxis(ap=idx_stage[s][:, g, t:t + 1], axis=0),
                        bounds_check=limit, oob_is_err=False).then_inc(landed[s], 16)

    start = 0
    if isinstance(turn0, int):
        turn(0)
        start = 1
    with pool.Fori(start, NIT) as i:
        turn(i)


def sort_step(k, rank=None, scatter=None, beside=None):
    nc = k.nc
    k.phase("sort")
    with ExitStack() as st:
        opened = k.opened = k.sem("sort_open", st)
        if scatter:
            stages = [k.sb(f"rec_stage{s}", [P, CH, REC], I32, st) for s in range(2)]
            idxs = [k.sb(f"rec_idx{s}", [P, CH], I32, st) for s in range(2)]
            staged = k.sem("rec_staged", st)
            sent = [k.sem(f"rec_sent{s}", st) for s in range(2)]
        if rank:
            rec, place, shift, source = rank
            dig_i = k.sb("dig_i", [P, T], I32, st)
            dig = k.sb("dig", [P, T], BF16, st)
            hot = k.sb("hot", [P, T + 1, DIG], BF16, st)
            cnt = k.sb("cnt", [P, DIG], BF16, st)
            tot = k.sb("tot", [P, DIG], F32, st)
            upto = k.sb("upto", [P, DIG], F32, st)
            start = k.sb("start", [P, DIG], F32, st)
            one = k.sb("one", [P, DIG], F32, st)
            prod = k.sb("prod", [P, 2, DIG], F32, st)
            rank_f = k.sb("rank_f", [P, T], F32, st)
            ps_cnt = k.pb("ps_cnt", [P, 512], F32, st)
            ps_tot = k.pb("ps_tot", [P, 512], F32, st)
            ps_x = [k.pb(f"ps_x{h}", [P, 512], F32, st) for h in range(2)]
            landed, dve_done, hot_made, counted, cnt_copied, totalled, start_made = (
                k.sem(x, st) for x in ("srt_landed", "srt_dve", "hot_made", "counted", "cnt_copied",
                                       "totalled", "start_made"))
            x_ready = [k.sem(f"x_ready{h}", st) for h in range(2)]
            x_read = [k.sem(f"x_read{h}", st) for h in range(2)]
            HOT = 28
        block = st.enter_context(nc.Block())

        @block.gpsimd
        def _(pool):
            if scatter:
                s_rec, s_rank, s_table = scatter
                pool.engine_nop().then_inc(opened, 1)
                scatter_rows(pool, k, s_rank, s_table, SLOTS - 1, stages, idxs, staged, sent, rows_all=s_rec)

        if not rank:
            if beside is not None:
                beside(st, block)
            return

        @block.sync
        def _(sp):
            if source is not None:
                sp.dma_start(rec[:, :, :].rearrange("p t w -> p (t w)"),
                             source.rearrange("(p t) w -> p (t w)", t=T)).then_inc(landed, 16)
                sp.wait_ge(landed, 16)

        if beside is not None:
            beside(st, block)

        @block.vector
        def _(dve):
            ch = Chain(dve, dve_done)
            if source is not None:
                dve.wait_ge(landed, 16)
            ch.link(dve.tensor_scalar(dig_i[:, :], rec[:, :, 0], shift, DIG - 1,
                                      ALU.logical_shift_right, ALU.bitwise_and))
            ch.link(dve.tensor_copy(dig[:, :], dig_i[:, :]))
            ch.link(dve.memset(hot[:, T, :], 0.0))
            ch.link(dve.memset(one[:, :], 1.0))
            for c in range(T // HOT):
                dve.tensor_tensor(
                    hot[:, c * HOT:(c + 1) * HOT, :],
                    dig[:, c * HOT:(c + 1) * HOT].rearrange("p (t o) -> p t o", o=1).to_broadcast([P, HOT, DIG]),
                    k.digits[:, :].rearrange("p (o d) -> p o d", o=1).to_broadcast([P, HOT, DIG]),
                    ALU.is_equal).then_inc(hot_made, 1)
            dve.wait_ge(counted, 1)
            dve.tensor_copy(cnt[:, :], ps_cnt[:, 0:DIG]).then_inc(cnt_copied, 1)
            dve.wait_ge(totalled, 1)
            ch.link(dve.tensor_copy(tot[:, :], ps_tot[:, 0:DIG]))
            ch.link(dve.tensor_tensor_scan(out=upto[:, :], data0=one[:, :], data1=tot[:, :], initial=0.0,
                                           op0=ALU.mult, op1=ALU.add))
            dve.tensor_tensor(start[:, :], upto[:, :], tot[:, :], ALU.subtract).then_inc(start_made, 1)
            with dve.Fori(0, T // 14) as i:
                for j in range(14):
                    h = j % 2
                    dve.wait_ge(x_ready[h], i * 7 + j // 2 + 1)
                    dve.scalar_tensor_tensor(
                        out=prod[:, h, :], in0=hot[:, bass.ds(i * 14 + j, 1), :].rearrange("p o d -> p (o d)"), scalar=1.0,
                        in1=ps_x[h][:, 0:DIG], op0=ALU.mult, op1=ALU.mult,
                        accum_out=rank_f[:, bass.ds(i * 14 + j, 1)]).then_inc(x_read[h], 1)
            dve.wait_ge(x_read[0], T // 2)
            dve.wait_ge(x_read[1], T // 2)
            ch.link(dve.tensor_copy(place[:, :], rank_f[:, :]))

        @block.tensor
        def _(pe):
            pe.wait_ge(hot_made, 1)
            pe.matmul(ps_cnt[:, 0:DIG], k.identb[:, :], hot[:, T, :], start=True, stop=True)
            with pe.Fori(0, T // HOT) as i:
                pe.wait_ge(hot_made, i + 1)
                for j in range(HOT):
                    pe.matmul(ps_cnt[:, 0:DIG], k.identb[:, :],
                              hot[:, bass.ds(i * HOT + j, 1), :].rearrange("p o d -> p (o d)"),
                              start=False, stop=True, skip_group_check=True)
            pe.matmul(ps_cnt[:, 0:DIG], k.identb[:, :], hot[:, T, :], start=False, stop=True,
                      skip_group_check=True).then_inc(counted, 1)
            pe.wait_ge(cnt_copied, 1)
            pe.matmul(ps_tot[:, 0:DIG], k.onesb[:, :], cnt[:, :], start=True, stop=True).then_inc(totalled, 1)
            pe.wait_ge(start_made, 1)
            for h in range(2):
                pe.matmul(ps_x[h][:, 0:DIG], k.ident[:, :], start[:, :], start=True, stop=False,
                          skip_group_check=True)
                last = pe.matmul(ps_x[h][:, 0:DIG], k.below[:, :], cnt[:, :], start=False, stop=h == 0,
                                 skip_group_check=True)
                if h:
                    last = pe.matmul(ps_x[h][:, 0:DIG], k.identb[:, :], hot[:, 0, :], start=False, stop=True,
                                     skip_group_check=True)
                last.then_inc(x_ready[h], 1)
            with pe.Fori(0, T // 14) as i:
                for j in range(14):
                    h = j % 2
                    pe.wait_ge(x_read[h], i * 7 + j // 2 + 1)
                    for q in range(2):
                        last = pe.matmul(ps_x[h][:, 0:DIG], k.identb[:, :],
                                         hot[:, bass.ds(i * 14 + (j + q), 1), :].rearrange("p o d -> p (o d)"),
                                         start=False, stop=True, skip_group_check=True)
                    last.then_inc(x_ready[h], 1)


def shift_columns(k, keyx, landed, sp):
    sp.dma_start(keyx[1:P, 0:1], keyx[0:P - 1, T:T + 1]).then_inc(landed, 16)
    sp.dma_start(keyx[0:P - 1, T + 1:T + 2], keyx[1:P, 1:2]).then_inc(landed, 16)


class Order:

    def __init__(self, k, name, attrs):
        k.phase(name)
        self.attrs = attrs
        self.key = k.sb("key", [P, T], I32)
        self.other = k.sb("other", [P, T], I32)
        self.last_row = k.sb("last_row", [P, T], I32)
        self.same = k.sb("same", [P, T], F32)
        self.cont = k.sb("cont", [P, T], F32)
        self.whole = k.sb("whole", [D + 1, P], F32)
        self.mask = k.sb("mask", [P, NCH, CH], BF16)
        self.val = {n: k.sb(n, [P, T, w], F32) for n, w in attrs}


def build_order(k, o, records):
    nc = k.nc
    k.phase("order")
    with ExitStack() as st:
        rec = k.sb("rec", [P, T, REC], I32, st)
        keyx = k.sb("keyx", [P, T + 2], F32, st)
        after = k.sb("after", [P, T], F32, st)
        tmp = k.sb("tmp", [P, T], F32, st)
        wide = k.sb("wide", [P, D + 1], F32, st)
        ps = k.pb("ps", [P, 512], F32, st)
        landed, shifted, key_made, done, wide_made, whole_made = (
            k.sem(x, st) for x in ("landed", "shifted", "key_made", "done", "wide_made", "whole_made"))
        block = st.enter_context(nc.Block())

        @block.sync
        def _(sp):
            sp.dma_start(rec[:, :, :].rearrange("p t w -> p (t w)"),
                         records.rearrange("(p t) w -> p (t w)", t=T)).then_inc(landed, 16)
            sp.wait_ge(landed, 16)
            sp.wait_ge(key_made, 1)
            shift_columns(k, keyx, shifted, sp)
            sp.wait_ge(shifted, 32)

        @block.tensor
        def _(pe):
            pe.wait_ge(wide_made, 1)
            pe.matmul(ps[0:D + 1, 0:P], wide[:, :], k.ident[:, :], start=True, stop=True).then_inc(whole_made, 1)

        @block.vector
        def _(dve):
            ch = Chain(dve, done)
            ch.link(dve.memset(keyx[:, :], -1.0))
            dve.wait_ge(landed, 16)
            dve.tensor_copy(keyx[:, 1:T + 1], rec[:, :, 0]).then_inc(key_made, 1)
            at = 2
            for name, w in o.attrs:
                ch.link(dve.tensor_copy(o.val[name][:, :, :], rec[:, :, at:at + w].bitcast(F32)))
                at += w
            ch.link(dve.tensor_scalar(o.key[:, :], rec[:, :, 0], float(N - 1), None, ALU.min))
            ch.link(dve.tensor_copy(o.other[:, :], rec[:, :, 1]))
            dve.wait_ge(key_made, 1)
            dve.wait_ge(shifted, 32)
            key = keyx[:, 1:T + 1]
            ch.link(dve.tensor_tensor(o.same[:, :], key, keyx[:, 0:T], ALU.is_equal))
            ch.link(dve.tensor_scalar(o.cont[:, :], key, keyx[:, 1:2], o.same[:, 0:1], ALU.is_equal, ALU.mult))
            ch.link(dve.memset(o.same[:, 0:1], 0.0))
            ch.link(dve.tensor_copy(o.mask[:, :, :], o.same[:, :].rearrange("p (c t) -> p c t", t=CH)))
            ch.link(dve.memset(o.mask[:, :, 0:1], 0.0))
            ch.link(dve.tensor_tensor(after[:, :], key, keyx[:, 2:T + 2], ALU.not_equal))
            ch.link(dve.scalar_tensor_tensor(out=tmp[:, :], in0=key, scalar=float(-NO_KEY), in1=after[:, :],
                                             op0=ALU.add, op1=ALU.mult))
            ch.link(dve.tensor_scalar(o.last_row[:, :], tmp[:, :], float(NO_KEY), None, ALU.add))
            ch.link(dve.memset(wide[:, :], 1.0))
            dve.tensor_scalar(wide[:, :], wide[:, :], o.cont[:, T - 1:T], None, ALU.mult).then_inc(wide_made, 1)
            dve.wait_ge(whole_made, 1)
            ch.link(dve.tensor_copy(o.whole[:, :], ps[0:D + 1, 0:P]))


def ln_buffers(k, st, tag, n):
    b = {x: k.sb(f"{tag}_{x}", [P, n], F32, st) for x in ("sum", "mean", "ssq", "var", "sd", "rstd")}
    b["sq"] = k.sb(f"{tag}_sq", [P, n, D], F32, st)
    b |= {x: k.sem(f"{tag}_{x}", st) for x in ("centred", "squared", "var_made", "sd_made")}
    b["n"] = n
    return b


def ln_vector(dve, ch, b, x, xc, y, call, floor, freed=None):
    ln_centre(dve, ch, b, x, xc)
    ln_var(dve, ch, b, call, freed)
    return ln_scale(dve, ch, b, xc, y, call, floor)


def ln_centre(dve, ch, b, x, xc):
    ch.link(dve.tensor_reduce(b["sum"][:, :], x, AX.X, ALU.add))
    ch.link(dve.tensor_scalar(b["mean"][:, :], b["sum"][:, :], 1.0 / D, None, ALU.mult))
    mean = b["mean"][:, :].rearrange("p (n o) -> p n o", o=1).to_broadcast([P, b["n"], D])
    dve.tensor_tensor(xc, x, mean, ALU.subtract).then_inc(b["centred"], 1)


def ln_var(dve, ch, b, call, freed=None):
    dve.wait_ge(b["squared"], call + 1)
    ssq = dve.tensor_reduce(b["ssq"][:, :], b["sq"][:, :, :], AX.X, ALU.add)
    if freed is None:
        ch.link(ssq)
    else:
        ssq.then_inc(freed[0], 1)
        dve.wait_ge(*freed)
    dve.tensor_scalar(b["var"][:, :], b["ssq"][:, :], 1.0 / D, 1e-5, ALU.mult, ALU.add).then_inc(b["var_made"], 1)


def ln_scale(dve, ch, b, xc, y, call, floor):
    dve.wait_ge(b["sd_made"], call + 1)
    ch.link(dve.reciprocal(b["rstd"][:, :], b["sd"][:, :]))
    rstd = b["rstd"][:, :].rearrange("p (n o) -> p n o", o=1).to_broadcast([P, b["n"], D])
    if floor is None:
        return dve.tensor_tensor(y, xc, rstd, ALU.mult)
    return dve.scalar_tensor_tensor(out=y, in0=xc, scalar=floor, in1=rstd, op0=ALU.max, op1=ALU.mult)


LN_LINKS = 4


def ln_scalar(act, b, xc, call, after_read=None):
    ln_square(act, b, xc, call)
    if after_read is not None:
        after_read()
    ln_root(act, b, call)


def ln_square(act, b, xc, call):
    act.wait_ge(b["centred"], call + 1)
    act.activation(b["sq"][:, :, :], xc, ACT.Square).then_inc(b["squared"], 1)


def ln_root(act, b, call):
    act.wait_ge(b["var_made"], call + 1)
    act.activation(b["sd"][:, :], b["var"][:, :], ACT.Sqrt).then_inc(b["sd_made"], 1)


def spread(ap, *shape):
    return ap.to_broadcast(list(shape))


BIG = 1.5e38
FMAX = 3.4028234663852886e38
PI = float(np.pi)


class Scan:

    def __init__(self, k, st, tag, o, f, largest=False, mask=None):
        self.own_mask = mask is None
        self.k, self.o, self.f, self.largest, self.tag = k, o, f, largest, tag
        self.mask = k.sb(f"{tag}_mask", [P, NCH, f, CH], BF16 if largest else U8, st) if mask is None else mask
        self.prev = k.sb(f"{tag}_prev", [P, P], F32, st)
        self.carry_t = k.sb(f"{tag}_carry_t", [P, P + 1], F32, st)
        self.carry = k.sb(f"{tag}_carry", [P, f], F32, st)
        if largest:
            self.wall = k.sb(f"{tag}_wall", [P, T], F32, st)
            self.far = k.sb(f"{tag}_far", [P, T], F32, st)
            self.chain = k.sb(f"{tag}_chain", [f, P], F32, st)
        self.turned, self.scanned, self.back = (k.sem(f"{tag}_{x}", st) for x in ("turned", "scanned", "back"))

    def prepare(self, dve, ch):
        o, f = self.o, self.f
        for_all = o.mask[:, :, :].rearrange("p c (o t) -> p c o t", o=1).to_broadcast([P, NCH, f, CH])
        zero = -BIG if self.largest else 0.0
        if self.own_mask:
            ch.link(dve.tensor_copy(self.mask[:, :, :, :], for_all))
        ch.link(dve.memset(self.carry_t[:, :], zero))
        ch.link(dve.memset(self.prev[:, :], zero))
        if self.largest:
            flat = self.mask[:, :, :, :].rearrange("p c f t -> p (c f t)")
            for out, x in ((flat, flat), (self.wall[:, :], o.same[:, :]), (self.far[:, :], o.cont[:, :]),
                           (self.chain[:, :], o.whole[0:f, :])):
                ch.link(dve.tensor_scalar(out, x, -1.0, BIG, ALU.add, ALU.mult))

    LINKS = 2

    def chunk(self, dve, ch, buf, c, run_made, turn=None):
        first = buf[:, :, 0]
        if self.largest:
            ch.link(dve.scalar_tensor_tensor(out=first, in0=self.prev[:, 0:self.f], scalar=self.wall[:, bass.ds(c * CH, 1)],
                                             in1=first, op0=ALU.add, op1=ALU.max))
        else:
            ch.link(dve.scalar_tensor_tensor(out=first, in0=self.prev[:, 0:self.f], scalar=self.o.same[:, bass.ds(c * CH, 1)],
                                             in1=first, op0=ALU.mult, op1=ALU.add))
        flat = buf.rearrange("p f t -> p (f t)")
        mask = self.mask[:, bass.ds(c, 1), 0:self.f, :].rearrange("p o f t -> p (o f t)")
        op0, op1 = (ALU.add, ALU.max) if self.largest else (ALU.mult, ALU.add)
        ch.link(dve.tensor_tensor_scan(out=flat, data0=mask, data1=flat, initial=0.0, op0=op0, op1=op1))
        dve.tensor_copy(self.prev[:, 0:self.f], buf[:, :, CH - 1]).then_inc(run_made, 1)
        dve.wait_ge(run_made, (c if turn is None else turn) + 1)

    def carries_vector(self, dve, ps, n=0):
        f = self.f
        dve.wait_ge(self.turned, n + 1)
        data0 = self.chain if self.largest else self.o.whole
        op0, op1 = (ALU.add, ALU.max) if self.largest else (ALU.mult, ALU.add)
        dve.tensor_tensor_scan(out=self.carry_t[0:f, 1:P + 1], data0=data0[0:f, :], data1=ps[0:f, 0:P],
                               initial=-BIG if self.largest else 0.0, op0=op0, op1=op1).then_inc(self.scanned, 1)
        dve.wait_ge(self.back, n + 1)
        return dve.tensor_copy(self.carry[:, :], ps[:, 256:256 + f])

    def carries_tensor(self, pe, ps, n=0):
        pe.transpose(ps[:, 0:P], self.prev[:, :], self.k.ident[:, :]).then_inc(self.turned, 1)
        pe.wait_ge(self.scanned, n + 1)
        pe.transpose(ps[:, 2 * P:3 * P], self.carry_t[:, 0:P], self.k.ident[:, :]).then_inc(self.back, 1)


def row(ap):
    return ap.rearrange("(o n) -> o n", o=1)


def col(ap):
    return ap.rearrange("(n o) -> n o", o=1)


def layer0(k, a, o, x1):
    nc = k.nc
    with ExitStack() as layer:
        k.phase("att")
        xs = k.sb("xs", [P, T, D], F32, layer)
        v = k.sb("v", [P, T, D], F32, layer)
        hs = k.sb("hs", [P, T, 2], F32, layer)
        att_rows(k, a, o, xs, v, hs)
        att = k.sb("att", [P, T], F32, layer)
        att_weights(k, a, o, hs, att)
        att_sums(k, o, xs, v, att, x1)


def att_rows(k, a, o, xs, v, hs):
    nc = k.nc
    k.phase("att_rows")
    G2 = 2 * CH
    GROUPS = CH // 2
    with ExitStack() as st:
        k.opened = k.sem("opened", st)
        gb = [k.sb(f"rows{s}", [P, CH, 2, D], F32, st) for s in range(2)]
        idx = [k.sb(f"idx{s}", [P, 2, CH], I32, st) for s in range(2)]
        wbd = k.sb("wbd", [P, 3 * D], F32, st)
        b2 = k.sb("b2", [P, 2 * D], F32, st)
        b1 = k.sb("b1", [P, D], F32, st)
        xc = k.sb("xc", [P, G2, D], F32, st)
        xc2 = k.sb("xc2", [P, G2, D], F32, st)
        h = [k.sb(f"h{s}", [P, G2, D], F32, st) for s in range(2)]
        q = k.sb("q", [P, G2, D], F32, st)
        ht = k.sb("ht", [P, 2, 256], F32, st)
        hsum = k.sb("hsum", [P, G2], F32, st)
        ln1, ln2 = ln_buffers(k, st, "ln1", G2), ln_buffers(k, st, "ln2", G2)
        ps_t = [k.pb(f"ps_t{g}", [P, 512], F32, st) for g in range(2)]
        ps_y = [k.pb(f"ps_y{g}", [P, 512], F32, st) for g in range(2)]
        staged, w_clear, w_landed, chain1, chain2, h_made, turned, ht_made, y_made, y_read, q_added, q_made = (
            k.sem(x, st) for x in ("staged", "w_clear", "w_landed", "chain1", "chain2", "h_made", "turned", "ht_made",
                                   "y_made", "y_read", "q_added", "q_made"))
        landed = [k.sem(f"landed{s}", st) for s in range(2)]
        freed = [k.sem(f"freed{s}", st) for s in range(2)]
        block = st.enter_context(nc.Block())

        @block.sync
        def _(sp):
            sp.wait_ge(w_clear, 1)
            for r, c, w in ((0, 0, "L0_gnn_W2"), (D, D, "L0_gnn_W2"), (D, 2 * D, "L0_gnn_W1")):
                sp.dma_start(wbd[r:r + D, c:c + D], a[w]).then_inc(w_landed, 16)
            for g in range(2):
                sp.dma_start(b2[:, g * D:(g + 1) * D], row(a["L0_gnn_b2"]).to_broadcast([P, D])).then_inc(w_landed, 16)
            sp.dma_start(b1[:, :], row(a["L0_gnn_b1"]).to_broadcast([P, D])).then_inc(w_landed, 16)
            sp.wait_ge(w_landed, 96)

        @block.gpsimd
        def _(pool):
            pool.engine_nop().then_inc(k.opened, 1)
            gather_rows(pool, k, a["x"], N - 1, [o.key, o.other], gb, idx, staged, landed, freed, 1)

        @block.scalar
        def _(act):
            def square(c, s):
                ln_square(act, ln1, xc[:, :, :], c)
                act.activation(xs[:, bass.ds(c * CH, CH), :], gb[s][:, :, 0, :], ACT.Copy).then_inc(freed[s], 1)

            def chunk(c, s, more):
                for g in range(GROUPS):
                    if g == 2 and more:
                        square(c + 1, 1 - s)
                    act.wait_ge(turned, c * GROUPS + g + 1)
                    if g >= 2:
                        act.wait_ge(y_made, c * GROUPS + g - 1)
                    act.activation(ht[:, g % 2, :], ps_t[g % 2][:, 0:256], ACT.Copy).then_inc(ht_made, 1)
                act.wait_ge(q_added, c + 1)
                act.activation(q[:, :, :], q[:, :, :], ACT.Relu).then_inc(q_made, 1)
                if more:
                    ln_root(act, ln1, c + 1)
                ln_scalar(act, ln2, xc2[:, :, :], c)

            square(0, 0)
            ln_root(act, ln1, 0)
            with act.Fori(0, NIT - 1) as i:
                for s in range(2):
                    chunk(2 * i + s, s, True)
            chunk(NCH - 2, 0, True)
            chunk(NCH - 1, 1, False)

        @block.tensor
        def _(pe):
            pe.wait_ge(w_landed, 96)
            def chunk(c, s):
                pe.wait_ge(h_made, c + 1)
                for g in range(GROUPS + 1):
                    if g < GROUPS:
                        if g >= 2:
                            pe.wait_ge(ht_made, c * GROUPS + g - 1)
                        for j in range(2):
                            last = pe.transpose(ps_t[g % 2][:, j * P:(j + 1) * P],
                                                h[s][:, 2 * (2 * g + j):2 * (2 * g + j) + 2, :].rearrange("p n f -> p (n f)"),
                                                k.ident[:, :])
                        last.then_inc(turned, 1)
                    if g >= 1:
                        m = g - 1
                        pe.wait_ge(ht_made, c * GROUPS + m + 1)
                        if m >= 2:
                            pe.wait_ge(y_read, c * GROUPS + m - 1)
                        for j in range(2):
                            last = pe.matmul(ps_y[m % 2][:, j * 3 * D:(j + 1) * 3 * D], ht[:, m % 2, j * P:(j + 1) * P],
                                             wbd[:, :], start=True, stop=True)
                        last.then_inc(y_made, 1)

            with pe.Fori(0, NIT) as i:
                for s in range(2):
                    chunk(2 * i + s, s)

        @block.vector
        def _(dve):
            dve.memset(wbd[:, :], 0.0).then_inc(w_clear, 1)
            dve.wait_ge(w_landed, 96)
            ch1 = Chain(dve, chain1, LN_LINKS)
            ch2 = Chain(dve, chain2, LN_LINKS + 2)

            def centre(c, s, turn):
                ch1.turn(c)
                dve.wait_ge(landed[s], turn * 16 * G2)
                dve.wait_ge(k.opened, 1)
                ln_centre(dve, ch1, ln1, gb[s][:, :, :, :].rearrange("p t g f -> p (t g) f"), xc[:, :, :])

            def scale(c, s):
                wait_for(dve, turned, (c - 1) * GROUPS)
                ln_scale(dve, ch1, ln1, xc[:, :, :], h[s][:, :, :], c, 0.0).then_inc(h_made, 1)
                dve.wait_ge(h_made, c + 1)

            def chunk(c, s, turn):
                if turn is not None:
                    centre(c + 1, 1 - s, turn)
                ch2.turn(c)
                for g in range(GROUPS):
                    dve.wait_ge(y_made, c * GROUPS + g + 1)
                    y = ps_y[g % 2][:, 0:6 * D].rearrange("p (t n) -> p t n", t=2)
                    q_in = dve.tensor_tensor(
                        q[:, 4 * g:4 * g + 4, :].rearrange("p (t g) f -> p t (g f)", t=2), y[:, :, 0:2 * D],
                        b2[:, :].rearrange("p (o n) -> p o n", o=1).to_broadcast([P, 2, 2 * D]), ALU.add)
                    if g == GROUPS - 1:
                        q_in.then_inc(q_added, 1)
                    dve.tensor_tensor(
                        v[:, bass.ds(c * CH + 2 * g, 2), :], y[:, :, 2 * D:3 * D],
                        b1[:, :].rearrange("p (o n) -> p o n", o=1).to_broadcast([P, 2, D]),
                        ALU.add).then_inc(y_read, 1)
                if turn is not None:
                    ln_var(dve, ch1, ln1, c + 1)
                dve.wait_ge(q_made, c + 1)
                ln_centre(dve, ch2, ln2, q[:, :, :], xc2[:, :, :])
                if turn is not None:
                    scale(c + 1, 1 - s)
                ln_var(dve, ch2, ln2, c)
                ch2.link(ln_scale(dve, ch2, ln2, xc2[:, :, :], q[:, :, :], c, None))
                ch2.link(dve.tensor_reduce(hsum[:, :], q[:, :, :], AX.X, ALU.add))
                dve.tensor_tensor(hs[:, bass.ds(c * CH, CH), :].rearrange("p t g -> p (t g)"), hsum[:, :],
                                  hsum[:, :], ALU.mult)

            def turn(i):
                for s in range(2):
                    chunk(2 * i + s, s, i + 1 + s)

            centre(0, 0, 1)
            ln_var(dve, ch1, ln1, 0)
            scale(0, 0)
            turn(0)
            with dve.Fori(1, NIT - 1) as i:
                turn(i)
            chunk(NCH - 2, 0, NIT)
            chunk(NCH - 1, 1, None)


def att_weights(k, a, o, hs, att):
    nc = k.nc
    k.phase("att_weights")
    ROUND = 1.5 * 2.0 ** 23
    with ExitStack() as st:
        valid, low, x, y, diff, z = (k.sb(n, [P, T], F32, st) for n in ("valid", "low", "x", "y", "diff", "z"))
        ends = k.sb("ends", [P, 2], F32, st)
        ends_all = k.sb("ends_all", [P, 2], F32, st)
        sc = k.sb("sc", [P, 3], F32, st)
        chain, ends_made, all_made, arg_made, att_made = (
            k.sem(n, st) for n in ("chain", "ends_made", "all_made", "arg_made", "att_made"))
        block = st.enter_context(nc.Block())

        @block.vector
        def _(dve):
            ch = Chain(dve, chain)
            source, other = hs[:, :, 0], hs[:, :, 1]
            ch.link(dve.tensor_scalar(valid[:, :], k.slot[:, :], float(E), None, ALU.is_lt))
            ch.link(dve.tensor_scalar(low[:, :], valid[:, :], -1.0, BIG, ALU.add, ALU.mult))
            ch.link(dve.tensor_tensor(x[:, :], source, valid[:, :], ALU.mult))
            ch.link(dve.tensor_tensor(y[:, :], x[:, :], low[:, :], ALU.add))
            ch.link(dve.tensor_reduce(ends[:, 0:1], y[:, :], AX.X, ALU.max))
            ch.link(dve.tensor_tensor(y[:, :], low[:, :], x[:, :], ALU.subtract))
            dve.tensor_reduce(ends[:, 1:2], y[:, :], AX.X, ALU.max).then_inc(ends_made, 1)
            ch.link(dve.tensor_tensor(diff[:, :], source, other, ALU.subtract))
            dve.wait_ge(all_made, 1)
            ch.link(dve.tensor_tensor(sc[:, 0:1], ends_all[:, 0:1], ends_all[:, 1:2], ALU.add))
            ch.link(dve.tensor_scalar(sc[:, 1:2], sc[:, 0:1], 2.0, 1e-10, ALU.mult, ALU.add))
            ch.link(dve.reciprocal(sc[:, 2:3], sc[:, 1:2]))
            ch.link(dve.tensor_scalar(z[:, :], diff[:, :], sc[:, 2:3], 0.5, ALU.mult, ALU.mult))
            ch.link(dve.tensor_scalar(x[:, :], z[:, :], ROUND, None, ALU.add))
            ch.link(dve.tensor_scalar(y[:, :], x[:, :], -ROUND, None, ALU.add))
            ch.link(dve.tensor_tensor(x[:, :], z[:, :], y[:, :], ALU.subtract))
            ch.link(dve.scalar_tensor_tensor(out=y[:, :], in0=x[:, :], scalar=-1.0, in1=x[:, :], op0=ALU.mult,
                                             op1=ALU.max))
            dve.tensor_scalar(z[:, :], y[:, :], -2.0 * PI, 0.5 * PI, ALU.mult, ALU.add).then_inc(arg_made, 1)

        @block.gpsimd
        def _(pool):
            pool.wait_ge(ends_made, 1)
            pool.partition_all_reduce(ends_all[:, :], ends[:, :], P, RMAX).then_inc(all_made, 1)

        @block.scalar
        def _(act):
            act.wait_ge(arg_made, 1)
            act.activation(att[:, :], z[:, :], ACT.Sin).then_inc(att_made, 1)
            act.wait_ge(att_made, 1)


def chunk_cols(c):
    return bass.ds(c * CH, CH)


def att_sums(k, o, xs, v, att, x1):
    nc = k.nc
    k.phase("att_sums")
    F1 = D + 1
    with ExitStack() as st:
        k.opened = k.sem("opened", st)
        run = k.sb("run", [P, T, F1], F32, st)
        buf = k.sb("buf", [P, F1, CH], F32, st)
        buf2 = k.sb("buf2", [P, D, CH], F32, st)
        stages = [k.sb(f"stage{s}", [P, CH, D], F32, st) for s in range(2)]
        idx = [k.sb(f"idx{s}", [P, CH], I32, st) for s in range(2)]
        part = k.sb("part", [P, CH, D], F32, st)
        rs = k.sb("rs", [P, T], F32, st)
        rinv = k.sb("rinv", [P, T], F32, st)
        ps = [k.pb(f"ps{n}", [P, 512], F32, st) for n in range(2)]
        one = Scan(k, st, "one", o, F1)
        two = Scan(k, st, "two", o, D, mask=one.mask)
        staged, chain0, chain, chain2, chain3, rows_made, run1, run2, copied1, copied2 = (
            k.sem(n, st) for n in ("staged", "chain0", "chain", "chain2", "chain3", "rows_made", "run1", "run2",
                                   "copied1", "copied2"))
        sent = [k.sem(f"sent{s}", st) for s in range(2)]
        block = st.enter_context(nc.Block())

        @block.gpsimd
        def _(pool):
            pool.engine_nop().then_inc(k.opened, 1)
            scatter_rows(pool, k, o.last_row, x1, N - 1, stages, idx, staged, sent, rows_made)

        @block.tensor
        def _(pe):
            pe.wait_ge(run1, NCH)
            one.carries_tensor(pe, ps[0])
            pe.wait_ge(run2, NCH)
            two.carries_tensor(pe, ps[1])

        @block.scalar
        def _(act):
            with act.Fori(0, NCH) as c:
                act.wait_ge(run1, c + 1)
                act.wait_ge(k.opened, 1)
                act.activation(run[:, chunk_cols(c), :].rearrange("p t f -> p f t"), buf[:, :, :],
                               ACT.Copy).then_inc(copied1, 1)
                act.wait_ge(run2, c + 1)
                act.wait_ge(k.opened, 1)
                act.activation(v[:, chunk_cols(c), :].rearrange("p t f -> p f t"), buf2[:, :, :],
                               ACT.Copy).then_inc(copied2, 1)

        @block.vector
        def _(dve):
            ch = Chain(dve, chain0)
            one.prepare(dve, ch)
            two.prepare(dve, ch)
            ch = Chain(dve, chain, 3 + 2 * Scan.LINKS)
            def turn(c):
                ch.turn(c)
                wait_for(dve, copied1, c)
                vt = v[:, chunk_cols(c), :].rearrange("p t f -> p f t")
                at = att[:, chunk_cols(c)].rearrange("p (o t) -> p o t", o=1)
                ch.link(dve.tensor_tensor(buf[:, 0:D, :], vt, at.to_broadcast([P, D, CH]), ALU.mult))
                ch.link(dve.tensor_scalar(buf[:, D:F1, :], at, 1.0, None, ALU.mult))
                one.chunk(dve, ch, buf[:, :, :], c, run1)
                wait_for(dve, copied2, c)
                dve.wait_ge(k.opened, 1)
                ch.link(dve.tensor_scalar(buf2[:, :, :], vt, 1.0, None, ALU.mult))
                two.chunk(dve, ch, buf2[:, :, :], c, run2)

            turn(0)
            with dve.Fori(1, NCH) as c:
                turn(c)
            ch = Chain(dve, chain2)
            ch.link(one.carries_vector(dve, ps[0]))
            ch.link(two.carries_vector(dve, ps[1]))
            dve.wait_ge(copied1, NCH)
            dve.wait_ge(copied2, NCH)
            ch.link(dve.scalar_tensor_tensor(out=rs[:, :], in0=o.cont[:, :], scalar=one.carry[:, D:F1],
                                             in1=run[:, :, D], op0=ALU.mult, op1=ALU.add))
            ch.link(dve.reciprocal(rinv[:, :], rs[:, :]))
            ch = Chain(dve, chain3, 2 * 6)
            def turn(i):
                ch.turn(i)
                for s in range(2):
                    c = 2 * i + s
                    stage = stages[s]
                    wait_for(dve, sent[s], i * 16 * CH)
                    cont = spread(col_of(o.cont, c), P, CH, D)
                    ch.link(dve.tensor_tensor(part[:, :, :], cont, spread(across(one.carry, D), P, CH, D), ALU.mult))
                    ch.link(dve.tensor_tensor(part[:, :, :], part[:, :, :], run[:, chunk_cols(c), 0:D], ALU.add))
                    ch.link(dve.tensor_tensor(part[:, :, :], part[:, :, :], spread(col_of(rinv, c), P, CH, D), ALU.mult))
                    ch.link(dve.tensor_tensor(part[:, :, :], part[:, :, :], xs[:, chunk_cols(c), :], ALU.add))
                    ch.link(dve.tensor_tensor(stage[:, :, :], cont, spread(across(two.carry, D), P, CH, D), ALU.mult))
                    ch.link(dve.tensor_tensor(stage[:, :, :], stage[:, :, :], v[:, chunk_cols(c), :], ALU.add))
                    dve.scalar_tensor_tensor(out=stage[:, :, :], in0=stage[:, :, :], scalar=1e-10, in1=part[:, :, :],
                                             op0=ALU.mult, op1=ALU.add).then_inc(rows_made, 1)
                    dve.wait_ge(rows_made, c + 1)

            turn(0)
            with dve.Fori(1, NIT) as i:
                turn(i)


def col_of(x, c):
    return x[:, chunk_cols(c)].rearrange("p (t o) -> p t o", o=1)


def across(x, n):
    return x[:, 0:n].rearrange("p (o f) -> p o f", o=1)


GROUPS = CH // 2


def pair_weights(k, a, w):
    nc = k.nc
    k.phase("pair_weights")
    NB = 8
    with ExitStack() as st:
        w2 = k.sb("w2", [P, P], F32, st)
        w2t = k.sb("w2t", [P, P], F32, st)
        pi1 = k.sb("pi1", [P, D], F32, st)
        pi1t = k.sb("pi1t", [D, P], F32, st)
        pi2 = k.sb("pi2", [D, D], F32, st)
        pi12 = k.sb("pi12", [P, D], F32, st)
        pi3 = k.sb("pi3", [D, D, NB], F32, st)
        pi3b = k.sb("pi3b", [D, NB, D], F32, st)
        pi3t = k.sb("pi3t", [D, NB, D], F32, st)
        ii1 = k.sb("ii1", [D, D], F32, st)
        b2 = k.sb("b2", [P, 1], F32, st)
        bs = k.sb("bs", [D, 3], F32, st)
        ps = [k.pb(f"ps{n}", [P, 512], F32, st) for n in range(4)]
        cleared, landed, pe_done, dve_done = (k.sem(n, st) for n in ("cleared", "landed", "pe_done", "dve_done"))
        block = st.enter_context(nc.Block())
        g = lambda n: a["L1_gnn_" + n]
        loads = []
        for q in range(2):
            h = slice(q * D, (q + 1) * D)
            loads += [(w.first[h, h], g("pp_W1")), (w2[h, h], g("pp_W2")), (w.last[h, h], g("ii_W2")),
                      (w.first_b[h, :], col(g("pp_b1"))), (b2[h, :], col(g("pp_b2"))),
                      (w.tanh_b[h, :], col(g("ii_b1"))),
                      (w.last_b[:, h], row(g("ii_b2")).to_broadcast([P, D]))]
        loads += [(pi1[:, :], g("pi_W1")), (pi2[:, :], g("pi_W2")), (ii1[:, :], g("ii_W1")),
                  (pi3[:, :, :].rearrange("p c b -> p (c b)"), g("pi_W3")),
                  (bs[:, 0:1], col(g("pi_b1"))), (bs[:, 1:2], col(g("pi_b2")))]

        @block.sync
        def _(sp):
            sp.wait_ge(cleared, 3)
            for to, src in loads:
                sp.dma_start(to, src).then_inc(landed, 16)
            sp.wait_ge(landed, 16 * len(loads))

        @block.tensor
        def _(pe):
            pe.wait_ge(landed, 16 * len(loads))
            pe.transpose(ps[0][0:D, 0:P], pi1[:, :], k.ident[:, :])
            pe.transpose(ps[0][:, P:2 * P], w2[:, :], k.ident[:, :])
            pe.matmul(ps[0][0:D, 300:301], pi1[:, :], b2[:, :], start=True, stop=True).then_inc(pe_done, 1)
            pe.wait_ge(dve_done, 1)
            for b in range(NB):
                last = pe.transpose(ps[1][0:D, b * D:(b + 1) * D], pi3b[:, b, :], k.ident[0:D, 0:D])
            last.then_inc(pe_done, 1)
            pe.wait_ge(dve_done, 2)
            pe.matmul(ps[2][:, 0:D], pi1t[:, :], pi2[:, :], start=True, stop=True)
            pe.matmul(ps[2][0:D, D:D + 1], pi2[:, :], bs[:, 2:3], start=True, stop=True).then_inc(pe_done, 1)
            pe.wait_ge(dve_done, 3)
            for b in range(NB):
                last = pe.matmul(ps[3][0:D, b * D:(b + 1) * D], pi3t[:, b, :], ii1[:, :], start=True, stop=True)
            last.then_inc(pe_done, 1)
            pe.wait_ge(dve_done, 4)
            pe.matmul(ps[2][:, 2 * D:3 * D], w2t[:, :], pi12[:, :], start=True, stop=True).then_inc(pe_done, 1)

        @block.vector
        def _(dve):
            for x in (w.first, w2, w.last):
                dve.memset(x[:, :], 0.0).then_inc(cleared, 1)
            dve.wait_ge(landed, 16 * len(loads))
            dve.tensor_copy(pi3b[:, :, :], pi3[:, :, :].rearrange("p c b -> p b c")).then_inc(dve_done, 1)
            dve.wait_ge(pe_done, 1)
            dve.tensor_copy(pi1t[:, :], ps[0][0:D, 0:P])
            dve.tensor_copy(w2t[:, :], ps[0][:, P:2 * P])
            dve.tensor_tensor(bs[:, 2:3], ps[0][0:D, 300:301], bs[:, 0:1], ALU.add).then_inc(dve_done, 1)
            dve.wait_ge(pe_done, 2)
            dve.tensor_copy(pi3t[:, :, :].rearrange("p b c -> p (b c)"), ps[1][0:D, :]).then_inc(dve_done, 1)
            dve.wait_ge(pe_done, 3)
            dve.tensor_tensor(w.middle_b[:, :], ps[2][0:D, D:D + 1], bs[:, 1:2], ALU.add)
            dve.tensor_copy(pi12[:, :], ps[2][:, 0:D]).then_inc(dve_done, 1)
            dve.wait_ge(pe_done, 4)
            dve.tensor_copy(w.basis[:, :], ps[3][0:D, :])
            dve.wait_ge(pe_done, 5)
            dve.tensor_copy(w.middle[:, :], ps[2][:, 2 * D:3 * D]).then_inc(dve_done, 1)
            dve.wait_ge(dve_done, 5)


class PairWeights:
    def __init__(self, k, st):
        self.first = k.sb("first", [P, P], F32, st)
        self.first_b = k.sb("first_b", [P, 1], F32, st)
        self.middle = k.sb("middle", [P, D], F32, st)
        self.middle_b = k.sb("middle_b", [D, 1], F32, st)
        self.basis = k.sb("basis", [D, 8 * D], F32, st)
        self.tanh_b = k.sb("tanh_b", [P, 1], F32, st)
        self.last = k.sb("last", [P, P], F32, st)
        self.last_b = k.sb("last_b", [P, P], F32, st)


def layer1(k, a, o, x1):
    nc = k.nc
    with ExitStack() as st:
        k.phase("pairs")
        w = PairWeights(k, st)
        xs = k.sb("xs", [P, T, D], F32, st)
        run = k.sb("run", [P, T, D], F32, st)
        scan = Scan(k, st, "sum", o, D)
        pair_weights(k, a, w)
        pair_rows(k, o, w, x1, xs, run, scan)
        send_rows(k, o, scan, run, x1, N - 1, o.last_row, add=xs)


def pair_rows(k, o, w, x1, xs, run, scan):
    nc = k.nc
    k.phase("pair_rows")
    G2 = 2 * CH
    with ExitStack() as st:
        k.opened = k.sem("opened", st)
        gb = [k.sb(f"rows{s}", [P, CH, 2, D], F32, st) for s in range(2)]
        idx = [k.sb(f"idx{s}", [P, 2, CH], I32, st) for s in range(2)]
        xc = k.sb("xc", [P, G2, D], F32, st)
        h = [k.sb(f"h{s}", [P, G2, D], F32, st) for s in range(2)]
        ht = k.sb("ht", [P, 2, 2 * P], F32, st)
        tt = k.sb("tt", [P, 2, 2 * P], F32, st)
        ut = k.sb("ut", [D, 2, 2 * P], F32, st)
        prod = k.sb("prod", [P, 2, 8, D], F32, st)
        i1 = k.sb("i1", [P, 2, 2, D], F32, st)
        th = k.sb("th", [P, 2, P], F32, st)
        buf = [k.sb(f"buf{s}", [P, D, CH], F32, st) for s in range(2)]
        ln1 = ln_buffers(k, st, "ln", G2)
        ps_t, ps_p, ps_u, ps_e = (k.pb(n, [P, 512], F32, st) for n in ("ps_t", "ps_p", "ps_u", "ps_e"))
        ps_o = [k.pb(f"ps_o{n}", [P, 512], F32, st) for n in range(2)]
        ps_i = [k.pb(f"ps_i{j}", [P, 512], F32, st) for j in range(2)]
        (staged, chain1, chain2, chain0, h_made, turned, ht_made, p_made, tt_made, u_made, ut_made, i_made, i_read, i1_made,
         e_made, th_made, o_made, o_read, run_made, copied) = (
            k.sem(x, st) for x in ("staged", "chain1", "chain2", "chain0", "h_made", "turned", "ht_made", "p_made", "tt_made",
                                   "u_made", "ut_made", "i_made", "i_read", "i1_made", "e_made", "th_made",
                                   "o_made", "o_read", "run_made", "copied"))
        landed = [k.sem(f"landed{s}", st) for s in range(2)]
        freed = [k.sem(f"freed{s}", st) for s in range(2)]
        block = st.enter_context(nc.Block())

        @block.gpsimd
        def _(pool):
            pool.engine_nop().then_inc(k.opened, 1)
            gather_rows(pool, k, x1, N - 1, [o.other, o.key], gb, idx, staged, landed, freed, 1)

        END = NCH * GROUPS
        assert END % 2 == 0

        def lagged(n, g, s, stages):
            for lag, stage in stages:
                if not isinstance(n, int) or n + g >= lag:
                    stage(n + (g - lag), (s * GROUPS + g - lag) % 2)

        def lagged_rest(stages):
            for e in range(max(lag for lag, _ in stages)):
                for lag, stage in stages:
                    if lag > e:
                        stage(END + e - lag, (e - lag) % 2)

        @block.scalar
        def _(act):
            def copy_turned(m, ring):
                wait_for(act, p_made, m - 1)
                act.wait_ge(turned, m + 1)
                act.activation(ht[:, ring, :], ps_t[:, 0:2 * P], ACT.Copy).then_inc(ht_made, 1)

            def first_tanh(m, ring):
                wait_for(act, u_made, m - 1)
                act.wait_ge(p_made, m + 1)
                act.activation(tt[:, ring, :], ps_p[:, 0:2 * P], ACT.Tanh, bias=w.first_b[:, :]).then_inc(tt_made, 1)

            def middle(m, ring):
                wait_for(act, i_made, (m - 1) * 2)
                act.wait_ge(u_made, m + 1)
                act.activation(ut[:, ring, :], ps_u[0:D, 0:2 * P], ACT.Identity,
                               bias=w.middle_b[:, :]).then_inc(ut_made, 1)

            def second_tanh(m, ring):
                wait_for(act, o_made, m - 1)
                act.wait_ge(e_made, m + 1)
                act.activation(th[:, ring, :], ps_e[:, 0:P], ACT.Tanh, bias=w.tanh_b[:, :]).then_inc(th_made, 1)

            def square(c, s):
                ln_square(act, ln1, xc[:, :, :], c)
                act.activation(xs[:, chunk_cols(c), :], gb[s][:, :, 1, :], ACT.Copy).then_inc(freed[s], 1)

            def copy(c, s):
                act.wait_ge(run_made, c + 1)
                act.wait_ge(k.opened, 1)
                act.activation(run[:, chunk_cols(c), :].rearrange("p t f -> p f t"), buf[s][:, :, :],
                               ACT.Copy).then_inc(copied, 1)

            stages = ((0, copy_turned), (1, first_tanh), (2, middle), (4, second_tanh))

            def chunk(c, s, more):
                for g in range(GROUPS):
                    lagged(c * GROUPS, g, s, stages)
                    if g == 4 and more:
                        square(c + 1, 1 - s)
                    if g == 5:
                        if not isinstance(c, int) or c > 0:
                            copy(c - 1, 1 - s)
                        if more:
                            ln_root(act, ln1, c + 1)

            square(0, 0)
            ln_root(act, ln1, 0)
            chunk(0, 0, True)
            chunk(1, 1, True)
            with act.Fori(1, NIT - 1) as i:
                for s in range(2):
                    chunk(2 * i + s, s, True)
            chunk(NCH - 2, 0, True)
            chunk(NCH - 1, 1, False)
            lagged_rest(stages[1:])
            copy(NCH - 1, 1)

        @block.tensor
        def _(pe):
            def first(m, ring):
                wait_for(pe, tt_made, m)
                pe.wait_ge(ht_made, m + 1)
                pe.matmul(ps_p[:, 0:2 * P], w.first[:, :], ht[:, ring, :], start=True, stop=True).then_inc(p_made, 1)

            def middle(m, ring):
                wait_for(pe, ut_made, m)
                pe.wait_ge(tt_made, m + 1)
                pe.matmul(ps_u[0:D, 0:2 * P], w.middle[:, :], tt[:, ring, :], start=True, stop=True).then_inc(u_made, 1)

            def basis(m, ring):
                pe.wait_ge(ut_made, m + 1)
                for j in range(2):
                    if not isinstance(m, int) or m >= 1:
                        pe.wait_ge(i_read, (m - 1) * 2 + (j + 1))
                    pe.matmul(ps_i[j][:, :], ut[:, ring, j * P:(j + 1) * P], w.basis[:, :], start=True,
                              stop=True).then_inc(i_made, 1)

            def turn_i1(m, ring):
                wait_for(pe, th_made, m)
                pe.wait_ge(i1_made, m + 1)
                pe.transpose(ps_e[:, 0:P], i1[:, ring, :, :].rearrange("p t f -> p (t f)"), k.ident[:, :]).then_inc(e_made, 1)

            def last(m, ring):
                wait_for(pe, o_read, m - 1)
                pe.wait_ge(th_made, m + 1)
                pe.matmul(ps_o[ring][:, 0:P], th[:, ring, :], w.last[:, :], start=True, stop=True).then_inc(o_made, 1)

            stages = ((1, first), (2, middle), (5, last), (3, basis), (4, turn_i1))

            def turn(i):
                for s in range(2):
                    n = (2 * i + s) * GROUPS
                    pe.wait_ge(h_made, 2 * i + (s + 1))
                    for g in range(GROUPS):
                        wait_for(pe, ht_made, n + g)
                        for j in range(2):
                            turning = pe.transpose(ps_t[:, j * P:(j + 1) * P],
                                                   h[s][:, 4 * g + 2 * j:4 * g + 2 * j + 2, :].rearrange("p n f -> p (n f)"),
                                                   k.ident[:, :])
                        turning.then_inc(turned, 1)
                        lagged(n, g, s, stages)

            turn(0)
            with pe.Fori(1, NIT) as i:
                turn(i)
            lagged_rest(stages)

        @block.vector
        def _(dve):
            scan.prepare(dve, Chain(dve, chain0))
            ch1 = Chain(dve, chain1, LN_LINKS)
            ch2 = Chain(dve, chain2, Scan.LINKS)

            def centre(c, s, turn):
                ch1.turn(c)
                dve.wait_ge(landed[s], turn * 16 * G2)
                dve.wait_ge(k.opened, 1)
                ln_centre(dve, ch1, ln1, gb[s][:, :, :, :].rearrange("p t g f -> p (t g) f"), xc[:, :, :])

            def scale(c, s):
                wait_for(dve, turned, (c - 1) * GROUPS)
                ln_scale(dve, ch1, ln1, xc[:, :, :], h[s][:, :, :], c, 0.0).then_inc(h_made, 1)
                dve.wait_ge(h_made, c + 1)

            def contract(c, g, ring):
                m = c * GROUPS + g
                for j in range(2):
                    dve.wait_ge(i_made, m * 2 + j + 1)
                    factor = o.val["basis"][:, bass.ds(c * CH + (2 * g + j), 1), :].rearrange("p o (b f) -> p (o b) f", f=1)
                    dve.tensor_tensor(prod[:, j, :, :], ps_i[j][:, :].rearrange("p (b f) -> p b f", b=8),
                                      factor.to_broadcast([P, 8, D]), ALU.mult).then_inc(i_read, 1)
                    dve.wait_ge(i_read, m * 2 + j + 1)
                    if j == 0:
                        wait_for(dve, e_made, m - 1)
                    made = dve.tensor_reduce(i1[:, ring, j, :], prod[:, j, :, :].rearrange("p b f -> p f b"), AX.X, ALU.add)
                made.then_inc(i1_made, 1)

            def take(m, g, s, ring):
                dve.wait_ge(o_made, m + 1)
                dve.tensor_tensor(buf[s][:, :, 2 * g:2 * g + 2].rearrange("p f t -> p t f"),
                                  ps_o[ring][:, 0:P].rearrange("p (t f) -> p t f", t=2),
                                  w.last_b[:, :].rearrange("p (t f) -> p t f", t=2), ALU.add).then_inc(o_read, 1)

            def scan_chunk(c, s):
                ch2.turn(c)
                dve.wait_ge(o_read, (c + 1) * GROUPS)
                scan.chunk(dve, ch2, buf[s][:, :, :], c, run_made)

            def chunk(c, s, turn):
                before = not isinstance(c, int) or c > 0
                for g in range(GROUPS):
                    contract(c, g, (s * GROUPS + g) % 2)
                    if g < 2:
                        if before:
                            take(c * GROUPS + (g - 2), GROUPS + g - 2, 1 - s, (s * GROUPS + g) % 2)
                    else:
                        if g == 2:
                            wait_for(dve, copied, c - 1)
                        take(c * GROUPS + (g - 2), g - 2, s, (s * GROUPS + g) % 2)
                    if g == 1 and before:
                        scan_chunk(c - 1, 1 - s)
                    if turn is not None:
                        if g == 1:
                            centre(c + 1, 1 - s, turn)
                        if g == 2:
                            ln_var(dve, ch1, ln1, c + 1)
                        if g == 3:
                            scale(c + 1, 1 - s)

            centre(0, 0, 1)
            ln_var(dve, ch1, ln1, 0)
            scale(0, 0)
            for c in range(2):
                chunk(c, c, c + 1)
            with dve.Fori(1, NIT - 1) as i:
                for s in range(2):
                    chunk(2 * i + s, s, i + 1 + s)
            chunk(NCH - 2, 0, NIT)
            chunk(NCH - 1, 1, None)
            for g in range(2):
                take(END + g - 2, GROUPS + g - 2, 1, g % 2)
            scan_chunk(NCH - 1, 1)


def send_rows(k, o, scan, run, table, bound, rows, add=None):
    nc = k.nc
    k.phase("send")
    with ExitStack() as st:
        k.opened = k.sem("opened", st)
        stages = [k.sb(f"stage{s}", [P, CH, D], F32, st) for s in range(2)]
        idx = [k.sb(f"idx{s}", [P, CH], I32, st) for s in range(2)]
        part = k.sb("part", [P, CH, D], F32, st)
        if scan.largest:
            size = k.sb("size", [P, CH, D], F32, st)
            finite = k.sb("finite", [P, CH, D], I32, st)
        ps = k.pb("ps", [P, 512], F32, st)
        staged, chain0, chain, rows_made = (k.sem(n, st) for n in ("staged", "chain0", "chain", "rows_made"))
        sent = [k.sem(f"sent{s}", st) for s in range(2)]
        block = st.enter_context(nc.Block())

        @block.gpsimd
        def _(pool):
            pool.engine_nop().then_inc(k.opened, 1)
            scatter_rows(pool, k, rows, table, bound, stages, idx, staged, sent, rows_made)

        @block.tensor
        def _(pe):
            scan.carries_tensor(pe, ps)

        @block.vector
        def _(dve):
            ch = Chain(dve, chain0)
            ch.link(scan.carries_vector(dve, ps))
            ch = Chain(dve, chain, 2 * (1 + (add is not None) + 3 * scan.largest))
            def turn(i):
                ch.turn(i)
                for s in range(2):
                    c = 2 * i + s
                    wait_for(dve, sent[s], i * 16 * CH)
                    carry = spread(across(scan.carry, D), P, CH, D)
                    if scan.largest:
                        ch.link(dve.tensor_tensor(part[:, :, :], spread(col_of(scan.far, c), P, CH, D), carry, ALU.add))
                        join = ALU.max
                    else:
                        ch.link(dve.tensor_tensor(part[:, :, :], spread(col_of(o.cont, c), P, CH, D), carry, ALU.mult))
                        join = ALU.add
                    if add is not None:
                        ch.link(dve.tensor_tensor(part[:, :, :], part[:, :, :], add[:, chunk_cols(c), :], ALU.add))
                    if not scan.largest:
                        dve.tensor_tensor(stages[s][:, :, :], part[:, :, :], run[:, chunk_cols(c), :],
                                          join).then_inc(rows_made, 1)
                    else:
                        ch.link(dve.tensor_tensor(part[:, :, :], part[:, :, :], run[:, chunk_cols(c), :], join))
                        ch.link(dve.scalar_tensor_tensor(out=size[:, :, :], in0=part[:, :, :], scalar=-1.0,
                                                         in1=part[:, :, :], op0=ALU.mult, op1=ALU.max))
                        ch.link(dve.tensor_scalar(finite[:, :, :], size[:, :, :], FMAX, -1.0, ALU.is_le, ALU.mult))
                        dve.tensor_tensor(stages[s][:, :, :].bitcast(I32), finite[:, :, :], part[:, :, :].bitcast(I32),
                                          ALU.bitwise_and).then_inc(rows_made, 1)
                    dve.wait_ge(rows_made, c + 1)

            turn(0)
            with dve.Fori(1, NIT) as i:
                turn(i)


def copy_rows(k, st, block, x, x1):
    k.phase("copy")
    copied = k.sem("copied", st)

    @block.sync
    def _(sp):
        sp.dma_start(x1.rearrange("(a b) f -> a (b f)", a=16),
                     x.rearrange("(a b) f -> a (b f)", a=16)).then_inc(copied, 16)
        sp.wait_ge(copied, 16)


def own_rows(k, st, block, place_of):
    k.phase("own")
    Q = 125
    own = k.sb("own", [Q, N // Q], I32, st)
    copied, made = k.sem("copied", st), k.sem("made", st)

    @block.gpsimd
    def _(pool):
        pool.iota(own[:, :], [[1, N // Q]], base=0, channel_multiplier=N // Q).then_inc(made, 1)

    @block.sync
    def _(sp):
        sp.wait_ge(made, 1)
        sp.dma_start(place_of.rearrange("(p j) o -> p (j o)", p=Q), own[:, :]).then_inc(copied, 16)
        sp.wait_ge(copied, 16)


J = 25
PD = 125
NBLK = N // (PD * J)
assert NBLK * PD * J == N and NBLK % 2 == 0


def node_block(table, c, j=J):
    return table[bass.ds(c * (PD * j), PD * j), :].rearrange("(p j) f -> p (j f)", j=j)


def flat(x):
    return x.rearrange("p j f -> p (j f)")


def move_blocks(sp, loads, stores, loaded, read, made, stored, cleared):
    def load(c, s):
        for table, tiles in loads:
            sp.dma_start(flat(tiles[s][0:PD, 0:J, :]), node_block(table, c)).then_inc(loaded[s], 16)

    def store(c, so_far, s):
        sp.wait_ge(made, so_far)
        for table, tiles in stores:
            sp.dma_start(node_block(table, c), flat(tiles[s][0:PD, 0:J, :])).then_inc(stored[s], 16)

    sp.wait_ge(cleared, 2 * len(loads))
    for s in range(2):
        load(s, s)
    with sp.Fori(0, NBLK // 2 - 1) as i:
        for s in range(2):
            for sem, n in read:
                sp.wait_ge(sem, (2 * i + (s + 1)) * n)
            load(2 * i + s + 2, s)
            store(2 * i + s, 2 * i + (s + 1), s)
    for s in range(2):
        store(NBLK - 2 + s, NBLK - 1 + s, s)
    for s in range(2):
        sp.wait_ge(stored[s], NBLK // 2 * 16 * len(stores))


def clear_blocks(dve, tiles, cleared):
    for x in tiles:
        dve.memset(x[:, :, :], 0.0).then_inc(cleared, 1)


def norm_nodes(k, stack, block, x, y):
    xt = [k.sb(f"xt{s}", [P, J, D], F32, stack) for s in range(2)]
    yt = [k.sb(f"yt{s}", [P, J, D], F32, stack) for s in range(2)]
    xc = k.sb("xc", [P, J, D], F32, stack)
    ln = ln_buffers(k, stack, "ln", J)
    chain, made, cleared, x_read = (k.sem(n, stack) for n in ("chain", "made", "cleared", "x_read"))
    loaded, stored = ([k.sem(f"{n}{s}", stack) for s in range(2)] for n in ("loaded", "stored"))

    @block.sync
    def _(sp):
        move_blocks(sp, [(x, xt)], [(y, yt)], loaded, [(x_read, 1)], made, stored, cleared)

    @block.scalar
    def _(act):
        with act.Fori(0, NBLK) as c:
            ln_scalar(act, ln, xc[:, :, :], c)

    @block.vector
    def _(dve):
        clear_blocks(dve, xt, cleared)
        ch = Chain(dve, chain, 2 * (LN_LINKS - 1))
        def turn(i):
            ch.turn(i)
            for s in range(2):
                c = 2 * i + s
                dve.wait_ge(loaded[s], (i + 1) * 16)
                wait_for(dve, stored[s], i * 16)
                ln_vector(dve, ch, ln, xt[s][:, :, :], xc[:, :, :], yt[s][:, :, :], c, 0.0,
                          freed=(x_read, c + 1)).then_inc(made, 1)

        turn(0)
        with dve.Fori(1, NBLK // 2) as i:
            turn(i)


class Perceptron:

    GROUP = 4

    def __init__(self, k, st, n, blocks, pt, xt, x3t, h3t):
        self.k, self.n, self.blocks = k, n, blocks
        self.pt, self.xt, self.x3t, self.h3t = pt, xt, x3t, h3t
        self.rows = [min(self.GROUP, n - at) for at in range(0, n, self.GROUP)]
        self.groups = len(self.rows)
        assert n % 2 == 0 and blocks % 2 == 0
        self.w0 = k.sb("w0", [P, 2, P], F32, st)
        self.b0 = k.sb("b0", [P, 2], F32, st)
        self.w1 = k.sb("w1", [P, 2, D], F32, st)
        self.b1 = k.sb("b1", [P, 1, D], F32, st)
        self.turned_p = k.sb("turned_p", [P, 2, 2 * P], F32, st)
        self.hidden = k.sb("hidden", [P, 2, 2, 2, 2 * P], F32, st)
        self.ln = ln_buffers(k, st, "mln", n)
        self.ps_t = [k.pb(f"ps_t{n}", [P, 512], F32, st) for n in range(2)]
        self.ps_u = [k.pb(f"ps_u{n}", [P, 1024], F32, st) for n in range(2)]
        self.ps_o = k.pb("ps_o", [P, 512], F32, st)
        (self.made, self.turned, self.copied, self.x_biased, self.x3_made, self.w_landed, self.u_made, self.o_made) = (
            k.sem(n, st) for n in ("mlp_made", "mlp_turned", "mlp_copied", "x_biased", "x3_made", "mlp_w_landed",
                                   "u_made", "o_made"))
        self.hidden_made = [k.sem(f"hidden_made{h}", st) for h in range(2)]
        self.chain = k.sem("mlp_chain", st)

    def load_weights(self, sp, a):
        loads = [(self.w0[q * D:(q + 1) * D, :, :].rearrange("p h n -> p (h n)"), a["L2_gnn_W0"]) for q in range(2)]
        loads += [(self.b0[:, h:h + 1], col(a["L2_gnn_b0"])[h * P:(h + 1) * P, :]) for h in range(2)]
        loads += [(self.w1[:, :, :], a["L2_gnn_W1"].rearrange("(h p) f -> p h f", h=2)),
                  (self.b1[:, 0, :], row(a["L2_gnn_b1"]).to_broadcast([P, D]))]
        self.weights = 16 * len(loads)
        for to, src in loads:
            sp.dma_start(to, src).then_inc(self.w_landed, 16)
        sp.wait_ge(self.w_landed, self.weights)

    WEIGHTS = 16 * 6


    def turn_rows(self, pe, n, g, s):
        ring = (s * self.groups + g) % 2
        wait_for(pe, self.copied, n + (g - 1))
        for q in range(self.rows[g] // 2):
            at = g * self.GROUP + 2 * q
            last = pe.transpose(self.ps_t[ring][:, q * P:(q + 1) * P],
                                self.pt[s][:, at:at + 2, :].rearrange("p j f -> p (j f)"), self.k.ident[:, :])
        last.then_inc(self.turned, 1)

    def first(self, pe, count, g, ring):
        pe.wait_ge(self.copied, count + 1)
        for h in range(2):
            wait_for(pe, self.hidden_made[h], count - 1)
        w = self.rows[g] // 2 * P
        for h in range(2):
            for e in range(2):
                rows, at = slice(e * D, (e + 1) * D), e * 512 + h * 2 * P
                last = pe.matmul(self.ps_u[ring][:, at:at + w], self.w0[rows, h, :], self.turned_p[rows, ring, 0:w],
                                 start=True, stop=True)
        last.then_inc(self.u_made, 1)

    def second(self, pe, count, g, ring):
        for h in range(2):
            pe.wait_ge(self.hidden_made[h], count + 1)
        wait_for(pe, self.x3_made, count)
        for q in range(self.rows[g]):
            for h in range(2):
                last = pe.matmul(self.ps_o[:, q * D:(q + 1) * D],
                                 self.hidden[:, ring, h, q % 2, q // 2 * P:(q // 2 + 1) * P], self.w1[:, h, :],
                                 start=h == 0, stop=h == 1)
        last.then_inc(self.o_made, 1)

    def tensor_block(self, pe, c, s):
        n, G = c * self.groups, self.groups
        for g in range(G):
            self.turn_rows(pe, n, g, s)
            for stage, lag in ((self.first, 1), (self.second, 3)):
                if not isinstance(n, int) or n + g >= lag:
                    stage(pe, n + (g - lag), (g - lag) % G, (s * G + g - lag) % 2)

    def tensor_rest(self, pe):
        G = self.groups
        end = self.blocks * G
        self.first(pe, end - 1, G - 1, 1)
        for lag in (3, 2, 1):
            self.second(pe, end - lag, G - lag, lag % 2)


    def hide(self, act, count, g, ring):
        act.wait_ge(self.u_made, count + 1)
        wait_for(act, self.o_made, count - 1)
        w = self.rows[g] // 2 * P
        for h in range(2):
            act.activation(self.hidden[:, ring, h, :, 0:w],
                           self.ps_u[ring][:, :].rearrange("p (e h n) -> p e h n", e=2, h=2)[:, :, h, 0:w], ACT.Relu,
                           bias=self.b0[:, h:h + 1]).then_inc(self.hidden_made[h], 1)

    def scalar_block(self, act, c, s):
        n, G = c * self.groups, self.groups
        for g in range(G):
            ring = (s * G + g) % 2
            act.wait_ge(self.turned, n + g + 1)
            wait_for(act, self.u_made, n + (g - 1))
            w = self.rows[g] // 2 * P
            act.activation(self.turned_p[:, ring, 0:w], self.ps_t[ring][:, 0:w], ACT.Copy).then_inc(self.copied, 1)
            if not isinstance(n, int) or n + g >= 1:
                self.hide(act, n + (g - 1), (g - 1) % G, 1 - ring)
            if not isinstance(c, int) or c > 0:
                if g == 2:
                    self.square(act, c - 1, 1 - s)
                if g == 3:
                    ln_root(act, self.ln, c - 1)

    def square(self, act, c, s):
        ln_square(act, self.ln, self.centred(s), c)

    def scalar_rest(self, act):
        self.hide(act, self.blocks * self.groups - 1, self.groups - 1, 1)
        self.square(act, self.blocks - 1, 1)
        ln_root(act, self.ln, self.blocks - 1)


    def centred(self, s):
        return self.h3t[s][:, :, :]

    def bias(self, dve, c, s):
        dve.tensor_tensor(self.xt[s][:, :, :], self.xt[s][:, :, :], spread(self.b1[:, :, :], P, self.n, D),
                          ALU.add).then_inc(self.x_biased, 1)
        dve.wait_ge(self.x_biased, c + 1)

    def add(self, dve, c, g, s):
        dve.wait_ge(self.o_made, c * self.groups + (g + 1))
        these = slice(g * self.GROUP, g * self.GROUP + self.rows[g])
        dve.tensor_tensor(self.x3t[s][:, these, :], self.ps_o[:, 0:self.rows[g] * D].rearrange("p (j f) -> p j f", f=D),
                          self.xt[s][:, these, :], ALU.add).then_inc(self.x3_made, 1)

    def centre(self, dve, ch, c, s):
        ch.turn(c)
        dve.wait_ge(self.x3_made, (c + 1) * self.groups)
        dve.wait_ge(self.turned, (c + 1) * self.groups)
        ln_centre(dve, ch, self.ln, self.x3t[s][:, :, :], self.centred(s))

    def var(self, dve, ch, c):
        ln_var(dve, ch, self.ln, c)

    def scale(self, dve, ch, c, s):
        ln_scale(dve, ch, self.ln, self.centred(s), self.h3t[s][:, :, :], c, 0.0).then_inc(self.made, 1)


class Propagation:

    def __init__(self, k, st):
        k.phase("prop")
        self.other = k.sb("other", [P, T], I32, st)
        self.inv = k.sb("inv", [P, T], F32, st)
        self.root = k.sb("root", [P, T], F32, st)
        self.uproot = k.sb("uproot", [P, T], F32, st)
        self.cont_inv = k.sb("cont_inv", [P, T], F32, st)
        self.g = k.sb("g", [P, T, D], F32, st)
        self.total = k.sb("total", [P, T, D], F32, st)


def locate(k, o, pr, place_of, beside):
    nc = k.nc
    k.phase("slots")
    with ExitStack() as st:
        k.opened = k.sem("opened", st)
        rows = k.sb("rows", [P, T, 1], I32, st)
        stages = [k.sb(f"stage{s}", [P, CH, 1], I32, st) for s in range(2)]
        idx = [k.sb(f"idx{s}", [P, CH], I32, st) for s in range(2)]
        staged, counted = k.sem("staged", st), k.sem("counted", st)
        sent = [k.sem(f"sent{s}", st) for s in range(2)]
        block = st.enter_context(nc.Block())
        beside(st, block)

        @block.gpsimd
        def _(pool):
            pool.engine_nop().then_inc(k.opened, 1)
            pool.iota(rows[:, :, 0], [[1, T]], base=N, channel_multiplier=T).then_inc(counted, 1)
            pool.wait_ge(counted, 1)
            scatter_rows(pool, k, o.last_row, place_of, N - 1, stages, idx, staged, sent, rows_all=rows)

    k.phase("find")
    with ExitStack() as st:
        k.opened = k.sem("opened", st)
        stages = [k.sb(f"stage{s}", [P, CH, 1, 1], I32, st) for s in range(2)]
        idx = [k.sb(f"idx{s}", [P, 1, CH], I32, st) for s in range(2)]
        run = k.sb("run", [P, T], F32, st)
        deg = k.sb("deg", [P, T], F32, st)
        row_t = k.sb("row_t", [1, P + 1], F32, st)
        carry = k.sb("carry", [P, 1], F32, st)
        ps = [k.pb(f"ps{n}", [P, 512], F32, st) for n in range(2)]
        staged, chain, run_made, turned, scanned, back, root_made, rooted = (
            k.sem(n, st) for n in ("staged", "chain", "run_made", "turned", "scanned", "back", "root_made", "rooted"))
        landed = [k.sem(f"landed{s}", st) for s in range(2)]
        freed = [k.sem(f"freed{s}", st) for s in range(2)]
        block = st.enter_context(nc.Block())

        @block.gpsimd
        def _(pool):
            pool.engine_nop().then_inc(k.opened, 1)
            gather_rows(pool, k, place_of, N - 1, [o.other], stages, idx, staged, landed, freed, 1)

        @block.tensor
        def _(pe):
            pe.wait_ge(run_made, 1)
            pe.transpose(ps[0][0:1, 0:P], run[:, T - 1:T], k.ident[:, :]).then_inc(turned, 1)
            pe.wait_ge(scanned, 1)
            pe.transpose(ps[1][:, 0:1], row_t[:, 0:P], k.ident[0:1, 0:1]).then_inc(back, 1)

        @block.scalar
        def _(act):
            act.wait_ge(root_made, 1)
            act.activation(pr.root[:, :], deg[:, :], ACT.Sqrt).then_inc(rooted, 1)

        @block.vector
        def _(dve):
            ch = Chain(dve, chain)
            w = o.val["weight"][:, :, 0]
            ch.link(dve.memset(row_t[:, :], 0.0))
            dve.tensor_tensor_scan(out=run[:, :], data0=o.same[:, :], data1=w, initial=0.0, op0=ALU.mult,
                                   op1=ALU.add).then_inc(run_made, 1)
            dve.wait_ge(turned, 1)
            dve.tensor_tensor_scan(out=row_t[:, 1:P + 1], data0=o.whole[0:1, :], data1=ps[0][0:1, 0:P], initial=0.0,
                                   op0=ALU.mult, op1=ALU.add).then_inc(scanned, 1)
            dve.wait_ge(back, 1)
            ch.link(dve.tensor_copy(carry[:, :], ps[1][:, 0:1]))
            ch.link(dve.scalar_tensor_tensor(out=deg[:, :], in0=o.cont[:, :], scalar=carry[:, :], in1=run[:, :],
                                             op0=ALU.mult, op1=ALU.add))
            ch.link(dve.tensor_scalar(run[:, :], deg[:, :], 1.0, 1e-12, ALU.add, ALU.max))
            dve.tensor_copy(deg[:, :], run[:, :]).then_inc(root_made, 1)
            ch.link(dve.reciprocal(pr.inv[:, :], run[:, :]))
            ch.link(dve.tensor_tensor(pr.cont_inv[:, :], pr.inv[:, :], o.cont[:, :], ALU.mult))
            dve.wait_ge(rooted, 1)
            ch.link(dve.reciprocal(pr.uproot[:, :], pr.root[:, :]))
            with dve.Fori(0, NIT) as i:
                for s in range(2):
                    c = 2 * i + s
                    dve.wait_ge(landed[s], (i + 1) * 16 * CH)
                    dve.tensor_scalar(pr.other[:, chunk_cols(c)], stages[s][:, :, 0, 0], 0.0, None,
                                      ALU.add).then_inc(freed[s], 1)


PARTS = 14
JM = 20
MBLK = N // (PD * JM)
assert MBLK * PD * JM == N


def slot_rows(table, q):
    w = T // PARTS * D
    return table.rearrange("(p t) f -> p (t f)", t=T)[:, bass.ds(q * w, w)]


def slot_cols(q):
    return bass.ds(q * (T // PARTS), T // PARTS)


def start_propagation(k, o, pr, x2, x2_slots):
    nc = k.nc
    k.phase("prop_init")
    with ExitStack() as st:
        k.opened = k.sem("opened", st)
        gb = [k.sb(f"rows{s}", [P, CH, 1, D], F32, st) for s in range(2)]
        idx = [k.sb(f"idx{s}", [P, 1, CH], I32, st) for s in range(2)]
        xc = k.sb("xc", [P, CH, D], F32, st)
        h = k.sb("h", [P, CH, D], F32, st)
        ln = ln_buffers(k, st, "ln", CH)
        staged, g_made, h_made, chain = (k.sem(n, st) for n in ("staged", "g_made", "h_made", "chain"))
        landed = [k.sem(f"landed{s}", st) for s in range(2)]
        freed = [k.sem(f"freed{s}", st) for s in range(2)]
        block = st.enter_context(nc.Block())

        @block.gpsimd
        def _(pool):
            pool.engine_nop().then_inc(k.opened, 1)
            gather_rows(pool, k, x2, N - 1, [o.key], gb, idx, staged, landed, freed, 16)

        @block.sync
        def _(sp):
            with sp.Fori(0, NIT) as i:
                for s in range(2):
                    sp.wait_ge(h_made, 2 * i + (s + 1))
                    sp.dma_start(slot_rows(x2_slots, 2 * i + s), gb[s][:, :, :, :].rearrange("p t g f -> p (t g f)")
                                 ).then_inc(freed[s], 16)
            for s in range(2):
                sp.wait_ge(freed[s], NIT * 16)

        @block.scalar
        def _(act):
            with act.Fori(0, NCH) as c:
                ln_scalar(act, ln, xc[:, :, :], c)

        @block.vector
        def _(dve):
            ch = Chain(dve, chain, LN_LINKS)

            def turn(i):
                for s in range(2):
                    c = 2 * i + s
                    ch.turn(c)
                    dve.wait_ge(landed[s], (i + 1) * 16 * CH)
                    dve.wait_ge(k.opened, 1)
                    wait_for(dve, g_made, c)
                    ln_vector(dve, ch, ln, gb[s][:, :, 0, :], xc[:, :, :], h[:, :, :], c, 0.0).then_inc(h_made, 1)
                    dve.wait_ge(h_made, c + 1)
                    dve.tensor_tensor(pr.g[:, chunk_cols(c), :], h[:, :, :], spread(col_of(pr.uproot, c), P, CH, D),
                                      ALU.mult).then_inc(g_made, 1)

            turn(0)
            with dve.Fori(1, NIT) as i:
                turn(i)
            dve.wait_ge(g_made, NCH)
            dve.tensor_scalar(pr.total[:, :, :], pr.g[:, :, :], 0.1 / 0.09 - 1.0, None, ALU.mult).then_inc(g_made, 1)
            dve.wait_ge(g_made, NCH + 1)


def propagate(k, a, o, pr, table, x2, x3, h3, steps=10):
    nc = k.nc
    k.phase("prop_steps")
    slot_table = table[N:N + SLOTS, :]
    with ExitStack() as st:
        k.opened = k.sem("opened", st)
        gb = [k.sb(f"rows{s}", [P, CH, 1, D], F32, st) for s in range(2)]
        idx = [k.sb(f"idx{s}", [P, 1, CH], I32, st) for s in range(2)]
        buf = k.sb("buf", [P, D, CH], F32, st)
        part = k.sb("part", [P, T // PARTS, D], F32, st)
        ps = k.pb("ps", [P, 512], F32, st)
        scan = Scan(k, st, "sum", o, D)
        ht, xt = ([k.sb(f"{n}{s}", [P, JM, D], F32, st) for s in range(2)] for n in ("ht", "xt"))
        mlp = Perceptron(k, st, JM, MBLK, ht, xt, xt, ht)
        assert MBLK == 2 * steps and 2 * mlp.groups + 4 <= NCH
        staged, chain0, chain, carried, chain2, run_made, fixed, stored, cleared = (
            k.sem(n, st) for n in ("staged", "chain0", "chain", "carried", "chain2", "run_made", "fixed", "stored",
                                   "cleared"))
        landed, freed, loaded, moved = ([k.sem(f"{n}{s}", st) for s in range(2)]
                                        for n in ("landed", "freed", "loaded", "moved"))
        block = st.enter_context(nc.Block())

        @block.gpsimd
        def _(pool):
            pool.engine_nop().then_inc(k.opened, 1)
            limits = bound_register(pool, k, SLOTS + N - 1)
            gather_rows(pool, k, table, None, [pr.other], gb, idx, staged, landed, freed, 1, limits=limits,
                        ready=(stored, 16 * PARTS))
            with pool.Fori(1, steps) as step:
                gather_rows(pool, k, table, None, [pr.other], gb, idx, staged, landed, freed, 1,
                            turn0=step * NIT, limits=limits, ready=(stored, (step + 1) * 16 * PARTS))

        @block.sync
        def _(sp):
            def load(c, s):
                for source, tiles in ((table, ht), (x2, xt)):
                    sp.dma_start(flat(tiles[s][0:PD, :, :]), node_block(source, c, JM)).then_inc(loaded[s], 16)

            def store(c, s, so_far, times):
                sp.wait_ge(mlp.made, so_far)
                for to, tiles in ((h3, ht), (x3, xt)):
                    sp.dma_start(node_block(to, c, JM), flat(tiles[s][0:PD, :, :])).then_inc(moved[s], 16)
                sp.wait_ge(moved[s], times * 32)

            def store_slots(step):
                with sp.Fori(0, PARTS) as q:
                    sp.wait_ge(fixed, step * PARTS + q + 1)
                    sp.dma_start(slot_rows(slot_table, q), flat(pr.g[:, slot_cols(q), :])).then_inc(stored, 16)

            with sp.Fori(0, PARTS) as q:
                sp.dma_start(slot_rows(slot_table, q), flat(pr.g[:, slot_cols(q), :])).then_inc(stored, 16)
            sp.wait_ge(cleared, 4)
            for s in range(2):
                load(s, s)
            mlp.load_weights(sp, a)
            store(0, 0, 1, 1)
            load(2, 0)
            store_slots(0)
            with sp.Fori(1, steps - 1) as step:
                store(2 * step - 1, 1, 2 * step, step)
                load(2 * step + 1, 1)
                store(2 * step, 0, 2 * step + 1, step + 1)
                load(2 * step + 2, 0)
                store_slots(step)
            store(MBLK - 3, 1, MBLK - 2, steps - 1)
            load(MBLK - 1, 1)
            store(MBLK - 2, 0, MBLK - 1, steps)
            store(MBLK - 1, 1, MBLK, steps)
            sp.wait_ge(stored, steps * 16 * PARTS)

        @block.tensor
        def _(pe):
            def turn(step):
                for s in range(2):
                    pe.wait_ge(loaded[s], (step + 1) * 32)
                    mlp.tensor_block(pe, 2 * step + s, s)
                pe.wait_ge(run_made, (step + 1) * NCH)
                scan.carries_tensor(pe, ps, step)

            pe.wait_ge(mlp.w_landed, mlp.WEIGHTS)
            turn(0)
            with pe.Fori(1, steps) as step:
                turn(step)
            mlp.tensor_rest(pe)

        @block.scalar
        def _(act):
            act.wait_ge(mlp.w_landed, mlp.WEIGHTS)
            for s in range(2):
                mlp.scalar_block(act, s, s)
            with act.Fori(1, steps) as step:
                for s in range(2):
                    mlp.scalar_block(act, 2 * step + s, s)
            mlp.scalar_rest(act)

        @block.vector
        def _(dve):
            clear_blocks(dve, ht + xt, cleared)
            scan.prepare(dve, Chain(dve, chain0))
            dve.wait_ge(mlp.w_landed, mlp.WEIGHTS)
            ch = Chain(dve, chain, 3 + Scan.LINKS)
            ch2 = Chain(dve, chain2, 1)
            ch3 = Chain(dve, mlp.chain, LN_LINKS)
            G, LAG = mlp.groups, 4

            def nodes(c, step):
                before = not isinstance(step, int) or step > 0
                m = c - LAG
                if m < 0:
                    if before:
                        mlp.add(dve, 2 * step - 1, m + G, 1)
                elif m < 2 * G - LAG:
                    s, g = m // G, m % G
                    if g == 0:
                        dve.wait_ge(loaded[s], (step + 1) * 32)
                        mlp.bias(dve, 2 * step + s, s)
                    mlp.add(dve, 2 * step + s, g, s)
                for end, there, block_c, s in ((LAG - 1, before, 2 * step - 1, 1), (LAG + G - 1, True, 2 * step, 0)):
                    if there and c == end:
                        mlp.centre(dve, ch3, block_c, s)
                    if there and c == end + 1:
                        mlp.var(dve, ch3, block_c)
                    if there and c == end + 2:
                        mlp.scale(dve, ch3, block_c, s)

            def turn(step):
                for c in range(NCH):
                    s, i = c % 2, c // 2
                    at = step * NCH + c
                    ch.turn(at)
                    g = pr.g[:, chunk_cols(c), :]
                    dve.wait_ge(stored, (step + 1) * 16 * PARTS)
                    ch.link(dve.tensor_tensor(pr.total[:, chunk_cols(c), :], pr.total[:, chunk_cols(c), :], g, ALU.add))
                    dve.wait_ge(landed[s], (step * NIT + (i + 1)) * 16 * CH)
                    weight = o.val["weight"][:, chunk_cols(c), :].rearrange("p t o -> p o t")
                    dve.tensor_tensor(buf[:, :, :], gb[s][:, :, 0, :].rearrange("p t f -> p f t"),
                                      weight.to_broadcast([P, D, CH]), ALU.mult).then_inc(freed[s], 1)
                    dve.wait_ge(freed[s], step * NIT + (i + 1))
                    scan.chunk(dve, ch, buf[:, :, :], c, run_made, turn=at)
                    ch.link(dve.tensor_tensor(g, g, buf[:, :, :].rearrange("p f t -> p t f"), ALU.add))
                    ch.link(dve.tensor_tensor(g, g, spread(col_of(pr.inv, c), P, CH, D), ALU.mult))
                    nodes(c, step)
                scan.carries_vector(dve, ps, step).then_inc(carried, 1)
                with dve.Fori(0, PARTS) as q:
                    ch2.turn(step * PARTS + q)
                    g = pr.g[:, slot_cols(q), :]
                    cont = pr.cont_inv[:, slot_cols(q)].rearrange("p (t o) -> p t o", o=1)
                    dve.wait_ge(carried, step + 1)
                    ch2.link(dve.tensor_tensor(part[:, :, :], spread(cont, P, T // PARTS, D),
                                               spread(across(scan.carry, D), P, T // PARTS, D), ALU.mult))
                    dve.tensor_tensor(g, g, part[:, :, :], ALU.add).then_inc(fixed, 1)
                    dve.wait_ge(fixed, step * PARTS + q + 1)

            turn(0)
            with dve.Fori(1, steps) as step:
                turn(step)
            for g in range(G - LAG, G):
                mlp.add(dve, MBLK - 1, g, 1)
            mlp.centre(dve, ch3, MBLK - 1, 1)
            mlp.var(dve, ch3, MBLK - 1)
            mlp.scale(dve, ch3, MBLK - 1, 1)


def slot_pass(k, a, o, pr, x2_slots, x3, h3, aggs):
    nc = k.nc
    k.phase("slot_pass")
    with ExitStack() as st:
        k.opened = k.sem("opened", st)
        pt, xt, x3t, h3t = ([k.sb(f"{n}{s}", [P, CH, D], F32, st) for s in range(2)] for n in ("pt", "xt", "x3t", "h3t"))
        idx = [k.sb(f"idx{s}", [P, CH], I32, st) for s in range(2)]
        share = k.sb("share", [P, T], F32, st)
        mlp = Perceptron(k, st, CH, NCH, pt, xt, x3t, h3t)
        G = mlp.groups
        zeros = k.sb("zeros", [P, 1000], F32, st)
        staged, shared, summed, p_made, zeroed, cleared = (
            k.sem(n, st) for n in ("staged", "shared", "summed", "p_made", "zeroed", "cleared"))
        loaded, sent = ([k.sem(f"{n}{s}", st) for s in range(2)] for n in ("loaded", "sent"))
        block = st.enter_context(nc.Block())

        @block.gpsimd
        def _(pool):
            pool.engine_nop().then_inc(k.opened, 1)
            limit, set_limit = bound_register(pool, k, N - 1)

            def turn(i):
                for s in range(2):
                    wait_for(pool, sent[s], i * 32 * CH)
                    pool.wait_ge(k.opened, 1)
                    pool.tensor_copy(idx[s][:, :], o.last_row[:, chunk_cols(2 * i + s)]).then_inc(staged, 1)
                    pool.wait_ge(staged, 2 * i + (s + 1))
                    pool.wait_ge(mlp.made, 2 * i + (s + 1))
                    set_limit()
                    for t in range(CH):
                        for table, tile in ((x3, mlp.x3t[s]), (h3, mlp.h3t[s])):
                            pool.indirect_dma_start(
                                table, bass.IndirectOffsetOnAxis(ap=idx[s][:, t:t + 1], axis=0),
                                tile[:, t, :], None, bounds_check=limit, oob_is_err=False).then_inc(sent[s], 16)

            turn(0)
            with pool.Fori(1, NIT) as i:
                turn(i)
            for s in range(2):
                pool.wait_ge(sent[s], NIT * 32 * CH)

        @block.sync
        def _(sp):
            mlp.load_weights(sp, a)
            sp.wait_ge(zeroed, 1)
            for s in range(2):
                sp.dma_start(flat(xt[s][:, :, :]), slot_rows(x2_slots, s)).then_inc(loaded[s], 16)
            for table in aggs:
                sp.dma_start(table.rearrange("n f -> (n f)").rearrange("(p r w) -> p r w", p=P, w=1000),
                             zeros[:, :].rearrange("p (o w) -> p o w", o=1).to_broadcast([P, N * D // P // 1000, 1000])
                             ).then_inc(cleared, 16)
            with sp.Fori(0, NIT - 1) as i:
                for s in range(2):
                    sp.wait_ge(mlp.x3_made, (2 * i + (s + 1)) * G)
                    sp.dma_start(flat(xt[s][:, :, :]), slot_rows(x2_slots, 2 * i + (s + 2))).then_inc(loaded[s], 16)
            for s in range(2):
                sp.wait_ge(loaded[s], NIT * 16)
            sp.wait_ge(cleared, 16 * len(aggs))

        @block.tensor
        def _(pe):
            def turn(i):
                for s in range(2):
                    pe.wait_ge(p_made, 2 * i + (s + 1))
                    mlp.tensor_block(pe, 2 * i + s, s)

            pe.wait_ge(mlp.w_landed, mlp.WEIGHTS)
            turn(0)
            with pe.Fori(1, NIT) as i:
                turn(i)
            mlp.tensor_rest(pe)

        @block.scalar
        def _(act):
            act.wait_ge(mlp.w_landed, mlp.WEIGHTS)
            for s in range(2):
                mlp.scalar_block(act, s, s)
            with act.Fori(1, NIT) as i:
                for s in range(2):
                    mlp.scalar_block(act, 2 * i + s, s)
            mlp.scalar_rest(act)

        @block.vector
        def _(dve):
            dve.memset(zeros[:, :], 0.0).then_inc(zeroed, 1)
            dve.wait_ge(mlp.w_landed, mlp.WEIGHTS)
            Chain(dve, shared).link(dve.tensor_scalar(share[:, :], pr.root[:, :], 0.09, None, ALU.mult))
            ch = Chain(dve, mlp.chain, LN_LINKS)

            def build(c, s):
                wait_for(dve, mlp.turned, (c - 1) * G)
                dve.tensor_tensor(pt[s][:, :, :], pr.total[:, chunk_cols(c), :], pr.g[:, chunk_cols(c), :],
                                  ALU.add).then_inc(summed, 1)
                dve.wait_ge(summed, c + 1)
                dve.tensor_tensor(pt[s][:, :, :], pt[s][:, :, :], spread(col_of(share, c), P, CH, D),
                                  ALU.mult).then_inc(p_made, 1)

            def chunk(c, i, s, more):
                if more:
                    build(c + 1, 1 - s)
                dve.wait_ge(loaded[s], (i + 1) * 16)
                mlp.bias(dve, c, s)
                wait_for(dve, sent[s], i * 32 * CH)
                for g in range(G):
                    mlp.add(dve, c, g, s)
                mlp.centre(dve, ch, c, s)
                mlp.var(dve, ch, c)
                mlp.scale(dve, ch, c, s)

            build(0, 0)
            for s in range(2):
                chunk(s, 0, s, True)
            with dve.Fori(1, NIT - 1) as i:
                for s in range(2):
                    chunk(2 * i + s, i, s, True)
            chunk(NCH - 2, NIT - 1, 0, True)
            chunk(NCH - 1, NIT - 1, 1, False)


def root_pass(k, h, root, bias, adds, y, relu):
    nc = k.nc
    k.phase("root")
    PAIRS = (J + 1) // 2
    GROUP = 4
    groups = [range(q, min(q + GROUP, PAIRS)) for q in range(0, PAIRS, GROUP)]
    NR = len(groups)
    assert NR % 2 == 0
    with ExitStack() as st:
        ht, yt = ([k.sb(f"{n}{s}", [P, J + 1, D], F32, st) for s in range(2)] for n in ("ht", "yt"))
        at = [[k.sb(f"add{q}_{s}", [P, J + 1, D], F32, st) for s in range(2)] for q in range(len(adds))]
        w = k.sb("w", [P, P], F32, st)
        b = k.sb("b", [P, 1, D], F32, st)
        turned_h = k.sb("turned_h", [P, 2, GROUP, P], F32, st)
        ps_t = [k.pb(f"ps_t{n}", [P, 512], F32, st) for n in range(2)]
        ps_y = [k.pb(f"ps_y{n}", [P, 512], F32, st) for n in range(2)]
        chain, made, cleared, w_clear, w_landed, turned, copied, y_made, y_read = (
            k.sem(n, st) for n in ("chain", "made", "cleared", "w_clear", "w_landed", "turned", "copied", "y_made",
                                   "y_read"))
        loaded, stored = ([k.sem(f"{n}{s}", st) for s in range(2)] for n in ("loaded", "stored"))
        block = st.enter_context(nc.Block())

        @block.sync
        def _(sp):
            sp.wait_ge(w_clear, 1)
            for q in range(2):
                sp.dma_start(w[q * D:(q + 1) * D, q * D:(q + 1) * D], root).then_inc(w_landed, 16)
            sp.dma_start(b[:, 0, :], row(bias).to_broadcast([P, D])).then_inc(w_landed, 16)
            sp.wait_ge(w_landed, 48)
            move_blocks(sp, [(h, ht), *zip(adds, at)], [(y, yt)], loaded, [(turned, NR), (y_read, NR)], made, stored,
                        cleared)

        @block.tensor
        def _(pe):
            def turn_rows(n, g, s):
                wait_for(pe, copied, n + (g - 1))
                for q, pair in enumerate(groups[g]):
                    last = pe.transpose(ps_t[g % 2][:, q * P:(q + 1) * P],
                                        ht[s][:, 2 * pair:2 * pair + 2, :].rearrange("p j f -> p (j f)"), k.ident[:, :])
                last.then_inc(turned, 1)

            def multiply(count, g):
                pe.wait_ge(copied, count + 1)
                wait_for(pe, y_read, count - 1)
                for q in range(len(groups[g])):
                    last = pe.matmul(ps_y[g % 2][:, q * P:(q + 1) * P], turned_h[:, g % 2, q, :], w[:, :],
                                     start=True, stop=True)
                last.then_inc(y_made, 1)

            def turn(i):
                for s in range(2):
                    n = (2 * i + s) * NR
                    pe.wait_ge(loaded[s], (i + 1) * 16 * (1 + len(adds)))
                    for g in range(NR):
                        turn_rows(n, g, s)
                        if not isinstance(i, int) or n + g > 0:
                            multiply(n + (g - 1), (g - 1) % NR)

            pe.wait_ge(w_landed, 48)
            turn(0)
            with pe.Fori(1, NBLK // 2) as i:
                turn(i)
            multiply(NBLK * NR - 1, NR - 1)

        @block.scalar
        def _(act):
            def copy(c):
                for g in range(NR):
                    act.wait_ge(turned, c * NR + g + 1)
                    wait_for(act, y_made, c * NR + (g - 1))
                    wide = len(groups[g]) * P
                    act.activation(turned_h[:, g % 2, 0:len(groups[g]), :].rearrange("p q n -> p (q n)"),
                                   ps_t[g % 2][:, 0:wide], ACT.Copy).then_inc(copied, 1)

            copy(0)
            with act.Fori(1, NBLK) as c:
                copy(c)

        @block.vector
        def _(dve):
            dve.memset(w[:, :], 0.0).then_inc(w_clear, 1)
            clear_blocks(dve, [x for xs in [ht, *at] for x in xs], cleared)
            dve.wait_ge(w_landed, 48)
            ch = Chain(dve, chain, 2 * len(adds))
            def turn(i):
                ch.turn(i)
                for s in range(2):
                    c = 2 * i + s
                    n = c * NR
                    dve.wait_ge(loaded[s], (i + 1) * 16 * (1 + len(adds)))
                    base = at[0][s]
                    ch.link(dve.tensor_tensor(base[:, :, :], base[:, :, :], spread(b[:, :, :], P, J + 1, D), ALU.add))
                    for more in at[1:]:
                        ch.link(dve.tensor_tensor(base[:, :, :], base[:, :, :], more[s][:, :, :], ALU.add))
                    wait_for(dve, stored[s], i * 16)
                    for g in range(NR):
                        dve.wait_ge(y_made, n + g + 1)
                        nodes = slice(2 * groups[g][0], 2 * groups[g][-1] + 2)
                        wide = len(groups[g]) * P
                        dve.tensor_tensor(yt[s][:, nodes, :], ps_y[g % 2][:, 0:wide].rearrange("p (j f) -> p j f", f=D),
                                          base[:, nodes, :], ALU.add).then_inc(y_read, 1)
                    dve.wait_ge(y_read, n + NR)
                    if relu:
                        dve.tensor_scalar(yt[s][:, :, :], yt[s][:, :, :], 0.0, None, ALU.max).then_inc(made, 1)
                    else:
                        dve.tensor_scalar(yt[s][:, 0:1, :], yt[s][:, 0:1, :], 1.0, None, ALU.mult).then_inc(made, 1)

            turn(0)
            with dve.Fori(1, NBLK // 2) as i:
                turn(i)


K5 = 5


class Spline:

    def __init__(self, k, st, o):
        nc = k.nc
        k.phase("spline")
        self.knots = k.sb("knots", [P, T, 2, K5], F32, st)
        with ExitStack() as tmp:
            v = k.sb("v", [P, 2 * T], F32, tmp)
            x = k.sb("x", [P, 2 * T], F32, tmp)
            y = k.sb("y", [P, 2 * T], F32, tmp)
            chain = k.sem("chain", tmp)
            block = tmp.enter_context(nc.Block())

            @block.vector
            def _(dve):
                ch = Chain(dve, chain)
                pseudo = o.val["pseudo"][:, :, :].rearrange("p t d -> p (t d)")
                ch.link(dve.tensor_scalar(x[:, :], pseudo, float(K5 - 1), 0.0, ALU.mult, ALU.max))
                ch.link(dve.tensor_scalar(v[:, :], x[:, :], float(K5 - 1), None, ALU.min))
                for n in range(K5):
                    ch.link(dve.tensor_scalar(x[:, :], v[:, :], float(-n), None, ALU.add))
                    ch.link(dve.scalar_tensor_tensor(out=y[:, :], in0=x[:, :], scalar=-1.0, in1=x[:, :], op0=ALU.mult,
                                                     op1=ALU.max))
                    ch.link(dve.tensor_scalar(x[:, :], y[:, :], -1.0, 1.0, ALU.mult, ALU.add))
                    ch.link(dve.tensor_scalar(self.knots[:, :, :, n].rearrange("p t d -> p (t d)"), x[:, :], 0.0, None,
                                              ALU.max))


def conv(k, o, spline, h, weight, agg):
    with ExitStack() as st:
        k.phase("conv")
        run = k.sb("run", [P, T, D], F32, st)
        scan = Scan(k, st, "max", o, D, largest=True)
        conv_rows(k, o, spline, h, weight, run, scan)
        send_rows(k, o, scan, run, agg, N - 1, o.last_row)


def conv_rows(k, o, spline, h, weight, run, scan):
    nc = k.nc
    k.phase("conv_rows")
    W = K5 * D
    with ExitStack() as st:
        k.opened = k.sem("opened", st)
        gb = [k.sb(f"rows{s}", [P, CH, 1, D], F32, st) for s in range(2)]
        idx = [k.sb(f"idx{s}", [P, 1, CH], I32, st) for s in range(2)]
        w = k.sb("w", [P, 3, W], F32, st)
        z4 = [k.sb(f"z4_{s}", [P, CH, 4, D], F32, st) for s in range(2)]
        z1 = [k.sb(f"z1_{s}", [P, CH, D], F32, st) for s in range(2)]
        zt = k.sb("zt", [P, 2, K5 * P], F32, st)
        prod = k.sb("prod", [P, 2, K5, D], F32, st)
        buf = [k.sb(f"buf{s}", [P, D, CH], F32, st) for s in range(2)]
        ps_z = k.pb("ps_z", [P, 1024], F32, st)
        ps_m = [k.pb(f"ps_m{n}", [P, 1024], F32, st) for n in range(2)]
        staged, chain0, chain, w_landed, turned, zt_made, m_made, m_read, reduced, run_made, copied = (
            k.sem(n, st) for n in ("staged", "chain0", "chain", "w_landed", "turned", "zt_made", "m_made",
                                   "m_read", "reduced", "run_made", "copied"))
        landed = [k.sem(f"landed{s}", st) for s in range(2)]
        z_made = [k.sem(f"z_made{s}", st) for s in range(2)]
        block = st.enter_context(nc.Block())

        @block.gpsimd
        def _(pool):
            pool.engine_nop().then_inc(k.opened, 1)
            gather_rows(pool, k, h, N - 1, [o.other], gb, idx, staged, landed, z_made, GROUPS)

        @block.sync
        def _(sp):
            by_knot = weight.rearrange("(k1 k0) i o -> k0 i k1 o", k0=K5)
            for c, q, k0 in ((0, 0, 0), (0, 1, 1), (1, 0, 2), (1, 1, 3), (2, 0, 4), (2, 1, 4)):
                sp.dma_start(w[q * D:(q + 1) * D, c, :].rearrange("p (k o) -> p k o", k=K5),
                             by_knot[k0]).then_inc(w_landed, 16)
            sp.wait_ge(w_landed, 96)

        @block.tensor
        def _(pe):
            def turn_z(n, g, s):
                wait_for(pe, zt_made, n + g)
                for e in range(2):
                    for q in range(2):
                        pe.transpose(ps_z[:, (2 * e + q) * P:(2 * e + q + 1) * P],
                                     z4[s][:, 2 * g + e, 2 * q:2 * q + 2, :].rearrange("p n f -> p (n f)"), k.ident[:, :])
                pe.transpose(ps_z[:, 4 * P:5 * P], z1[s][:, 2 * g:2 * g + 2, :].rearrange("p t f -> p (t f)"),
                             k.ident[:, :]).then_inc(turned, 1)

            def multiply(pair, ring):
                pe.wait_ge(zt_made, pair + 1)
                wait_for(pe, m_read, pair - 1)
                to = [ps_m[ring][:, e * 512:e * 512 + W] for e in range(2)]
                for e in range(2):
                    for q in range(2):
                        pe.matmul(to[e], zt[:, ring, (2 * e + q) * P:(2 * e + q + 1) * P], w[:, q, :],
                                  start=q == 0, stop=False)
                for e in range(2):
                    rows = slice(e * D, (e + 1) * D)
                    last = pe.matmul(to[e], zt[rows, ring, 4 * P:5 * P], w[rows, 2, :], start=False, stop=True)
                last.then_inc(m_made, 1)

            def turn(i):
                for s in range(2):
                    n = (2 * i + s) * GROUPS
                    for g in range(GROUPS):
                        pe.wait_ge(z_made[s], i * GROUPS + (g + 1))
                        turn_z(n, g, s)
                        if not isinstance(i, int) or n + g > 0:
                            multiply(n + g - 1, (s * GROUPS + g + 1) % 2)

            pe.wait_ge(w_landed, 96)
            turn(0)
            with pe.Fori(1, NIT) as i:
                turn(i)
            multiply(NCH * GROUPS - 1, 1)

        @block.scalar
        def _(act):
            def chunk(c, s, copies):
                for g in range(GROUPS):
                    act.wait_ge(turned, c * GROUPS + g + 1)
                    wait_for(act, m_made, c * GROUPS + (g - 1))
                    act.activation(zt[:, (s * GROUPS + g) % 2, :], ps_z[:, 0:K5 * P], ACT.Copy).then_inc(zt_made, 1)
                    if g == 3 and copies:
                        copy(c - 1, 1 - s)

            def copy(c, s):
                act.wait_ge(run_made, c + 1)
                act.wait_ge(k.opened, 1)
                act.activation(run[:, chunk_cols(c), :].rearrange("p t f -> p f t"), buf[s][:, :, :],
                               ACT.Copy).then_inc(copied, 1)

            chunk(0, 0, False)
            chunk(1, 1, True)
            with act.Fori(1, NIT) as i:
                for s in range(2):
                    chunk(2 * i + s, s, True)
            copy(NCH - 1, 1)

        @block.vector
        def _(dve):
            scan.prepare(dve, Chain(dve, chain0))
            ch = Chain(dve, chain, 2 * Scan.LINKS)

            def build(c, s, g, turn):
                if g == 0:
                    dve.wait_ge(landed[s], turn * 16 * CH)
                    wait_for(dve, turned, (c - 1) * GROUPS)
                    dve.wait_ge(k.opened, 1)
                pair = slice(2 * g, 2 * g + 2)
                first = spline.knots[:, bass.ds(c * CH + 2 * g, 2), 0, :]
                rows = gb[s][:, pair, :, :]
                dve.tensor_tensor(z4[s][:, pair, :, :],
                                  first[:, :, 0:4].rearrange("p t (n o) -> p t n o", o=1).to_broadcast([P, 2, 4, D]),
                                  rows.to_broadcast([P, 2, 4, D]), ALU.mult)
                dve.tensor_tensor(z1[s][:, pair, :], first[:, :, 4:5].to_broadcast([P, 2, D]), rows[:, :, 0, :],
                                  ALU.mult).then_inc(z_made[s], 1)

            def chunk(c, s, turn):
                wait_for(dve, copied, c - 1)
                for g in range(GROUPS):
                    n = c * GROUPS + g
                    dve.wait_ge(m_made, n + 1)
                    wait_for(dve, reduced, n)
                    second = spline.knots[:, bass.ds(c * CH + 2 * g, 2), 1, :]
                    dve.tensor_tensor(prod[:, :, :, :],
                                      ps_m[(s * GROUPS + g) % 2][:, :].rearrange("p (e w) -> p e w", e=2)[:, :, 0:W].rearrange(
                                          "p e (n f) -> p e n f", f=D),
                                      second.rearrange("p t (n o) -> p t n o", o=1).to_broadcast([P, 2, K5, D]),
                                      ALU.mult).then_inc(m_read, 1)
                    if turn is not None:
                        build(c + 1, 1 - s, g, turn)
                    dve.wait_ge(m_read, n + 1)
                    dve.tensor_reduce(buf[s][:, :, 2 * g:2 * g + 2].rearrange("p f t -> p t f"),
                                      prod[:, :, :, :].rearrange("p e n f -> p e f n"), AX.X,
                                      ALU.add).then_inc(reduced, 1)
                dve.wait_ge(reduced, (c + 1) * GROUPS)
                scan.chunk(dve, ch, buf[s][:, :, :], c, run_made)

            def turn(i):
                ch.turn(i)
                for s in range(2):
                    chunk(2 * i + s, s, i + 1 + s)

            for g in range(GROUPS):
                build(0, 0, g, 1)
            turn(0)
            with dve.Fori(1, NIT - 1) as i:
                turn(i)
            ch.turn(NIT - 1)
            chunk(NCH - 2, 0, NIT)
            chunk(NCH - 1, 1, None)


def gnn_kernel(nc, a, out):
    with ExitStack() as stack:
        k = Core(nc, stack)
        k.phase("all")
        constants(k)
        s, d = "src", "dst"
        k.rec_dram = {o: [nc.dram_tensor(f"rec_{o}{i}", (SLOTS, REC), I32, kind="Internal").ap() for i in range(2)]
                      for o in (s, d)}
        x1 = nc.dram_tensor("x1", (N, D), F32, kind="Internal").ap()
        place_of = nc.dram_tensor("place_of", (N, 1), I32, kind="Internal").ap()
        table = nc.dram_tensor("table", (N + SLOTS, D), F32, kind="Internal").ap()
        agg = [nc.dram_tensor(f"agg{n}", (N, D), F32, kind="Internal").ap() for n in range(2)]
        with ExitStack() as st:
            rec = {o: k.sb(f"rec_{o}", [P, T, REC], I32, st) for o in (s, d)}
            place = {o: k.sb(f"place_{o}", [P, T], I32, st) for o in (s, d)}
            load_records(k, a[s], a[d], [(a["edge_weight"].bitcast(I32).rearrange("(e w) -> e w", w=1), 1)], rec[s])
            load_records(k, a[d], a[s], [(a["edge_attr_2"].bitcast(I32), 2), (a["edge_attr_8"].bitcast(I32), 8)],
                         rec[d])
            sort_step(k, (rec[s], place[s], 0, None))
            sort_step(k, (rec[d], place[d], 0, None), (rec[s], place[s], k.rec_dram[s][0]))
            sort_step(k, (rec[s], place[s], 8, k.rec_dram[s][0]), (rec[d], place[d], k.rec_dram[d][0]))
            sort_step(k, (rec[d], place[d], 8, k.rec_dram[d][0]), (rec[s], place[s], k.rec_dram[s][1]),
                      beside=lambda st, block: copy_rows(k, st, block, a["x"], x1))
            sort_step(k, None, (rec[d], place[d], k.rec_dram[d][1]), beside=lambda st, block: own_rows(k, st, block, place_of))
        by_src = Order(k, "by_src", [("weight", 1)])
        build_order(k, by_src, k.rec_dram[s][1])
        layer0(k, a, by_src, x1)
        by_dst = Order(k, "by_dst", [("pseudo", 2), ("basis", 8)])
        build_order(k, by_dst, k.rec_dram[d][1])
        k.recycle()
        layer1(k, a, by_dst, x1)
        k.recycle()
        x2_slots = nc.dram_tensor("x2_slots", (SLOTS, D), F32, kind="Internal").ap()
        x3, h3, h4 = (nc.dram_tensor(n, (N, D), F32, kind="Internal").ap() for n in ("x3", "h3", "h4"))
        with ExitStack() as st:
            pr = Propagation(k, st)
            locate(k, by_src, pr, place_of, lambda st, block: norm_nodes(k, st, block, x1, table[0:N, :]))
            start_propagation(k, by_src, pr, x1, x2_slots)
            propagate(k, a, by_src, pr, table, x1, x3, h3)
            k.recycle()
            slot_pass(k, a, by_src, pr, x2_slots, x3, h3, agg)
        k.recycle()
        spline = Spline(k, stack, by_dst)
        conv(k, by_dst, spline, h3, a["L3_gnn_W1"], agg[0])
        root_pass(k, h3, a["L3_gnn_root1"], a["L3_gnn_bias1"], [agg[0]], h4, True)
        k.recycle()
        conv(k, by_dst, spline, h4, a["L3_gnn_W2"], agg[1])
        root_pass(k, h4, a["L3_gnn_root2"], a["L3_gnn_bias2"], [x3, agg[1]], out, False)


def kernel(**inputs):
    import concourse.bacc as bacc
    from concourse.bass_utils import run_bass_kernel_spmd

    nc = bacc.Bacc("TRN2", target_bir_lowering=False, num_devices=1)
    arrays, args = {}, {}
    for name, value in inputs.items():
        value = np.ascontiguousarray(value)
        arrays[f"in_{name}_dram"] = value
        args[name] = nc.dram_tensor(f"in_{name}_dram", value.shape, mybir.dt.from_np(value.dtype),
                                    kind="ExternalInput").ap()
    out = nc.dram_tensor("out_0_dram", (N, D), F32, kind="ExternalOutput").ap()
    gnn_kernel(nc, args, out)
    return run_bass_kernel_spmd(nc, [arrays], core_ids=[0]).results[0]["out_0_dram"]
```

```python
from contextlib import ExitStack, contextmanager

import numpy as np

import concourse.bass as bass
from concourse import mybir

P = 128
F32 = mybir.dt.float32
BF16 = mybir.dt.bfloat16
I32 = mybir.dt.int32
U8 = mybir.dt.uint8
RMAX = bass.bass_isa.ReduceOp.max
ALU = mybir.AluOpType
ACT = mybir.ActivationFunctionType
AX = mybir.AxisListType

N, D = 50000, 64
E = 25000
T = 196
SLOTS = P * T
CH = 14
NCH = T // CH
NIT = NCH // 2
REC = 16
NO_KEY = 65535
DIG = 256
FULL_P = E // T
TAIL = E - FULL_P * T


def wait_for(eng, sem, count):
    if not isinstance(count, int) or count > 0:
        eng.wait_ge(sem, count)


class Chain:

    def __init__(self, eng, sem, per=0):
        self.eng, self.sem, self.per, self.n, self.base = eng, sem, per, 0, 0

    def turn(self, i):
        assert self.n in (0, self.per), self.n
        self.base, self.n = i * self.per, 0

    def link(self, ins):
        ins.then_inc(self.sem, 1)
        self.n += 1
        self.eng.wait_ge(self.sem, self.base + self.n)


class Core:

    def __init__(self, nc, stack):
        self.nc, self.stack, self.phases = nc, stack, 0
        self.sems, self.sem_stack = [], stack.enter_context(ExitStack())

    def phase(self, name):
        self.phases += 1
        self.prefix = f"{name}{self.phases}_"

    def sb(self, name, shape, dt, stack=None):
        return (stack or self.stack).enter_context(self.nc.sbuf_tensor(self.prefix + name, shape, dt))

    def pb(self, name, shape, dt, stack=None):
        return (stack or self.stack).enter_context(self.nc.psum_tensor(self.prefix + name, shape, dt))

    def sem(self, name, stack=None):
        self.sems.append(self.sem_stack.enter_context(self.nc.semaphore(self.prefix + name)))
        return self.sems[-1]

    def recycle(self):
        with self.nc.Block() as block:
            @block.gpsimd
            def _(pool):
                pool.dma_reset()
                for s in self.sems:
                    pool.sem_clear(s)
        self.sem_stack.close()
        self.sems = []


def constants(k):
    nc = k.nc
    k.ident = k.sb("ident", [P, P], F32)
    k.identb = k.sb("identb", [P, P], BF16)
    k.onesb = k.sb("onesb", [P, P], BF16)
    k.ones = k.sb("ones", [P, P], F32)
    k.below = k.sb("below", [P, P], BF16)
    k.digits = k.sb("digits", [P, DIG], BF16)
    k.slot = k.sb("slot", [P, T], I32)
    with ExitStack() as st:
        digits_i = k.sb("digits_i", [P, DIG], I32, st)
        made = k.sem("const_made", st)
        block = st.enter_context(nc.Block())

        @block.gpsimd
        def _(pool):
            pool.memset(k.ident[:, :], 0.0).then_inc(made, 1)
            pool.memset(k.ones[:, :], 1.0).then_inc(made, 1)
            pool.memset(k.onesb[:, :], 1.0).then_inc(made, 1)
            pool.iota(digits_i[:, :], [[1, DIG]], base=0, channel_multiplier=0).then_inc(made, 1)
            pool.iota(k.slot[:, :], [[1, T]], base=0, channel_multiplier=T).then_inc(made, 1)
            pool.wait_ge(made, 5)
            pool.affine_select(out=k.ident[:, :], in_=k.ident[:, :], compare_op=ALU.not_equal, fill=1.0,
                               base=0, pattern=[[-1, P]], channel_multiplier=1).then_inc(made, 1)
            pool.affine_select(out=k.below[:, :], in_=k.onesb[:, :], compare_op=ALU.is_gt, fill=0.0,
                               base=0, pattern=[[1, P]], channel_multiplier=-1).then_inc(made, 1)
            pool.wait_ge(made, 7)
            pool.tensor_copy(k.identb[:, :], k.ident[:, :]).then_inc(made, 1)
            pool.tensor_copy(k.digits[:, :], digits_i[:, :]).then_inc(made, 1)
            pool.wait_ge(made, 9)


def load_records(k, keys, others, attrs, rec):
    nc = k.nc
    k.phase("load")
    with ExitStack() as st:
        words = 2 + sum(w for _, w in attrs)
        flat = k.sb("rec_in", [P, words * T], I32, st)
        cleared, landed, filed = (k.sem(x, st) for x in ("rec_cleared", "rec_landed", "rec_filed"))
        block = st.enter_context(nc.Block())
        parts = [(keys.rearrange("(e w) -> e w", w=1), 1), (others.rearrange("(e w) -> e w", w=1), 1), *attrs]

        @block.vector
        def _(dve):
            dve.memset(flat[:, 0:T], NO_KEY).then_inc(cleared, 1)
            dve.memset(flat[:, T:words * T], 0).then_inc(cleared, 1)
            dve.memset(rec[:, :, :], 0).then_inc(cleared, 1)
            dve.wait_ge(cleared, 3)
            dve.wait_ge(landed, 32 * len(parts))
            at = w0 = 0
            for _, w in parts:
                src = flat[:, at:at + w * T].rearrange("p (t w) -> p t w", w=w)
                dve.tensor_copy(rec[:, :, w0:w0 + w], src).then_inc(filed, 1)
                at, w0 = at + w * T, w0 + w
            dve.wait_ge(filed, len(parts))

        @block.sync
        def _(sp):
            sp.wait_ge(cleared, 2)
            at = 0
            for ap, w in parts:
                sp.dma_start(flat[0:FULL_P, at:at + w * T],
                             ap[0:FULL_P * T, :].rearrange("(p t) w -> p (t w)", t=T)).then_inc(landed, 16)
                sp.dma_start(flat[FULL_P:FULL_P + 1, at:at + w * TAIL],
                             ap[FULL_P * T:E, :].rearrange("(p t) w -> p (t w)", p=1)).then_inc(landed, 16)
                at += w * T
            sp.wait_ge(landed, 32 * len(parts))


def bound_register(pool, k, bound):
    none = pool.alloc_register(k.prefix + "none")
    limit = pool.alloc_register(k.prefix + "limit")
    pool.reg_mov(none, 0)
    return limit, lambda: pool.reg_add(limit, none, bound)


def scatter_rows(pool, k, idx_all, table, bound, stages, idx_stage, staged, sent, rows_made=None, rows_all=None):
    limit, set_limit = bound_register(pool, k, bound)
    def turn(i):
        for s in range(2):
            c = 2 * i + s
            wait_for(pool, sent[s], i * 16 * CH)
            pool.wait_ge(k.opened, 1)
            n = 1
            pool.tensor_copy(idx_stage[s][:, :], idx_all[:, bass.ds(c * CH, CH)]).then_inc(staged, 1)
            if rows_all is not None:
                pool.tensor_copy(stages[s][:, :, :], rows_all[:, bass.ds(c * CH, CH), :]).then_inc(staged, 1)
                n = 2
            pool.wait_ge(staged, (i * 2 + s + 1) * n)
            if rows_made is not None:
                pool.wait_ge(rows_made, c + 1)
            set_limit()
            for t in range(CH):
                pool.indirect_dma_start(
                    table, bass.IndirectOffsetOnAxis(ap=idx_stage[s][:, t:t + 1], axis=0),
                    stages[s][:, t, :], None, bounds_check=limit, oob_is_err=False).then_inc(sent[s], 16)

    turn(0)
    with pool.Fori(1, NIT) as i:
        turn(i)
    for s in range(2):
        pool.wait_ge(sent[s], NIT * 16 * CH)
    return limit


def gather_rows(pool, k, table, bound, idxs, stages, idx_stage, staged, landed, freed, per_turn, turn0=0, limits=None, ready=()):
    limit, set_limit = bound_register(pool, k, bound) if limits is None else limits

    def turn(i):
        for s in range(2):
            c = 2 * i + s
            wait_for(pool, freed[s], (turn0 + i) * per_turn)
            for is_ready in ready:
                pool.wait_ge(*is_ready)
            pool.wait_ge(k.opened, 1)
            for g, idx in enumerate(idxs):
                pool.tensor_copy(idx_stage[s][:, g, :], idx[:, bass.ds(c * CH, CH)]).then_inc(staged, 1)
            pool.wait_ge(staged, ((turn0 + i) * 2 + s + 1) * len(idxs))
            set_limit()
            for t in range(CH):
                for g in range(len(idxs)):
                    pool.indirect_dma_start(
                        stages[s][:, t, g, :], None, table,
                        bass.IndirectOffsetOnAxis(ap=idx_stage[s][:, g, t:t + 1], axis=0),
                        bounds_check=limit, oob_is_err=False).then_inc(landed[s], 16)

    start = 0
    if isinstance(turn0, int) and turn0 == 0:
        turn(0)
        start = 1
    with pool.Fori(start, NIT) as i:
        turn(i)


def sort_step(k, rank=None, scatter=None, beside=None):
    nc = k.nc
    k.phase("sort")
    with ExitStack() as st:
        opened = k.opened = k.sem("sort_open", st)
        if scatter:
            stages = [k.sb(f"rec_stage{s}", [P, CH, REC], I32, st) for s in range(2)]
            idxs = [k.sb(f"rec_idx{s}", [P, CH], I32, st) for s in range(2)]
            staged = k.sem("rec_staged", st)
            sent = [k.sem(f"rec_sent{s}", st) for s in range(2)]
        if rank:
            rec, place, shift, source = rank
            dig_i = k.sb("dig_i", [P, T], I32, st)
            dig = k.sb("dig", [P, T], BF16, st)
            hot = k.sb("hot", [P, T + 1, DIG], BF16, st)
            cnt = k.sb("cnt", [P, DIG], BF16, st)
            tot = k.sb("tot", [P, DIG], F32, st)
            upto = k.sb("upto", [P, DIG], F32, st)
            start = k.sb("start", [P, DIG], F32, st)
            one = k.sb("one", [P, DIG], F32, st)
            prod = k.sb("prod", [P, 2, DIG], F32, st)
            rank_f = k.sb("rank_f", [P, T], F32, st)
            ps_cnt = k.pb("ps_cnt", [P, 512], F32, st)
            ps_tot = k.pb("ps_tot", [P, 512], F32, st)
            ps_x = [k.pb(f"ps_x{h}", [P, 512], F32, st) for h in range(2)]
            landed, dve_done, hot_made, counted, cnt_copied, totalled, start_made = (
                k.sem(x, st) for x in ("srt_landed", "srt_dve", "hot_made", "counted", "cnt_copied",
                                       "totalled", "start_made"))
            x_ready = [k.sem(f"x_ready{h}", st) for h in range(2)]
            x_read = [k.sem(f"x_read{h}", st) for h in range(2)]
            HOT = 28
        block = st.enter_context(nc.Block())

        @block.gpsimd
        def _(pool):
            if scatter:
                s_rec, s_rank, s_table = scatter
                pool.engine_nop().then_inc(opened, 1)
                scatter_rows(pool, k, s_rank, s_table, SLOTS - 1, stages, idxs, staged, sent, rows_all=s_rec)

        if not rank:
            if beside is not None:
                beside(st, block)
            return

        @block.sync
        def _(sp):
            if source is not None:
                sp.dma_start(rec[:, :, :].rearrange("p t w -> p (t w)"),
                             source.rearrange("(p t) w -> p (t w)", t=T)).then_inc(landed, 16)
                sp.wait_ge(landed, 16)

        if beside is not None:
            beside(st, block)

        @block.vector
        def _(dve):
            ch = Chain(dve, dve_done)
            if source is not None:
                dve.wait_ge(landed, 16)
            ch.link(dve.tensor_scalar(dig_i[:, :], rec[:, :, 0], shift, DIG - 1,
                                      ALU.logical_shift_right, ALU.bitwise_and))
            ch.link(dve.tensor_copy(dig[:, :], dig_i[:, :]))
            ch.link(dve.memset(hot[:, T, :], 0.0))
            ch.link(dve.memset(one[:, :], 1.0))
            for c in range(T // HOT):
                dve.tensor_tensor(
                    hot[:, c * HOT:(c + 1) * HOT, :],
                    dig[:, c * HOT:(c + 1) * HOT].rearrange("p (t o) -> p t o", o=1).to_broadcast([P, HOT, DIG]),
                    k.digits[:, :].rearrange("p (o d) -> p o d", o=1).to_broadcast([P, HOT, DIG]),
                    ALU.is_equal).then_inc(hot_made, 1)
            dve.wait_ge(counted, 1)
            dve.tensor_copy(cnt[:, :], ps_cnt[:, 0:DIG]).then_inc(cnt_copied, 1)
            dve.wait_ge(totalled, 1)
            ch.link(dve.tensor_copy(tot[:, :], ps_tot[:, 0:DIG]))
            ch.link(dve.tensor_tensor_scan(out=upto[:, :], data0=one[:, :], data1=tot[:, :], initial=0.0,
                                           op0=ALU.mult, op1=ALU.add))
            dve.tensor_tensor(start[:, :], upto[:, :], tot[:, :], ALU.subtract).then_inc(start_made, 1)
            with dve.Fori(0, T // 14) as i:
                for j in range(14):
                    h = j % 2
                    dve.wait_ge(x_ready[h], i * 7 + j // 2 + 1)
                    dve.scalar_tensor_tensor(
                        out=prod[:, h, :], in0=hot[:, bass.ds(i * 14 + j, 1), :].rearrange("p o d -> p (o d)"), scalar=1.0,
                        in1=ps_x[h][:, 0:DIG], op0=ALU.mult, op1=ALU.mult,
                        accum_out=rank_f[:, bass.ds(i * 14 + j, 1)]).then_inc(x_read[h], 1)
            dve.wait_ge(x_read[0], T // 2)
            dve.wait_ge(x_read[1], T // 2)
            ch.link(dve.tensor_copy(place[:, :], rank_f[:, :]))

        @block.tensor
        def _(pe):
            pe.wait_ge(hot_made, 1)
            pe.matmul(ps_cnt[:, 0:DIG], k.identb[:, :], hot[:, T, :], start=True, stop=True)
            with pe.Fori(0, T // HOT) as i:
                pe.wait_ge(hot_made, i + 1)
                for j in range(HOT):
                    pe.matmul(ps_cnt[:, 0:DIG], k.identb[:, :],
                              hot[:, bass.ds(i * HOT + j, 1), :].rearrange("p o d -> p (o d)"),
                              start=False, stop=True, skip_group_check=True)
            pe.matmul(ps_cnt[:, 0:DIG], k.identb[:, :], hot[:, T, :], start=False, stop=True,
                      skip_group_check=True).then_inc(counted, 1)
            pe.wait_ge(cnt_copied, 1)
            pe.matmul(ps_tot[:, 0:DIG], k.onesb[:, :], cnt[:, :], start=True, stop=True).then_inc(totalled, 1)
            pe.wait_ge(start_made, 1)
            for h in range(2):
                pe.matmul(ps_x[h][:, 0:DIG], k.ident[:, :], start[:, :], start=True, stop=False,
                          skip_group_check=True)
                last = pe.matmul(ps_x[h][:, 0:DIG], k.below[:, :], cnt[:, :], start=False, stop=h == 0,
                                 skip_group_check=True)
                if h:
                    last = pe.matmul(ps_x[h][:, 0:DIG], k.identb[:, :], hot[:, 0, :], start=False, stop=True,
                                     skip_group_check=True)
                last.then_inc(x_ready[h], 1)
            with pe.Fori(0, T // 14) as i:
                for j in range(14):
                    h = j % 2
                    pe.wait_ge(x_read[h], i * 7 + j // 2 + 1)
                    for q in range(2):
                        last = pe.matmul(ps_x[h][:, 0:DIG], k.identb[:, :],
                                         hot[:, bass.ds(i * 14 + (j + q), 1), :].rearrange("p o d -> p (o d)"),
                                         start=False, stop=True, skip_group_check=True)
                    last.then_inc(x_ready[h], 1)


def shift_columns(k, keyx, landed, sp):
    sp.dma_start(keyx[1:P, 0:1], keyx[0:P - 1, T:T + 1]).then_inc(landed, 16)
    sp.dma_start(keyx[0:P - 1, T + 1:T + 2], keyx[1:P, 1:2]).then_inc(landed, 16)


class Order:

    def __init__(self, k, name, attrs):
        k.phase(name)
        self.attrs = attrs
        self.key = k.sb("key", [P, T], I32)
        self.other = k.sb("other", [P, T], I32)
        self.last_row = k.sb("last_row", [P, T], I32)
        self.last_in = k.sb("last_in", [P, T], I32)
        self.last_over = k.sb("last_over", [P, 1], I32)
        self.over = k.sb("over", [P, T], F32)
        self.same = k.sb("same", [P, T], F32)
        self.cont = k.sb("cont", [P, T], F32)
        self.whole = k.sb("whole", [D + 1, P], F32)
        self.mask = k.sb("mask", [P, NCH, CH], BF16)
        self.val = {n: k.sb(n, [P, T, w], F32) for n, w in attrs}


def build_order(k, o, records):
    nc = k.nc
    k.phase("order")
    with ExitStack() as st:
        rec = k.sb("rec", [P, T, REC], I32, st)
        keyx = k.sb("keyx", [P, T + 2], F32, st)
        after = k.sb("after", [P, T], F32, st)
        tmp = k.sb("tmp", [P, T], F32, st)
        wide = k.sb("wide", [P, D + 1], F32, st)
        wide_tmp = k.sb("wide_tmp", [P, T], F32, st)
        over_key = k.sb("over_key", [P, 1], F32, st)
        ps = k.pb("ps", [P, 512], F32, st)
        landed, shifted, key_made, done, wide_made, whole_made = (
            k.sem(x, st) for x in ("landed", "shifted", "key_made", "done", "wide_made", "whole_made"))
        block = st.enter_context(nc.Block())

        @block.sync
        def _(sp):
            sp.dma_start(rec[:, :, :].rearrange("p t w -> p (t w)"),
                         records.rearrange("(p t) w -> p (t w)", t=T)).then_inc(landed, 16)
            sp.wait_ge(landed, 16)
            sp.wait_ge(key_made, 1)
            shift_columns(k, keyx, shifted, sp)
            sp.wait_ge(shifted, 32)

        @block.tensor
        def _(pe):
            pe.wait_ge(wide_made, 1)
            pe.matmul(ps[0:D + 1, 0:P], wide[:, :], k.ident[:, :], start=True, stop=True).then_inc(whole_made, 1)

        @block.vector
        def _(dve):
            ch = Chain(dve, done)
            ch.link(dve.memset(keyx[:, :], -1.0))
            dve.wait_ge(landed, 16)
            dve.tensor_copy(keyx[:, 1:T + 1], rec[:, :, 0]).then_inc(key_made, 1)
            at = 2
            for name, w in o.attrs:
                ch.link(dve.tensor_copy(o.val[name][:, :, :], rec[:, :, at:at + w].bitcast(F32)))
                at += w
            ch.link(dve.tensor_scalar(o.key[:, :], rec[:, :, 0], float(N - 1), None, ALU.min))
            ch.link(dve.tensor_copy(o.other[:, :], rec[:, :, 1]))
            dve.wait_ge(key_made, 1)
            dve.wait_ge(shifted, 32)
            key = keyx[:, 1:T + 1]
            ch.link(dve.tensor_tensor(o.same[:, :], key, keyx[:, 0:T], ALU.is_equal))
            ch.link(dve.tensor_scalar(o.cont[:, :], key, keyx[:, 1:2], o.same[:, 0:1], ALU.is_equal, ALU.mult))
            ch.link(dve.memset(o.same[:, 0:1], 0.0))
            ch.link(dve.tensor_copy(o.mask[:, :, :], o.same[:, :].rearrange("p (c t) -> p c t", t=CH)))
            ch.link(dve.memset(o.mask[:, :, 0:1], 0.0))
            ch.link(dve.tensor_tensor(after[:, :], key, keyx[:, 2:T + 2], ALU.not_equal))
            ch.link(dve.scalar_tensor_tensor(out=tmp[:, :], in0=key, scalar=float(-NO_KEY), in1=after[:, :],
                                             op0=ALU.add, op1=ALU.mult))
            ch.link(dve.tensor_scalar(o.last_row[:, :], tmp[:, :], float(NO_KEY), None, ALU.add))
            ch.link(dve.tensor_tensor(wide_tmp[:, :], tmp[:, :], o.cont[:, :], ALU.mult))
            ch.link(dve.tensor_scalar(o.over[:, :], wide_tmp[:, :], 0.0, None, ALU.is_lt))
            ch.link(dve.tensor_reduce(over_key[:, :], wide_tmp[:, :], AX.X, ALU.min))
            ch.link(dve.tensor_scalar(o.last_over[:, :], over_key[:, :], float(NO_KEY), None, ALU.add))
            ch.link(dve.tensor_tensor(tmp[:, :], tmp[:, :], wide_tmp[:, :], ALU.subtract))
            ch.link(dve.tensor_scalar(o.last_in[:, :], tmp[:, :], float(NO_KEY), None, ALU.add))
            ch.link(dve.memset(wide[:, :], 1.0))
            dve.tensor_scalar(wide[:, :], wide[:, :], o.cont[:, T - 1:T], None, ALU.mult).then_inc(wide_made, 1)
            dve.wait_ge(whole_made, 1)
            ch.link(dve.tensor_copy(o.whole[:, :], ps[0:D + 1, 0:P]))


def ln_buffers(k, st, tag, n):
    b = {x: k.sb(f"{tag}_{x}", [P, n], F32, st) for x in ("sum", "mean", "ssq", "var", "sd", "rstd")}
    b["sq"] = k.sb(f"{tag}_sq", [P, n, D], F32, st)
    b |= {x: k.sem(f"{tag}_{x}", st) for x in ("centred", "squared", "var_made", "sd_made")}
    b["n"] = n
    return b


def ln_vector(dve, ch, b, x, xc, y, call, floor, freed=None):
    ln_centre(dve, ch, b, x, xc)
    ln_var(dve, ch, b, call, freed)
    return ln_scale(dve, ch, b, xc, y, call, floor)


def ln_centre(dve, ch, b, x, xc):
    ch.link(dve.tensor_reduce(b["sum"][:, :], x, AX.X, ALU.add))
    ch.link(dve.tensor_scalar(b["mean"][:, :], b["sum"][:, :], 1.0 / D, None, ALU.mult))
    mean = b["mean"][:, :].rearrange("p (n o) -> p n o", o=1).to_broadcast([P, b["n"], D])
    dve.tensor_tensor(xc, x, mean, ALU.subtract).then_inc(b["centred"], 1)


def ln_var(dve, ch, b, call, freed=None):
    dve.wait_ge(b["squared"], call + 1)
    ssq = dve.tensor_reduce(b["ssq"][:, :], b["sq"][:, :, :], AX.X, ALU.add)
    if freed is None:
        ch.link(ssq)
    else:
        ssq.then_inc(freed[0], 1)
        dve.wait_ge(*freed)
    dve.tensor_scalar(b["var"][:, :], b["ssq"][:, :], 1.0 / D, 1e-5, ALU.mult, ALU.add).then_inc(b["var_made"], 1)


def ln_scale(dve, ch, b, xc, y, call, floor):
    dve.wait_ge(b["sd_made"], call + 1)
    ch.link(dve.reciprocal(b["rstd"][:, :], b["sd"][:, :]))
    rstd = b["rstd"][:, :].rearrange("p (n o) -> p n o", o=1).to_broadcast([P, b["n"], D])
    if floor is None:
        return dve.tensor_tensor(y, xc, rstd, ALU.mult)
    return dve.scalar_tensor_tensor(out=y, in0=xc, scalar=floor, in1=rstd, op0=ALU.max, op1=ALU.mult)


LN_LINKS = 4


def ln_scalar(act, b, xc, call, after_read=None):
    ln_square(act, b, xc, call)
    if after_read is not None:
        after_read()
    ln_root(act, b, call)


def ln_square(act, b, xc, call):
    act.wait_ge(b["centred"], call + 1)
    act.activation(b["sq"][:, :, :], xc, ACT.Square).then_inc(b["squared"], 1)


def ln_root(act, b, call):
    act.wait_ge(b["var_made"], call + 1)
    act.activation(b["sd"][:, :], b["var"][:, :], ACT.Sqrt).then_inc(b["sd_made"], 1)


def spread(ap, *shape):
    return ap.to_broadcast(list(shape))


BIG = 1.5e38
FMAX = 3.4028234663852886e38
PI = float(np.pi)


class Scan:

    def __init__(self, k, st, tag, o, f, largest=False, mask=None):
        self.own_mask = mask is None
        self.k, self.o, self.f, self.largest, self.tag = k, o, f, largest, tag
        self.mask = k.sb(f"{tag}_mask", [P, NCH, f, CH], BF16 if largest else U8, st) if mask is None else mask
        self.prev = k.sb(f"{tag}_prev", [P, P], F32, st)
        self.carry_t = k.sb(f"{tag}_carry_t", [P, P + 1], F32, st)
        self.carry = k.sb(f"{tag}_carry", [P, f], F32, st)
        if largest:
            self.wall = k.sb(f"{tag}_wall", [P, T], F32, st)
            self.far = k.sb(f"{tag}_far", [P, T], F32, st)
            self.chain = k.sb(f"{tag}_chain", [f, P], F32, st)
        self.turned, self.scanned, self.back = (k.sem(f"{tag}_{x}", st) for x in ("turned", "scanned", "back"))

    def prepare(self, dve, ch):
        o, f = self.o, self.f
        for_all = o.mask[:, :, :].rearrange("p c (o t) -> p c o t", o=1).to_broadcast([P, NCH, f, CH])
        zero = -BIG if self.largest else 0.0
        if self.own_mask:
            ch.link(dve.tensor_copy(self.mask[:, :, :, :], for_all))
        ch.link(dve.memset(self.carry_t[:, :], zero))
        ch.link(dve.memset(self.prev[:, :], zero))
        if self.largest:
            flat = self.mask[:, :, :, :].rearrange("p c f t -> p (c f t)")
            for out, x in ((flat, flat), (self.wall[:, :], o.same[:, :]), (self.far[:, :], o.cont[:, :]),
                           (self.chain[:, :], o.whole[0:f, :])):
                ch.link(dve.tensor_scalar(out, x, -1.0, BIG, ALU.add, ALU.mult))

    LINKS = 2

    def chunk(self, dve, ch, buf, c, run_made, turn=None):
        first = buf[:, :, 0]
        if self.largest:
            ch.link(dve.scalar_tensor_tensor(out=first, in0=self.prev[:, 0:self.f], scalar=self.wall[:, bass.ds(c * CH, 1)],
                                             in1=first, op0=ALU.add, op1=ALU.max))
        else:
            ch.link(dve.scalar_tensor_tensor(out=first, in0=self.prev[:, 0:self.f], scalar=self.o.same[:, bass.ds(c * CH, 1)],
                                             in1=first, op0=ALU.mult, op1=ALU.add))
        flat = buf.rearrange("p f t -> p (f t)")
        mask = self.mask[:, bass.ds(c, 1), 0:self.f, :].rearrange("p o f t -> p (o f t)")
        op0, op1 = (ALU.add, ALU.max) if self.largest else (ALU.mult, ALU.add)
        ch.link(dve.tensor_tensor_scan(out=flat, data0=mask, data1=flat, initial=0.0, op0=op0, op1=op1))
        dve.tensor_copy(self.prev[:, 0:self.f], buf[:, :, CH - 1]).then_inc(run_made, 1)
        dve.wait_ge(run_made, (c if turn is None else turn) + 1)

    def carries_vector(self, dve, ps, n=0):
        f = self.f
        dve.wait_ge(self.turned, n + 1)
        data0 = self.chain if self.largest else self.o.whole
        op0, op1 = (ALU.add, ALU.max) if self.largest else (ALU.mult, ALU.add)
        dve.tensor_tensor_scan(out=self.carry_t[0:f, 1:P + 1], data0=data0[0:f, :], data1=ps[0:f, 0:P],
                               initial=-BIG if self.largest else 0.0, op0=op0, op1=op1).then_inc(self.scanned, 1)
        dve.wait_ge(self.back, n + 1)
        return dve.tensor_copy(self.carry[:, :], ps[:, 256:256 + f])

    def carries_tensor(self, pe, ps, n=0):
        pe.transpose(ps[:, 0:P], self.prev[:, :], self.k.ident[:, :]).then_inc(self.turned, 1)
        pe.wait_ge(self.scanned, n + 1)
        pe.transpose(ps[:, 2 * P:3 * P], self.carry_t[:, 0:P], self.k.ident[:, :]).then_inc(self.back, 1)


def row(ap):
    return ap.rearrange("(o n) -> o n", o=1)


def col(ap):
    return ap.rearrange("(n o) -> n o", o=1)


def layer0(k, a, o, x1):
    nc = k.nc
    with ExitStack() as layer:
        k.phase("att")
        xs = k.sb("xs", [P, T, D], F32, layer)
        v = k.sb("v", [P, T, D], F32, layer)
        hs = k.sb("hs", [P, T, 2], F32, layer)
        att_rows(k, a, o, xs, v, hs)
        att = k.sb("att", [P, T], F32, layer)
        att_weights(k, a, o, hs, att)
        att_sums(k, o, xs, v, att, x1)


def att_rows(k, a, o, xs, v, hs):
    nc = k.nc
    k.phase("att_rows")
    G2 = 2 * CH
    GROUPS = CH // 2
    with ExitStack() as st:
        k.opened = k.sem("opened", st)
        gb = [k.sb(f"rows{s}", [P, CH, 2, D], F32, st) for s in range(2)]
        idx = [k.sb(f"idx{s}", [P, 2, CH], I32, st) for s in range(2)]
        wbd = k.sb("wbd", [P, 3 * D], F32, st)
        b2 = k.sb("b2", [P, 2 * D], F32, st)
        b1 = k.sb("b1", [P, D], F32, st)
        xc = k.sb("xc", [P, G2, D], F32, st)
        xc2 = k.sb("xc2", [P, G2, D], F32, st)
        h = [k.sb(f"h{s}", [P, G2, D], F32, st) for s in range(2)]
        q = k.sb("q", [P, G2, D], F32, st)
        ht = k.sb("ht", [P, 2, 256], F32, st)
        hsum = k.sb("hsum", [P, G2], F32, st)
        ln1, ln2 = ln_buffers(k, st, "ln1", G2), ln_buffers(k, st, "ln2", G2)
        ps_t = [k.pb(f"ps_t{g}", [P, 512], F32, st) for g in range(2)]
        ps_y = [k.pb(f"ps_y{g}", [P, 512], F32, st) for g in range(2)]
        staged, w_clear, w_landed, chain1, chain2, h_made, turned, ht_made, y_made, y_read, q_added, q_made = (
            k.sem(x, st) for x in ("staged", "w_clear", "w_landed", "chain1", "chain2", "h_made", "turned", "ht_made",
                                   "y_made", "y_read", "q_added", "q_made"))
        landed = [k.sem(f"landed{s}", st) for s in range(2)]
        freed = [k.sem(f"freed{s}", st) for s in range(2)]
        block = st.enter_context(nc.Block())

        @block.sync
        def _(sp):
            sp.wait_ge(w_clear, 1)
            for r, c, w in ((0, 0, "L0_gnn_W2"), (D, D, "L0_gnn_W2"), (D, 2 * D, "L0_gnn_W1")):
                sp.dma_start(wbd[r:r + D, c:c + D], a[w]).then_inc(w_landed, 16)
            for g in range(2):
                sp.dma_start(b2[:, g * D:(g + 1) * D], row(a["L0_gnn_b2"]).to_broadcast([P, D])).then_inc(w_landed, 16)
            sp.dma_start(b1[:, :], row(a["L0_gnn_b1"]).to_broadcast([P, D])).then_inc(w_landed, 16)
            sp.wait_ge(w_landed, 96)

        @block.gpsimd
        def _(pool):
            pool.engine_nop().then_inc(k.opened, 1)
            gather_rows(pool, k, a["x"], N - 1, [o.key, o.other], gb, idx, staged, landed, freed, 1)

        @block.scalar
        def _(act):
            def square(c, s):
                ln_square(act, ln1, xc[:, :, :], c)
                act.activation(xs[:, bass.ds(c * CH, CH), :], gb[s][:, :, 0, :], ACT.Copy).then_inc(freed[s], 1)

            def chunk(c, s, more):
                for g in range(GROUPS):
                    if g == 2 and more:
                        square(c + 1, 1 - s)
                    act.wait_ge(turned, c * GROUPS + g + 1)
                    if g >= 2:
                        act.wait_ge(y_made, c * GROUPS + g - 1)
                    act.activation(ht[:, g % 2, :], ps_t[g % 2][:, 0:256], ACT.Copy).then_inc(ht_made, 1)
                act.wait_ge(q_added, c + 1)
                act.activation(q[:, :, :], q[:, :, :], ACT.Relu).then_inc(q_made, 1)
                if more:
                    ln_root(act, ln1, c + 1)
                ln_scalar(act, ln2, xc2[:, :, :], c)

            square(0, 0)
            ln_root(act, ln1, 0)
            with act.Fori(0, NIT - 1) as i:
                for s in range(2):
                    chunk(2 * i + s, s, True)
            chunk(NCH - 2, 0, True)
            chunk(NCH - 1, 1, False)

        @block.tensor
        def _(pe):
            pe.wait_ge(w_landed, 96)
            def chunk(c, s):
                pe.wait_ge(h_made, c + 1)
                for g in range(GROUPS + 1):
                    if g < GROUPS:
                        if g >= 2:
                            pe.wait_ge(ht_made, c * GROUPS + g - 1)
                        for j in range(2):
                            last = pe.transpose(ps_t[g % 2][:, j * P:(j + 1) * P],
                                                h[s][:, 2 * (2 * g + j):2 * (2 * g + j) + 2, :].rearrange("p n f -> p (n f)"),
                                                k.ident[:, :])
                        last.then_inc(turned, 1)
                    if g >= 1:
                        m = g - 1
                        pe.wait_ge(ht_made, c * GROUPS + m + 1)
                        if m >= 2:
                            pe.wait_ge(y_read, c * GROUPS + m - 1)
                        for j in range(2):
                            last = pe.matmul(ps_y[m % 2][:, j * 3 * D:(j + 1) * 3 * D], ht[:, m % 2, j * P:(j + 1) * P],
                                             wbd[:, :], start=True, stop=True)
                        last.then_inc(y_made, 1)

            with pe.Fori(0, NIT) as i:
                for s in range(2):
                    chunk(2 * i + s, s)

        @block.vector
        def _(dve):
            dve.memset(wbd[:, :], 0.0).then_inc(w_clear, 1)
            dve.wait_ge(w_landed, 96)
            ch1 = Chain(dve, chain1, LN_LINKS)
            ch2 = Chain(dve, chain2, LN_LINKS + 2)

            def centre(c, s, turn):
                ch1.turn(c)
                dve.wait_ge(landed[s], turn * 16 * G2)
                dve.wait_ge(k.opened, 1)
                ln_centre(dve, ch1, ln1, gb[s][:, :, :, :].rearrange("p t g f -> p (t g) f"), xc[:, :, :])

            def scale(c, s):
                wait_for(dve, turned, (c - 1) * GROUPS)
                ln_scale(dve, ch1, ln1, xc[:, :, :], h[s][:, :, :], c, 0.0).then_inc(h_made, 1)
                dve.wait_ge(h_made, c + 1)

            def chunk(c, s, turn):
                if turn is not None:
                    centre(c + 1, 1 - s, turn)
                ch2.turn(c)
                for g in range(GROUPS):
                    dve.wait_ge(y_made, c * GROUPS + g + 1)
                    y = ps_y[g % 2][:, 0:6 * D].rearrange("p (t n) -> p t n", t=2)
                    q_in = dve.tensor_tensor(
                        q[:, 4 * g:4 * g + 4, :].rearrange("p (t g) f -> p t (g f)", t=2), y[:, :, 0:2 * D],
                        b2[:, :].rearrange("p (o n) -> p o n", o=1).to_broadcast([P, 2, 2 * D]), ALU.add)
                    if g == GROUPS - 1:
                        q_in.then_inc(q_added, 1)
                    dve.tensor_tensor(
                        v[:, bass.ds(c * CH + 2 * g, 2), :], y[:, :, 2 * D:3 * D],
                        b1[:, :].rearrange("p (o n) -> p o n", o=1).to_broadcast([P, 2, D]),
                        ALU.add).then_inc(y_read, 1)
                if turn is not None:
                    ln_var(dve, ch1, ln1, c + 1)
                dve.wait_ge(q_made, c + 1)
                ln_centre(dve, ch2, ln2, q[:, :, :], xc2[:, :, :])
                if turn is not None:
                    scale(c + 1, 1 - s)
                ln_var(dve, ch2, ln2, c)
                ch2.link(ln_scale(dve, ch2, ln2, xc2[:, :, :], q[:, :, :], c, None))
                ch2.link(dve.tensor_reduce(hsum[:, :], q[:, :, :], AX.X, ALU.add))
                dve.tensor_tensor(hs[:, bass.ds(c * CH, CH), :].rearrange("p t g -> p (t g)"), hsum[:, :],
                                  hsum[:, :], ALU.mult)

            def turn(i):
                for s in range(2):
                    chunk(2 * i + s, s, i + 1 + s)

            centre(0, 0, 1)
            ln_var(dve, ch1, ln1, 0)
            scale(0, 0)
            turn(0)
            with dve.Fori(1, NIT - 1) as i:
                turn(i)
            chunk(NCH - 2, 0, NIT)
            chunk(NCH - 1, 1, None)


def att_weights(k, a, o, hs, att):
    nc = k.nc
    k.phase("att_weights")
    ROUND = 1.5 * 2.0 ** 23
    with ExitStack() as st:
        valid, low, x, y, diff, z = (k.sb(n, [P, T], F32, st) for n in ("valid", "low", "x", "y", "diff", "z"))
        ends = k.sb("ends", [P, 2], F32, st)
        ends_all = k.sb("ends_all", [P, 2], F32, st)
        sc = k.sb("sc", [P, 3], F32, st)
        chain, ends_made, all_made, arg_made, att_made = (
            k.sem(n, st) for n in ("chain", "ends_made", "all_made", "arg_made", "att_made"))
        block = st.enter_context(nc.Block())

        @block.vector
        def _(dve):
            ch = Chain(dve, chain)
            source, other = hs[:, :, 0], hs[:, :, 1]
            ch.link(dve.tensor_scalar(valid[:, :], k.slot[:, :], float(E), None, ALU.is_lt))
            ch.link(dve.tensor_scalar(low[:, :], valid[:, :], -1.0, BIG, ALU.add, ALU.mult))
            ch.link(dve.tensor_tensor(x[:, :], source, valid[:, :], ALU.mult))
            ch.link(dve.tensor_tensor(y[:, :], x[:, :], low[:, :], ALU.add))
            ch.link(dve.tensor_reduce(ends[:, 0:1], y[:, :], AX.X, ALU.max))
            ch.link(dve.tensor_tensor(y[:, :], low[:, :], x[:, :], ALU.subtract))
            dve.tensor_reduce(ends[:, 1:2], y[:, :], AX.X, ALU.max).then_inc(ends_made, 1)
            ch.link(dve.tensor_tensor(diff[:, :], source, other, ALU.subtract))
            dve.wait_ge(all_made, 1)
            ch.link(dve.tensor_tensor(sc[:, 0:1], ends_all[:, 0:1], ends_all[:, 1:2], ALU.add))
            ch.link(dve.tensor_scalar(sc[:, 1:2], sc[:, 0:1], 2.0, 1e-10, ALU.mult, ALU.add))
            ch.link(dve.reciprocal(sc[:, 2:3], sc[:, 1:2]))
            ch.link(dve.tensor_scalar(z[:, :], diff[:, :], sc[:, 2:3], 0.5, ALU.mult, ALU.mult))
            ch.link(dve.tensor_scalar(x[:, :], z[:, :], ROUND, None, ALU.add))
            ch.link(dve.tensor_scalar(y[:, :], x[:, :], -ROUND, None, ALU.add))
            ch.link(dve.tensor_tensor(x[:, :], z[:, :], y[:, :], ALU.subtract))
            ch.link(dve.scalar_tensor_tensor(out=y[:, :], in0=x[:, :], scalar=-1.0, in1=x[:, :], op0=ALU.mult,
                                             op1=ALU.max))
            dve.tensor_scalar(z[:, :], y[:, :], -2.0 * PI, 0.5 * PI, ALU.mult, ALU.add).then_inc(arg_made, 1)

        @block.gpsimd
        def _(pool):
            pool.wait_ge(ends_made, 1)
            pool.partition_all_reduce(ends_all[:, :], ends[:, :], P, RMAX).then_inc(all_made, 1)

        @block.scalar
        def _(act):
            act.wait_ge(arg_made, 1)
            act.activation(att[:, :], z[:, :], ACT.Sin).then_inc(att_made, 1)
            act.wait_ge(att_made, 1)


def chunk_cols(c):
    return bass.ds(c * CH, CH)


def att_sums(k, o, xs, v, att, x1):
    nc = k.nc
    k.phase("att_sums")
    F1 = D + 1
    with ExitStack() as st:
        k.opened = k.sem("opened", st)
        buf = k.sb("buf", [P, F1, CH], F32, st)
        buf2 = k.sb("buf2", [P, D, CH], F32, st)
        stages = [k.sb(f"stage{s}", [P, CH, D], F32, st) for s in range(2)]
        idx = [k.sb(f"idx{s}", [P, CH], I32, st) for s in range(2)]
        part = k.sb("part", [P, D, CH], F32, st)
        rest = k.sb("rest", [P, D, CH], F32, st)
        rinv = k.sb("rinv", [P, 1, CH], F32, st)
        picked = k.sb("picked", [P, F1, CH], F32, st)
        pick = k.sb("pick", [P, F1], F32, st)
        over1 = k.sb("over1", [P, F1], F32, st)
        over2 = k.sb("over2", [P, D], F32, st)
        rinv_over = k.sb("rinv_over", [P, 1], F32, st)
        last = k.sb("last", [P, D], F32, st)
        ps = [k.pb(f"ps{n}", [P, 512], F32, st) for n in range(2)]
        one = Scan(k, st, "one", o, F1)
        two = Scan(k, st, "two", o, D, mask=one.mask)
        staged, chain0, chain, chain2, rows_made, run1, run2, last_made, last_sent = (
            k.sem(n, st) for n in ("staged", "chain0", "chain", "chain2", "rows_made", "run1", "run2", "last_made",
                                   "last_sent"))
        sent = [k.sem(f"sent{s}", st) for s in range(2)]
        block = st.enter_context(nc.Block())

        @block.gpsimd
        def _(pool):
            pool.engine_nop().then_inc(k.opened, 1)
            limit = scatter_rows(pool, k, o.last_in, x1, N - 1, stages, idx, staged, sent, rows_made)
            pool.wait_ge(last_made, 1)
            pool.indirect_dma_start(x1, bass.IndirectOffsetOnAxis(ap=o.last_over[:, :], axis=0), last[:, :], None,
                                    bounds_check=limit, oob_is_err=False).then_inc(last_sent, 16)
            pool.wait_ge(last_sent, 16)

        @block.tensor
        def _(pe):
            pe.wait_ge(run1, NCH)
            one.carries_tensor(pe, ps[0])
            pe.wait_ge(run2, NCH)
            two.carries_tensor(pe, ps[1])

        @block.vector
        def _(dve):
            ch = Chain(dve, chain0)
            one.prepare(dve, ch)
            two.prepare(dve, ch)
            ch.link(dve.memset(over1[:, :], 0.0))
            ch.link(dve.memset(over2[:, :], 0.0))
            ch = Chain(dve, chain, 12 + 2 * Scan.LINKS)

            def turn(i):
                for s in range(2):
                    c = 2 * i + s
                    ch.turn(c)
                    vt = v[:, chunk_cols(c), :].rearrange("p t f -> p f t")
                    at = att[:, chunk_cols(c)].rearrange("p (o t) -> p o t", o=1)
                    over = o.over[:, chunk_cols(c)].rearrange("p (o t) -> p o t", o=1)
                    ch.link(dve.tensor_tensor(buf[:, 0:D, :], vt, at.to_broadcast([P, D, CH]), ALU.mult))
                    ch.link(dve.tensor_scalar(buf[:, D:F1, :], at, 1.0, None, ALU.mult))
                    one.chunk(dve, ch, buf[:, :, :], c, run1)
                    ch.link(dve.tensor_scalar(buf2[:, :, :], vt, 1.0, None, ALU.mult))
                    two.chunk(dve, ch, buf2[:, :, :], c, run2)
                    ch.link(dve.reciprocal(rinv[:, :, :], buf[:, D:F1, :]))
                    ch.link(dve.tensor_tensor(part[:, :, :], buf[:, 0:D, :], rinv[:, :, :].to_broadcast([P, D, CH]), ALU.mult))
                    ch.link(dve.scalar_tensor_tensor(out=rest[:, :, :], in0=buf2[:, :, :], scalar=1e-10,
                                                     in1=xs[:, chunk_cols(c), :].rearrange("p t f -> p f t"),
                                                     op0=ALU.mult, op1=ALU.add))
                    wait_for(dve, sent[s], i * 16 * CH)
                    dve.tensor_tensor(stages[s][:, :, :].rearrange("p t f -> p f t"), part[:, :, :], rest[:, :, :],
                                      ALU.add).then_inc(rows_made, 1)
                    ch.link(dve.tensor_tensor(picked[:, :, :], buf[:, :, :], over.to_broadcast([P, F1, CH]), ALU.mult))
                    ch.link(dve.tensor_reduce(pick[:, :], picked[:, :, :], AX.X, ALU.add))
                    ch.link(dve.tensor_tensor(over1[:, :], over1[:, :], pick[:, :], ALU.add))
                    ch.link(dve.tensor_tensor(picked[:, 0:D, :], rest[:, :, :], over.to_broadcast([P, D, CH]), ALU.mult))
                    ch.link(dve.tensor_reduce(pick[:, 0:D], picked[:, 0:D, :], AX.X, ALU.add))
                    ch.link(dve.tensor_tensor(over2[:, :], over2[:, :], pick[:, 0:D], ALU.add))
                    dve.wait_ge(rows_made, c + 1)

            turn(0)
            with dve.Fori(1, NIT) as i:
                turn(i)
            ch = Chain(dve, chain2)
            ch.link(one.carries_vector(dve, ps[0]))
            ch.link(two.carries_vector(dve, ps[1]))
            ch.link(dve.tensor_tensor(over1[:, :], over1[:, :], one.carry[:, 0:F1], ALU.add))
            ch.link(dve.tensor_reduce(pick[:, 0:1], o.over[:, :], AX.X, ALU.add))
            ch.link(dve.tensor_scalar(pick[:, 0:1], pick[:, 0:1], -1.0, 1.0, ALU.mult, ALU.add))
            ch.link(dve.tensor_tensor(pick[:, 0:1], pick[:, 0:1], over1[:, D:F1], ALU.add))
            ch.link(dve.reciprocal(rinv_over[:, :], pick[:, 0:1]))
            ch.link(dve.scalar_tensor_tensor(out=over2[:, :], in0=two.carry[:, 0:D], scalar=1e-10, in1=over2[:, :],
                                             op0=ALU.mult, op1=ALU.add))
            dve.scalar_tensor_tensor(out=last[:, :], in0=over1[:, 0:D], scalar=rinv_over[:, :], in1=over2[:, :],
                                     op0=ALU.mult, op1=ALU.add).then_inc(last_made, 1)
            dve.wait_ge(last_made, 1)


def col_of(x, c):
    return x[:, chunk_cols(c)].rearrange("p (t o) -> p t o", o=1)


def across(x, n):
    return x[:, 0:n].rearrange("p (o f) -> p o f", o=1)


GROUPS = CH // 2


def pair_weights(k, a, w):
    nc = k.nc
    k.phase("pair_weights")
    NB = 8
    with ExitStack() as st:
        w2 = k.sb("w2", [P, P], F32, st)
        w2t = k.sb("w2t", [P, P], F32, st)
        pi1 = k.sb("pi1", [P, D], F32, st)
        pi1t = k.sb("pi1t", [D, P], F32, st)
        pi2 = k.sb("pi2", [D, D], F32, st)
        pi12 = k.sb("pi12", [P, D], F32, st)
        pi3 = k.sb("pi3", [D, D, NB], F32, st)
        pi3b = k.sb("pi3b", [D, NB, D], F32, st)
        pi3t = k.sb("pi3t", [D, NB, D], F32, st)
        ii1 = k.sb("ii1", [D, D], F32, st)
        b2 = k.sb("b2", [P, 1], F32, st)
        bs = k.sb("bs", [D, 3], F32, st)
        ps = [k.pb(f"ps{n}", [P, 512], F32, st) for n in range(4)]
        cleared, landed, pe_done, dve_done = (k.sem(n, st) for n in ("cleared", "landed", "pe_done", "dve_done"))
        block = st.enter_context(nc.Block())
        g = lambda n: a["L1_gnn_" + n]
        loads = []
        for q in range(2):
            h = slice(q * D, (q + 1) * D)
            loads += [(w.first[h, h], g("pp_W1")), (w2[h, h], g("pp_W2")), (w.last[h, h], g("ii_W2")),
                      (w.first_b[h, :], col(g("pp_b1"))), (b2[h, :], col(g("pp_b2"))),
                      (w.tanh_b[h, :], col(g("ii_b1"))),
                      (w.last_b[:, h], row(g("ii_b2")).to_broadcast([P, D]))]
        loads += [(pi1[:, :], g("pi_W1")), (pi2[:, :], g("pi_W2")), (ii1[:, :], g("ii_W1")),
                  (pi3[:, :, :].rearrange("p c b -> p (c b)"), g("pi_W3")),
                  (bs[:, 0:1], col(g("pi_b1"))), (bs[:, 1:2], col(g("pi_b2")))]

        @block.sync
        def _(sp):
            sp.wait_ge(cleared, 3)
            for to, src in loads:
                sp.dma_start(to, src).then_inc(landed, 16)
            sp.wait_ge(landed, 16 * len(loads))

        @block.tensor
        def _(pe):
            pe.wait_ge(landed, 16 * len(loads))
            pe.transpose(ps[0][0:D, 0:P], pi1[:, :], k.ident[:, :])
            pe.transpose(ps[0][:, P:2 * P], w2[:, :], k.ident[:, :])
            pe.matmul(ps[0][0:D, 300:301], pi1[:, :], b2[:, :], start=True, stop=True).then_inc(pe_done, 1)
            pe.wait_ge(dve_done, 1)
            for b in range(NB):
                last = pe.transpose(ps[1][0:D, b * D:(b + 1) * D], pi3b[:, b, :], k.ident[0:D, 0:D])
            last.then_inc(pe_done, 1)
            pe.wait_ge(dve_done, 2)
            pe.matmul(ps[2][:, 0:D], pi1t[:, :], pi2[:, :], start=True, stop=True)
            pe.matmul(ps[2][0:D, D:D + 1], pi2[:, :], bs[:, 2:3], start=True, stop=True).then_inc(pe_done, 1)
            pe.wait_ge(dve_done, 3)
            for b in range(NB):
                last = pe.matmul(ps[3][0:D, b * D:(b + 1) * D], pi3t[:, b, :], ii1[:, :], start=True, stop=True)
            last.then_inc(pe_done, 1)
            pe.wait_ge(dve_done, 4)
            pe.matmul(ps[2][:, 2 * D:3 * D], w2t[:, :], pi12[:, :], start=True, stop=True).then_inc(pe_done, 1)

        @block.vector
        def _(dve):
            for x in (w.first, w2, w.last):
                dve.memset(x[:, :], 0.0).then_inc(cleared, 1)
            dve.wait_ge(landed, 16 * len(loads))
            dve.tensor_copy(pi3b[:, :, :], pi3[:, :, :].rearrange("p c b -> p b c")).then_inc(dve_done, 1)
            dve.wait_ge(pe_done, 1)
            dve.tensor_copy(pi1t[:, :], ps[0][0:D, 0:P])
            dve.tensor_copy(w2t[:, :], ps[0][:, P:2 * P])
            dve.tensor_tensor(bs[:, 2:3], ps[0][0:D, 300:301], bs[:, 0:1], ALU.add).then_inc(dve_done, 1)
            dve.wait_ge(pe_done, 2)
            dve.tensor_copy(pi3t[:, :, :].rearrange("p b c -> p (b c)"), ps[1][0:D, :]).then_inc(dve_done, 1)
            dve.wait_ge(pe_done, 3)
            dve.tensor_tensor(w.middle_b[:, :], ps[2][0:D, D:D + 1], bs[:, 1:2], ALU.add)
            dve.tensor_copy(pi12[:, :], ps[2][:, 0:D]).then_inc(dve_done, 1)
            dve.wait_ge(pe_done, 4)
            dve.tensor_copy(w.basis[:, :], ps[3][0:D, :])
            dve.wait_ge(pe_done, 5)
            dve.tensor_copy(w.middle[:, :], ps[2][:, 2 * D:3 * D]).then_inc(dve_done, 1)
            dve.wait_ge(dve_done, 5)


class PairWeights:
    def __init__(self, k, st):
        self.first = k.sb("first", [P, P], F32, st)
        self.first_b = k.sb("first_b", [P, 1], F32, st)
        self.middle = k.sb("middle", [P, D], F32, st)
        self.middle_b = k.sb("middle_b", [D, 1], F32, st)
        self.basis = k.sb("basis", [D, 8 * D], F32, st)
        self.tanh_b = k.sb("tanh_b", [P, 1], F32, st)
        self.last = k.sb("last", [P, P], F32, st)
        self.last_b = k.sb("last_b", [P, P], F32, st)


def layer1(k, a, o, x1, x2):
    nc = k.nc
    with ExitStack() as st:
        k.phase("pairs")
        w = PairWeights(k, st)
        xs = k.sb("xs", [P, T, D], F32, st)
        scan = Scan(k, st, "sum", o, D)
        pair_weights(k, a, w)
        sender = Sender(k, st, o, scan)
        pair_rows(k, o, w, x1, x2, xs, scan, sender)


def pair_rows(k, o, w, x1, x2, xs, scan, sender):
    nc = k.nc
    k.phase("pair_rows")
    G2 = 2 * CH
    with ExitStack() as st:
        k.opened = k.sem("opened", st)
        gb = [k.sb(f"rows{s}", [P, CH, 2, D], F32, st) for s in range(2)]
        idx = [k.sb(f"idx{s}", [P, 2, CH], I32, st) for s in range(2)]
        xc = k.sb("xc", [P, G2, D], F32, st)
        h = [k.sb(f"h{s}", [P, G2, D], F32, st) for s in range(2)]
        ht = k.sb("ht", [P, 2, 2 * P], F32, st)
        tt = k.sb("tt", [P, 2, 2 * P], F32, st)
        ut = k.sb("ut", [D, 2, 2 * P], F32, st)
        prod = k.sb("prod", [P, 2, 8, D], F32, st)
        i1 = k.sb("i1", [P, 2, 2, D], F32, st)
        th = k.sb("th", [P, 2, P], F32, st)
        buf = [k.sb(f"buf{s}", [P, D, CH], F32, st) for s in range(2)]
        rows_copied = k.sem("rows_copied", st)
        ln1 = ln_buffers(k, st, "ln", G2)
        ps_t, ps_p, ps_u, ps_e = (k.pb(n, [P, 512], F32, st) for n in ("ps_t", "ps_p", "ps_u", "ps_e"))
        ps_o = [k.pb(f"ps_o{n}", [P, 512], F32, st) for n in range(2)]
        ps_i = [k.pb(f"ps_i{j}", [P, 512], F32, st) for j in range(2)]
        (staged, chain1, chain2, chain0, h_made, turned, ht_made, p_made, tt_made, u_made, ut_made, i_made, i_read, i1_made,
         e_made, th_made, o_made, o_read, run_made) = (
            k.sem(x, st) for x in ("staged", "chain1", "chain2", "chain0", "h_made", "turned", "ht_made", "p_made", "tt_made",
                                   "u_made", "ut_made", "i_made", "i_read", "i1_made", "e_made", "th_made",
                                   "o_made", "o_read", "run_made"))
        landed = [k.sem(f"landed{s}", st) for s in range(2)]
        freed = [k.sem(f"freed{s}", st) for s in range(2)]
        block = st.enter_context(nc.Block())

        @block.gpsimd
        def _(pool):
            pool.engine_nop().then_inc(k.opened, 1)
            gather_and_send(pool, k, x1, [o.other, o.key], gb, idx, staged, landed, freed, 1, sender, x2,
                            ready=(rows_copied, 16))

        @block.sync
        def _(sp):
            sp.dma_start(x2.rearrange("(a b) f -> a (b f)", a=16),
                         x1.rearrange("(a b) f -> a (b f)", a=16)).then_inc(rows_copied, 16)
            sp.wait_ge(rows_copied, 16)

        END = NCH * GROUPS
        assert END % 2 == 0

        def lagged(n, g, s, stages):
            for lag, stage in stages:
                if not isinstance(n, int) or n + g >= lag:
                    stage(n + (g - lag), (s * GROUPS + g - lag) % 2)

        def lagged_rest(stages):
            for e in range(max(lag for lag, _ in stages)):
                for lag, stage in stages:
                    if lag > e:
                        stage(END + e - lag, (e - lag) % 2)

        @block.scalar
        def _(act):
            def copy_turned(m, ring):
                wait_for(act, p_made, m - 1)
                act.wait_ge(turned, m + 1)
                act.activation(ht[:, ring, :], ps_t[:, 0:2 * P], ACT.Copy).then_inc(ht_made, 1)

            def first_tanh(m, ring):
                wait_for(act, u_made, m - 1)
                act.wait_ge(p_made, m + 1)
                act.activation(tt[:, ring, :], ps_p[:, 0:2 * P], ACT.Tanh, bias=w.first_b[:, :]).then_inc(tt_made, 1)

            def middle(m, ring):
                wait_for(act, i_made, (m - 1) * 2)
                act.wait_ge(u_made, m + 1)
                act.activation(ut[:, ring, :], ps_u[0:D, 0:2 * P], ACT.Identity,
                               bias=w.middle_b[:, :]).then_inc(ut_made, 1)

            def second_tanh(m, ring):
                wait_for(act, o_made, m - 1)
                act.wait_ge(e_made, m + 1)
                act.activation(th[:, ring, :], ps_e[:, 0:P], ACT.Tanh, bias=w.tanh_b[:, :]).then_inc(th_made, 1)

            def square(c, s):
                ln_square(act, ln1, xc[:, :, :], c)
                act.activation(xs[:, chunk_cols(c), :], gb[s][:, :, 1, :], ACT.Copy).then_inc(freed[s], 1)

            stages = ((0, copy_turned), (1, first_tanh), (2, middle), (4, second_tanh))

            def chunk(c, s, more):
                for g in range(GROUPS):
                    lagged(c * GROUPS, g, s, stages)
                    if g == 4 and more:
                        square(c + 1, 1 - s)
                    if g == 5 and more:
                        ln_root(act, ln1, c + 1)

            square(0, 0)
            ln_root(act, ln1, 0)
            chunk(0, 0, True)
            chunk(1, 1, True)
            with act.Fori(1, NIT - 1) as i:
                for s in range(2):
                    chunk(2 * i + s, s, True)
            chunk(NCH - 2, 0, True)
            chunk(NCH - 1, 1, False)
            lagged_rest(stages[1:])

        @block.tensor
        def _(pe):
            def first(m, ring):
                wait_for(pe, tt_made, m)
                pe.wait_ge(ht_made, m + 1)
                pe.matmul(ps_p[:, 0:2 * P], w.first[:, :], ht[:, ring, :], start=True, stop=True).then_inc(p_made, 1)

            def middle(m, ring):
                wait_for(pe, ut_made, m)
                pe.wait_ge(tt_made, m + 1)
                pe.matmul(ps_u[0:D, 0:2 * P], w.middle[:, :], tt[:, ring, :], start=True, stop=True).then_inc(u_made, 1)

            def basis(m, ring):
                pe.wait_ge(ut_made, m + 1)
                for j in range(2):
                    if not isinstance(m, int) or m >= 1:
                        pe.wait_ge(i_read, (m - 1) * 2 + (j + 1))
                    pe.matmul(ps_i[j][:, :], ut[:, ring, j * P:(j + 1) * P], w.basis[:, :], start=True,
                              stop=True).then_inc(i_made, 1)

            def turn_i1(m, ring):
                wait_for(pe, th_made, m)
                pe.wait_ge(i1_made, m + 1)
                pe.transpose(ps_e[:, 0:P], i1[:, ring, :, :].rearrange("p t f -> p (t f)"), k.ident[:, :]).then_inc(e_made, 1)

            def last(m, ring):
                wait_for(pe, o_read, m - 1)
                pe.wait_ge(th_made, m + 1)
                pe.matmul(ps_o[ring][:, 0:P], th[:, ring, :], w.last[:, :], start=True, stop=True).then_inc(o_made, 1)

            stages = ((1, first), (2, middle), (5, last), (3, basis), (4, turn_i1))

            def turn(i):
                for s in range(2):
                    n = (2 * i + s) * GROUPS
                    pe.wait_ge(h_made, 2 * i + (s + 1))
                    for g in range(GROUPS):
                        wait_for(pe, ht_made, n + g)
                        for j in range(2):
                            turning = pe.transpose(ps_t[:, j * P:(j + 1) * P],
                                                   h[s][:, 4 * g + 2 * j:4 * g + 2 * j + 2, :].rearrange("p n f -> p (n f)"),
                                                   k.ident[:, :])
                        turning.then_inc(turned, 1)
                        lagged(n, g, s, stages)

            turn(0)
            with pe.Fori(1, NIT) as i:
                turn(i)
            lagged_rest(stages)
            pe.wait_ge(ht_made, END)
            pe.wait_ge(run_made, NCH)
            scan.carries_tensor(pe, ps_t)

        @block.vector
        def _(dve):
            ch0 = Chain(dve, chain0)
            scan.prepare(dve, ch0)
            sender.prepare(dve, ch0)
            sender.start(dve)
            ch1 = Chain(dve, chain1, LN_LINKS)
            ch2 = Chain(dve, chain2, Scan.LINKS)

            def centre(c, s, turn):
                ch1.turn(c)
                dve.wait_ge(landed[s], turn * 16 * G2)
                dve.wait_ge(k.opened, 1)
                ln_centre(dve, ch1, ln1, gb[s][:, :, :, :].rearrange("p t g f -> p (t g) f"), xc[:, :, :])

            def scale(c, s):
                wait_for(dve, turned, (c - 1) * GROUPS)
                ln_scale(dve, ch1, ln1, xc[:, :, :], h[s][:, :, :], c, 0.0).then_inc(h_made, 1)
                dve.wait_ge(h_made, c + 1)

            def contract(c, g, ring):
                m = c * GROUPS + g
                for j in range(2):
                    dve.wait_ge(i_made, m * 2 + j + 1)
                    factor = o.val["basis"][:, bass.ds(c * CH + (2 * g + j), 1), :].rearrange("p o (b f) -> p (o b) f", f=1)
                    dve.tensor_tensor(prod[:, j, :, :], ps_i[j][:, :].rearrange("p (b f) -> p b f", b=8),
                                      factor.to_broadcast([P, 8, D]), ALU.mult).then_inc(i_read, 1)
                    dve.wait_ge(i_read, m * 2 + j + 1)
                    if j == 0:
                        wait_for(dve, e_made, m - 1)
                    made = dve.tensor_reduce(i1[:, ring, j, :], prod[:, j, :, :].rearrange("p b f -> p f b"), AX.X, ALU.add)
                made.then_inc(i1_made, 1)

            def take(m, g, s, ring):
                dve.wait_ge(o_made, m + 1)
                dve.tensor_tensor(buf[s][:, :, 2 * g:2 * g + 2].rearrange("p f t -> p t f"),
                                  ps_o[ring][:, 0:P].rearrange("p (t f) -> p t f", t=2),
                                  w.last_b[:, :].rearrange("p (t f) -> p t f", t=2), ALU.add).then_inc(o_read, 1)

            def scan_chunk(c, i, s):
                ch2.turn(c)
                dve.wait_ge(o_read, (c + 1) * GROUPS)
                scan.chunk(dve, ch2, buf[s][:, :, :], c, run_made)
                sender.vector_chunk(dve, c, i, s, buf[s][:, :, :], add=xs)

            def chunk(c, i, s, turn):
                before = not isinstance(c, int) or c > 0
                for g in range(GROUPS):
                    contract(c, g, (s * GROUPS + g) % 2)
                    if g < 2:
                        if before:
                            take(c * GROUPS + (g - 2), GROUPS + g - 2, 1 - s, (s * GROUPS + g) % 2)
                    else:
                        take(c * GROUPS + (g - 2), g - 2, s, (s * GROUPS + g) % 2)
                    if g == 1 and before:
                        scan_chunk(c - 1, i - 1 + s, 1 - s)
                    if turn is not None:
                        if g == 1:
                            centre(c + 1, 1 - s, turn)
                        if g == 2:
                            ln_var(dve, ch1, ln1, c + 1)
                        if g == 3:
                            scale(c + 1, 1 - s)

            centre(0, 0, 1)
            ln_var(dve, ch1, ln1, 0)
            scale(0, 0)
            for s in range(2):
                chunk(s, 0, s, s + 1)
            with dve.Fori(1, NIT - 1) as i:
                for s in range(2):
                    chunk(2 * i + s, i, s, i + 1 + s)
            chunk(NCH - 2, NIT - 1, 0, NIT)
            chunk(NCH - 1, NIT - 1, 1, None)
            for g in range(2):
                take(END + g - 2, GROUPS + g - 2, 1, g % 2)
            scan_chunk(NCH - 1, NIT - 1, 1)
            sender.vector_end(dve, ps_t)


class Sender:

    def __init__(self, k, st, o, scan):
        self.k, self.o, self.scan = k, o, scan
        self.stages = [k.sb(f"stage{s}", [P, CH, D], F32, st) for s in range(2)]
        self.idx = [k.sb(f"send_idx{s}", [P, CH], I32, st) for s in range(2)]
        self.picked = k.sb("picked", [P, D, CH], F32, st)
        self.pick = k.sb("pick", [P, D], F32, st)
        self.over = k.sb("over", [P, D], F32, st)
        self.row = k.sb("row", [P, D], F32, st)
        if scan.largest:
            self.size = k.sb("size", [P, D, CH], F32, st)
            self.finite = k.sb("finite", [P, D, CH], I32, st)
            self.away = k.sb("away", [P, T], F32, st)
        self.staged, self.rows_made, self.row_made, self.row_sent, self.chain, self.chain_end = (
            k.sem(f"send_{x}", st) for x in ("staged", "rows_made", "row_made", "row_sent", "chain", "chain_end"))
        self.sent = [k.sem(f"sent{s}", st) for s in range(2)]
        self.links = 6 if scan.largest else 3

    def prepare(self, dve, ch):
        ch.link(dve.memset(self.over[:, :], -BIG if self.scan.largest else 0.0))
        if self.scan.largest:
            ch.link(dve.tensor_scalar(self.away[:, :], self.o.over[:, :], -1.0, BIG, ALU.add, ALU.mult))

    def start(self, dve):
        self.ch = Chain(dve, self.chain, self.links)

    def finite_only(self, dve, ch, to, x, size, finite):
        ch.link(dve.scalar_tensor_tensor(out=size, in0=x, scalar=-1.0, in1=x, op0=ALU.mult, op1=ALU.max))
        ch.link(dve.tensor_scalar(finite, size, FMAX, -1.0, ALU.is_le, ALU.mult))
        return dve.tensor_tensor(to.bitcast(I32), finite, x.bitcast(I32), ALU.bitwise_and)

    PARTS = 6

    def vector_part(self, dve, n, c, i, s, buf):
        ch, picked = self.ch, self.picked[:, :, :]
        if n == 0:
            ch.turn(c)
            away = self.away[:, chunk_cols(c)].rearrange("p (o t) -> p o t", o=1).to_broadcast([P, D, CH])
            ch.link(dve.tensor_tensor(picked, buf, away, ALU.add))
        if n == 1:
            ch.link(dve.tensor_reduce(self.pick[:, :], picked, AX.X, ALU.max))
        if n == 2:
            ch.link(dve.tensor_tensor(self.over[:, :], self.over[:, :], self.pick[:, :], ALU.max))
            ch.link(dve.scalar_tensor_tensor(out=self.size[:, :, :], in0=buf, scalar=-1.0, in1=buf, op0=ALU.mult,
                                             op1=ALU.max))
        if n == 3:
            ch.link(dve.tensor_scalar(self.finite[:, :, :], self.size[:, :, :], FMAX, -1.0, ALU.is_le, ALU.mult))
        if n == 4:
            ch.link(dve.tensor_tensor(picked.bitcast(I32), self.finite[:, :, :], buf.bitcast(I32), ALU.bitwise_and))
        if n == 5:
            wait_for(dve, self.sent[s], i * 16 * CH)
            dve.tensor_scalar(self.stages[s][:, :, :].rearrange("p t f -> p f t"), picked, 1.0, None,
                              ALU.mult).then_inc(self.rows_made, 1)
            dve.wait_ge(self.rows_made, c + 1)

    def vector_chunk(self, dve, c, i, s, buf, add=None):
        ch = self.ch
        if self.scan.largest:
            for n in range(self.PARTS):
                self.vector_part(dve, n, c, i, s, buf)
            return
        ch.turn(c)
        wait_for(dve, self.sent[s], i * 16 * CH)
        stage = self.stages[s]
        dve.tensor_tensor(stage[:, :, :], buf.rearrange("p f t -> p t f"), add[:, chunk_cols(c), :],
                          ALU.add).then_inc(self.rows_made, 1)
        dve.wait_ge(self.rows_made, c + 1)
        over = self.o.over[:, chunk_cols(c)].rearrange("p (o t) -> p o t", o=1).to_broadcast([P, D, CH])
        ch.link(dve.tensor_tensor(self.picked[:, :, :], stage[:, :, :].rearrange("p t f -> p f t"), over, ALU.mult))
        ch.link(dve.tensor_reduce(self.pick[:, :], self.picked[:, :, :], AX.X, ALU.add))
        ch.link(dve.tensor_tensor(self.over[:, :], self.over[:, :], self.pick[:, :], ALU.add))

    def vector_end(self, dve, ps):
        ch = Chain(dve, self.chain_end)
        ch.link(self.scan.carries_vector(dve, ps))
        carry = self.scan.carry[:, 0:D]
        if self.scan.largest:
            ch.link(dve.tensor_tensor(self.pick[:, :], self.over[:, :], carry, ALU.max))
            self.finite_only(dve, ch, self.row[:, :], self.pick[:, :], self.size[:, :, 0], self.finite[:, :, 0]
                             ).then_inc(self.row_made, 1)
        else:
            dve.tensor_tensor(self.row[:, :], self.over[:, :], carry, ALU.add).then_inc(self.row_made, 1)

    def send(self, pool, set_limit, limit, table, c, i, s):
        wait_for(pool, self.sent[s], i * 16 * CH)
        pool.wait_ge(self.k.opened, 1)
        pool.tensor_copy(self.idx[s][:, :], self.o.last_in[:, chunk_cols(c)]).then_inc(self.staged, 1)
        pool.wait_ge(self.staged, c + 1)
        pool.wait_ge(self.rows_made, c + 1)
        set_limit()
        for t in range(CH):
            pool.indirect_dma_start(table, bass.IndirectOffsetOnAxis(ap=self.idx[s][:, t:t + 1], axis=0),
                                    self.stages[s][:, t, :], None, bounds_check=limit,
                                    oob_is_err=False).then_inc(self.sent[s], 16)

    def send_end(self, pool, limit, table):
        pool.wait_ge(self.row_made, 1)
        pool.indirect_dma_start(table, bass.IndirectOffsetOnAxis(ap=self.o.last_over[:, :], axis=0), self.row[:, :],
                                None, bounds_check=limit, oob_is_err=False).then_inc(self.row_sent, 16)
        for s in range(2):
            pool.wait_ge(self.sent[s], NIT * 16 * CH)
        pool.wait_ge(self.row_sent, 16)


def gather_and_send(pool, k, gather, idxs, stages, idx_stage, staged, landed, freed, per_turn, sender, table, ready=None):
    limit, set_limit = bound_register(pool, k, N - 1)

    def gather_chunk(c, i, s):
        wait_for(pool, freed[s], i * per_turn)
        pool.wait_ge(k.opened, 1)
        for g, idx in enumerate(idxs):
            pool.tensor_copy(idx_stage[s][:, g, :], idx[:, chunk_cols(c)]).then_inc(staged, 1)
        pool.wait_ge(staged, (c + 1) * len(idxs))
        set_limit()
        for t in range(CH):
            for g in range(len(idxs)):
                pool.indirect_dma_start(
                    stages[s][:, t, g, :], None, gather,
                    bass.IndirectOffsetOnAxis(ap=idx_stage[s][:, g, t:t + 1], axis=0),
                    bounds_check=limit, oob_is_err=False).then_inc(landed[s], 16)

    def send(c, i, s):
        sender.send(pool, set_limit, limit, table, c, i, s)

    for s in range(2):
        gather_chunk(s, 0, s)
    gather_chunk(2, 1, 0)
    gather_chunk(3, 1, 1)
    if ready is not None:
        pool.wait_ge(*ready)
    send(0, 0, 0)
    gather_chunk(4, 2, 0)
    send(1, 0, 1)
    gather_chunk(5, 2, 1)
    send(2, 1, 0)
    with pool.Fori(3, NIT) as i:
        gather_chunk(2 * i, i, 0)
        send(2 * i - 3, i - 2, 1)
        gather_chunk(2 * i + 1, i, 1)
        send(2 * i - 2, i - 1, 0)
    send(NCH - 3, NIT - 2, 1)
    send(NCH - 2, NIT - 1, 0)
    send(NCH - 1, NIT - 1, 1)
    sender.send_end(pool, limit, table)


def copy_rows(k, st, block, x, x1):
    k.phase("copy")
    copied = k.sem("copied", st)

    @block.sync
    def _(sp):
        sp.dma_start(x1.rearrange("(a b) f -> a (b f)", a=16),
                     x.rearrange("(a b) f -> a (b f)", a=16)).then_inc(copied, 16)
        sp.wait_ge(copied, 16)


def own_rows(k, st, block, place_of):
    k.phase("own")
    Q = 125
    own = k.sb("own", [Q, N // Q], I32, st)
    copied, made = k.sem("copied", st), k.sem("made", st)

    @block.gpsimd
    def _(pool):
        pool.iota(own[:, :], [[1, N // Q]], base=0, channel_multiplier=N // Q).then_inc(made, 1)

    @block.sync
    def _(sp):
        sp.wait_ge(made, 1)
        sp.dma_start(place_of.rearrange("(p j) o -> p (j o)", p=Q), own[:, :]).then_inc(copied, 16)
        sp.wait_ge(copied, 16)


J = 25
PD = 125
NBLK = N // (PD * J)
assert NBLK * PD * J == N and NBLK % 2 == 0


def node_block(table, c, j=J):
    return table[bass.ds(c * (PD * j), PD * j), :].rearrange("(p j) f -> p (j f)", j=j)


def flat(x):
    return x.rearrange("p j f -> p (j f)")


def move_blocks(sp, loads, stores, loaded, read, made, stored, cleared):
    def load(c, s):
        for table, tiles in loads:
            sp.dma_start(flat(tiles[s][0:PD, 0:J, :]), node_block(table, c)).then_inc(loaded[s], 16)

    def store(c, so_far, s):
        sp.wait_ge(made, so_far)
        for table, tiles in stores:
            sp.dma_start(node_block(table, c), flat(tiles[s][0:PD, 0:J, :])).then_inc(stored[s], 16)

    sp.wait_ge(cleared, 2 * len(loads))
    for s in range(2):
        load(s, s)
    with sp.Fori(0, NBLK // 2 - 1) as i:
        for s in range(2):
            for sem, n in read:
                sp.wait_ge(sem, (2 * i + (s + 1)) * n)
            load(2 * i + s + 2, s)
            store(2 * i + s, 2 * i + (s + 1), s)
    for s in range(2):
        store(NBLK - 2 + s, NBLK - 1 + s, s)
    for s in range(2):
        sp.wait_ge(stored[s], NBLK // 2 * 16 * len(stores))


def clear_blocks(dve, tiles, cleared):
    for x in tiles:
        dve.memset(x[:, :, :], 0.0).then_inc(cleared, 1)


def norm_nodes(k, stack, block, x, ys):
    xt = [k.sb(f"xt{s}", [P, J, D], F32, stack) for s in range(2)]
    yt = [k.sb(f"yt{s}", [P, J, D], F32, stack) for s in range(2)]
    xc = k.sb("xc", [P, J, D], F32, stack)
    ln = ln_buffers(k, stack, "ln", J)
    chain, made, cleared, x_read = (k.sem(n, stack) for n in ("chain", "made", "cleared", "x_read"))
    loaded, stored = ([k.sem(f"{n}{s}", stack) for s in range(2)] for n in ("loaded", "stored"))

    @block.sync
    def _(sp):
        move_blocks(sp, [(x, xt)], [(y, yt) for y in ys], loaded, [(x_read, 1)], made, stored, cleared)

    @block.scalar
    def _(act):
        with act.Fori(0, NBLK) as c:
            ln_scalar(act, ln, xc[:, :, :], c)

    @block.vector
    def _(dve):
        clear_blocks(dve, xt, cleared)
        ch = Chain(dve, chain, 2 * (LN_LINKS - 1))
        def turn(i):
            ch.turn(i)
            for s in range(2):
                c = 2 * i + s
                dve.wait_ge(loaded[s], (i + 1) * 16)
                wait_for(dve, stored[s], i * 16 * len(ys))
                ln_vector(dve, ch, ln, xt[s][:, :, :], xc[:, :, :], yt[s][:, :, :], c, 0.0,
                          freed=(x_read, c + 1)).then_inc(made, 1)

        turn(0)
        with dve.Fori(1, NBLK // 2) as i:
            turn(i)


class Perceptron:

    GROUP = 4

    def __init__(self, k, st, n, blocks, pt, xt, x3t, h3t):
        self.k, self.n, self.blocks = k, n, blocks
        self.pt, self.xt, self.x3t, self.h3t = pt, xt, x3t, h3t
        self.rows = [min(self.GROUP, n - at) for at in range(0, n, self.GROUP)]
        self.groups = len(self.rows)
        assert n % 2 == 0 and blocks % 2 == 0
        self.w0 = k.sb("w0", [P, 2, P], F32, st)
        self.b0 = k.sb("b0", [P, 2], F32, st)
        self.w1 = k.sb("w1", [P, 2, D], F32, st)
        self.b1 = k.sb("b1", [P, 1, D], F32, st)
        self.turned_p = k.sb("turned_p", [P, 2, 2 * P], F32, st)
        self.hidden = k.sb("hidden", [P, 2, 2, 2, 2 * P], F32, st)
        self.ln = ln_buffers(k, st, "mln", n)
        self.ps_t = [k.pb(f"ps_t{n}", [P, 512], F32, st) for n in range(2)]
        self.ps_u = [k.pb(f"ps_u{n}", [P, 1024], F32, st) for n in range(2)]
        self.ps_o = k.pb("ps_o", [P, 512], F32, st)
        (self.made, self.turned, self.copied, self.x_biased, self.x3_made, self.w_landed, self.u_made, self.o_made) = (
            k.sem(n, st) for n in ("mlp_made", "mlp_turned", "mlp_copied", "x_biased", "x3_made", "mlp_w_landed",
                                   "u_made", "o_made"))
        self.hidden_made = [k.sem(f"hidden_made{h}", st) for h in range(2)]
        self.chain = k.sem("mlp_chain", st)

    def load_weights(self, sp, a):
        loads = [(self.w0[q * D:(q + 1) * D, :, :].rearrange("p h n -> p (h n)"), a["L2_gnn_W0"]) for q in range(2)]
        loads += [(self.b0[:, h:h + 1], col(a["L2_gnn_b0"])[h * P:(h + 1) * P, :]) for h in range(2)]
        loads += [(self.w1[:, :, :], a["L2_gnn_W1"].rearrange("(h p) f -> p h f", h=2)),
                  (self.b1[:, 0, :], row(a["L2_gnn_b1"]).to_broadcast([P, D]))]
        self.weights = 16 * len(loads)
        for to, src in loads:
            sp.dma_start(to, src).then_inc(self.w_landed, 16)
        sp.wait_ge(self.w_landed, self.weights)

    WEIGHTS = 16 * 6


    def turn_rows(self, pe, n, g, s):
        ring = (s * self.groups + g) % 2
        wait_for(pe, self.copied, n + (g - 1))
        for q in range(self.rows[g] // 2):
            at = g * self.GROUP + 2 * q
            last = pe.transpose(self.ps_t[ring][:, q * P:(q + 1) * P],
                                self.pt[s][:, at:at + 2, :].rearrange("p j f -> p (j f)"), self.k.ident[:, :])
        last.then_inc(self.turned, 1)

    def first(self, pe, count, g, ring):
        pe.wait_ge(self.copied, count + 1)
        for h in range(2):
            wait_for(pe, self.hidden_made[h], count - 1)
        w = self.rows[g] // 2 * P
        for h in range(2):
            for e in range(2):
                rows, at = slice(e * D, (e + 1) * D), e * 512 + h * 2 * P
                last = pe.matmul(self.ps_u[ring][:, at:at + w], self.w0[rows, h, :], self.turned_p[rows, ring, 0:w],
                                 start=True, stop=True)
        last.then_inc(self.u_made, 1)

    def second(self, pe, count, g, ring):
        for h in range(2):
            pe.wait_ge(self.hidden_made[h], count + 1)
        wait_for(pe, self.x3_made, count)
        for q in range(self.rows[g]):
            for h in range(2):
                last = pe.matmul(self.ps_o[:, q * D:(q + 1) * D],
                                 self.hidden[:, ring, h, q % 2, q // 2 * P:(q // 2 + 1) * P], self.w1[:, h, :],
                                 start=h == 0, stop=h == 1)
        last.then_inc(self.o_made, 1)

    def tensor_block(self, pe, c, s):
        n, G = c * self.groups, self.groups
        for g in range(G):
            self.turn_rows(pe, n, g, s)
            for stage, lag in ((self.first, 1), (self.second, 3)):
                if not isinstance(n, int) or n + g >= lag:
                    stage(pe, n + (g - lag), (g - lag) % G, (s * G + g - lag) % 2)

    def tensor_rest(self, pe):
        G = self.groups
        end = self.blocks * G
        self.first(pe, end - 1, G - 1, 1)
        for lag in (3, 2, 1):
            self.second(pe, end - lag, G - lag, lag % 2)


    def hide(self, act, count, g, ring):
        act.wait_ge(self.u_made, count + 1)
        wait_for(act, self.o_made, count - 1)
        w = self.rows[g] // 2 * P
        for h in range(2):
            act.activation(self.hidden[:, ring, h, :, 0:w],
                           self.ps_u[ring][:, :].rearrange("p (e h n) -> p e h n", e=2, h=2)[:, :, h, 0:w], ACT.Relu,
                           bias=self.b0[:, h:h + 1]).then_inc(self.hidden_made[h], 1)

    def scalar_block(self, act, c, s):
        n, G = c * self.groups, self.groups
        for g in range(G):
            ring = (s * G + g) % 2
            act.wait_ge(self.turned, n + g + 1)
            wait_for(act, self.u_made, n + (g - 1))
            w = self.rows[g] // 2 * P
            act.activation(self.turned_p[:, ring, 0:w], self.ps_t[ring][:, 0:w], ACT.Copy).then_inc(self.copied, 1)
            if not isinstance(n, int) or n + g >= 1:
                self.hide(act, n + (g - 1), (g - 1) % G, 1 - ring)
            if not isinstance(c, int) or c > 0:
                if g == 2:
                    self.square(act, c - 1, 1 - s)
                if g == 3:
                    ln_root(act, self.ln, c - 1)

    def square(self, act, c, s):
        ln_square(act, self.ln, self.centred(s), c)

    def scalar_rest(self, act):
        self.hide(act, self.blocks * self.groups - 1, self.groups - 1, 1)
        self.square(act, self.blocks - 1, 1)
        ln_root(act, self.ln, self.blocks - 1)


    def centred(self, s):
        return self.h3t[s][:, :, :]

    def bias(self, dve, c, s):
        dve.tensor_tensor(self.xt[s][:, :, :], self.xt[s][:, :, :], spread(self.b1[:, :, :], P, self.n, D),
                          ALU.add).then_inc(self.x_biased, 1)
        dve.wait_ge(self.x_biased, c + 1)

    def add(self, dve, c, g, s):
        dve.wait_ge(self.o_made, c * self.groups + (g + 1))
        these = slice(g * self.GROUP, g * self.GROUP + self.rows[g])
        dve.tensor_tensor(self.x3t[s][:, these, :], self.ps_o[:, 0:self.rows[g] * D].rearrange("p (j f) -> p j f", f=D),
                          self.xt[s][:, these, :], ALU.add).then_inc(self.x3_made, 1)

    def centre(self, dve, ch, c, s):
        ch.turn(c)
        dve.wait_ge(self.x3_made, (c + 1) * self.groups)
        dve.wait_ge(self.turned, (c + 1) * self.groups)
        ln_centre(dve, ch, self.ln, self.x3t[s][:, :, :], self.centred(s))

    def var(self, dve, ch, c):
        ln_var(dve, ch, self.ln, c)

    def scale(self, dve, ch, c, s):
        ln_scale(dve, ch, self.ln, self.centred(s), self.h3t[s][:, :, :], c, 0.0).then_inc(self.made, 1)


class Propagation:

    def __init__(self, k, st):
        k.phase("prop")
        self.other = k.sb("other", [P, T], I32, st)
        self.inv = k.sb("inv", [P, T], F32, st)
        self.root = k.sb("root", [P, T], F32, st)
        self.uproot = k.sb("uproot", [P, T], F32, st)
        self.g = k.sb("g", [P, T, D], F32, st)
        self.total = k.sb("total", [P, T, D], F32, st)
        self.over_inv = k.sb("over_inv", [P, 1], F32, st)
        self.over_g = k.sb("over_g", [P, D], F32, st)
        self.over_total = k.sb("over_total", [P, D], F32, st)


def locate(k, o, pr, place_of, beside):
    nc = k.nc
    k.phase("slots")
    with ExitStack() as st:
        k.opened = k.sem("opened", st)
        rows = k.sb("rows", [P, T, 1], I32, st)
        own, apart = k.sb("own", [P, T], I32, st), k.sb("apart", [P, T], I32, st)
        located = k.sem("located", st)
        stages = [k.sb(f"stage{s}", [P, CH, 1], I32, st) for s in range(2)]
        idx = [k.sb(f"idx{s}", [P, CH], I32, st) for s in range(2)]
        staged, counted = k.sem("staged", st), k.sem("counted", st)
        sent = [k.sem(f"sent{s}", st) for s in range(2)]
        block = st.enter_context(nc.Block())

        @block.gpsimd
        def _(pool):
            pool.engine_nop().then_inc(k.opened, 1)
            pool.iota(own[:, :], [[1, T]], base=N, channel_multiplier=T).then_inc(counted, 1)
            pool.iota(apart[:, :], [[0, T]], base=N + SLOTS, channel_multiplier=1).then_inc(counted, 1)
            pool.wait_ge(located, 3)
            scatter_rows(pool, k, o.last_row, place_of, N - 1, stages, idx, staged, sent, rows_all=rows)

        @block.vector
        def _(dve):
            ch = Chain(dve, located)
            dve.wait_ge(counted, 2)
            ch.link(dve.tensor_tensor(apart[:, :], apart[:, :], own[:, :], ALU.subtract))
            ch.link(dve.tensor_tensor(apart[:, :], apart[:, :], o.over[:, :], ALU.mult))
            ch.link(dve.tensor_tensor(rows[:, :, 0], own[:, :], apart[:, :], ALU.add))

        beside(st, block)

    k.phase("find")
    with ExitStack() as st:
        k.opened = k.sem("opened", st)
        stages = [k.sb(f"stage{s}", [P, CH, 1, 1], I32, st) for s in range(2)]
        idx = [k.sb(f"idx{s}", [P, 1, CH], I32, st) for s in range(2)]
        run = k.sb("run", [P, T], F32, st)
        deg = k.sb("deg", [P, T], F32, st)
        deg_over = k.sb("deg_over", [P, T], F32, st)
        row_t = k.sb("row_t", [1, P + 1], F32, st)
        carry = k.sb("carry", [P, 1], F32, st)
        ps = [k.pb(f"ps{n}", [P, 512], F32, st) for n in range(2)]
        staged, chain, run_made, turned, scanned, back, root_made, rooted = (
            k.sem(n, st) for n in ("staged", "chain", "run_made", "turned", "scanned", "back", "root_made", "rooted"))
        landed = [k.sem(f"landed{s}", st) for s in range(2)]
        freed = [k.sem(f"freed{s}", st) for s in range(2)]
        block = st.enter_context(nc.Block())

        @block.gpsimd
        def _(pool):
            pool.engine_nop().then_inc(k.opened, 1)
            gather_rows(pool, k, place_of, N - 1, [o.other], stages, idx, staged, landed, freed, 1)

        @block.tensor
        def _(pe):
            pe.wait_ge(run_made, 1)
            pe.transpose(ps[0][0:1, 0:P], run[:, T - 1:T], k.ident[:, :]).then_inc(turned, 1)
            pe.wait_ge(scanned, 1)
            pe.transpose(ps[1][:, 0:1], row_t[:, 0:P], k.ident[0:1, 0:1]).then_inc(back, 1)

        @block.scalar
        def _(act):
            act.wait_ge(root_made, 1)
            act.activation(pr.root[:, :], deg[:, :], ACT.Sqrt).then_inc(rooted, 1)

        @block.vector
        def _(dve):
            ch = Chain(dve, chain)
            w = o.val["weight"][:, :, 0]
            ch.link(dve.memset(row_t[:, :], 0.0))
            dve.tensor_tensor_scan(out=run[:, :], data0=o.same[:, :], data1=w, initial=0.0, op0=ALU.mult,
                                   op1=ALU.add).then_inc(run_made, 1)
            dve.wait_ge(turned, 1)
            dve.tensor_tensor_scan(out=row_t[:, 1:P + 1], data0=o.whole[0:1, :], data1=ps[0][0:1, 0:P], initial=0.0,
                                   op0=ALU.mult, op1=ALU.add).then_inc(scanned, 1)
            dve.wait_ge(back, 1)
            ch.link(dve.tensor_copy(carry[:, :], ps[1][:, 0:1]))
            ch.link(dve.scalar_tensor_tensor(out=deg[:, :], in0=o.cont[:, :], scalar=carry[:, :], in1=run[:, :],
                                             op0=ALU.mult, op1=ALU.add))
            ch.link(dve.tensor_scalar(run[:, :], deg[:, :], 1.0, 1e-12, ALU.add, ALU.max))
            dve.tensor_copy(deg[:, :], run[:, :]).then_inc(root_made, 1)
            ch.link(dve.reciprocal(pr.inv[:, :], run[:, :]))
            ch.link(dve.tensor_tensor(deg_over[:, :], pr.inv[:, :], o.over[:, :], ALU.mult))
            ch.link(dve.tensor_reduce(pr.over_inv[:, :], deg_over[:, :], AX.X, ALU.add))
            dve.wait_ge(rooted, 1)
            ch.link(dve.reciprocal(pr.uproot[:, :], pr.root[:, :]))
            with dve.Fori(0, NIT) as i:
                for s in range(2):
                    c = 2 * i + s
                    dve.wait_ge(landed[s], (i + 1) * 16 * CH)
                    dve.tensor_scalar(pr.other[:, chunk_cols(c)], stages[s][:, :, 0, 0], 0.0, None,
                                      ALU.add).then_inc(freed[s], 1)


PARTS = 14
JM = 20
MBLK = N // (PD * JM)
assert MBLK * PD * JM == N


def slot_rows(table, q):
    w = T // PARTS * D
    return table.rearrange("(p t) f -> p (t f)", t=T)[:, bass.ds(q * w, w)]


def slot_cols(q):
    return bass.ds(q * (T // PARTS), T // PARTS)


def start_propagation(k, o, pr, x2, x2_slots):
    nc = k.nc
    k.phase("prop_init")
    with ExitStack() as st:
        k.opened = k.sem("opened", st)
        gb = [k.sb(f"rows{s}", [P, CH, 1, D], F32, st) for s in range(2)]
        idx = [k.sb(f"idx{s}", [P, 1, CH], I32, st) for s in range(2)]
        xc = k.sb("xc", [P, CH, D], F32, st)
        h = k.sb("h", [P, CH, D], F32, st)
        ln = ln_buffers(k, st, "ln", CH)
        staged, g_made, h_made, chain, over_chain = (
            k.sem(n, st) for n in ("staged", "g_made", "h_made", "chain", "over_chain"))
        landed = [k.sem(f"landed{s}", st) for s in range(2)]
        freed = [k.sem(f"freed{s}", st) for s in range(2)]
        block = st.enter_context(nc.Block())

        @block.gpsimd
        def _(pool):
            pool.engine_nop().then_inc(k.opened, 1)
            gather_rows(pool, k, x2, N - 1, [o.key], gb, idx, staged, landed, freed, 16)

        @block.sync
        def _(sp):
            with sp.Fori(0, NIT) as i:
                for s in range(2):
                    sp.wait_ge(h_made, 2 * i + (s + 1))
                    sp.dma_start(slot_rows(x2_slots, 2 * i + s), gb[s][:, :, :, :].rearrange("p t g f -> p (t g f)")
                                 ).then_inc(freed[s], 16)
            for s in range(2):
                sp.wait_ge(freed[s], NIT * 16)

        @block.scalar
        def _(act):
            with act.Fori(0, NCH) as c:
                ln_scalar(act, ln, xc[:, :, :], c)

        @block.vector
        def _(dve):
            ch = Chain(dve, chain, LN_LINKS)

            def turn(i):
                for s in range(2):
                    c = 2 * i + s
                    ch.turn(c)
                    dve.wait_ge(landed[s], (i + 1) * 16 * CH)
                    dve.wait_ge(k.opened, 1)
                    wait_for(dve, g_made, c)
                    ln_vector(dve, ch, ln, gb[s][:, :, 0, :], xc[:, :, :], h[:, :, :], c, 0.0).then_inc(h_made, 1)
                    dve.wait_ge(h_made, c + 1)
                    dve.tensor_tensor(pr.g[:, chunk_cols(c), :], h[:, :, :], spread(col_of(pr.uproot, c), P, CH, D),
                                      ALU.mult).then_inc(g_made, 1)

            turn(0)
            with dve.Fori(1, NIT) as i:
                turn(i)
            dve.wait_ge(g_made, NCH)
            ch4 = Chain(dve, over_chain)
            over = spread(o.over[:, :].rearrange("p (t o) -> p t o", o=1), P, T, D)
            ch4.link(dve.tensor_tensor(pr.total[:, :, :], pr.g[:, :, :], over, ALU.mult))
            ch4.link(dve.tensor_reduce(pr.over_g[:, :], pr.total[:, :, :].rearrange("p t f -> p f t"), AX.X, ALU.add))
            ch4.link(dve.tensor_scalar(pr.total[:, :, :], pr.g[:, :, :], 0.1 / 0.09 - 1.0, None, ALU.mult))
            ch4.link(dve.tensor_scalar(pr.over_total[:, :], pr.over_g[:, :], 0.1 / 0.09 - 1.0, None, ALU.mult))


def propagate(k, a, o, pr, tables, x2, x3, h3, steps=10):
    nc = k.nc
    k.phase("prop_steps")
    slot_tables = [t[N:N + SLOTS, :] for t in tables]
    assert PARTS == NCH and steps % 2 == 0
    with ExitStack() as st:
        k.opened = k.sem("opened", st)
        gb = [k.sb(f"rows{s}", [P, CH, 1, D], F32, st) for s in range(2)]
        idx = [k.sb(f"idx{s}", [P, 1, CH], I32, st) for s in range(2)]
        buf = k.sb("buf", [P, D, CH], F32, st)
        picked = k.sb("picked", [P, D, CH], F32, st)
        pick = k.sb("pick", [P, D], F32, st)
        over_sum = k.sb("over_sum", [P, D], F32, st)
        ps = k.pb("ps", [P, 512], F32, st)
        scan = Scan(k, st, "sum", o, D)
        ht, xt = ([k.sb(f"{n}{s}", [P, JM, D], F32, st) for s in range(2)] for n in ("ht", "xt"))
        mlp = Perceptron(k, st, JM, MBLK, ht, xt, xt, ht)
        assert MBLK == 2 * steps and 2 * mlp.groups + 4 <= NCH
        staged, chain0, chain, chain2, run_made, g_made, over_made, over_stored, stored, cleared = (
            k.sem(n, st) for n in ("staged", "chain0", "chain", "chain2", "run_made", "g_made", "over_made",
                                   "over_stored", "stored", "cleared"))
        landed, freed, loaded, moved = ([k.sem(f"{n}{s}", st) for s in range(2)]
                                        for n in ("landed", "freed", "loaded", "moved"))
        block = st.enter_context(nc.Block())

        @block.gpsimd
        def _(pool):
            pool.engine_nop().then_inc(k.opened, 1)
            limits = bound_register(pool, k, N + SLOTS + P - 1)

            def step(n, table):
                gather_rows(pool, k, table, None, [pr.other], gb, idx, staged, landed, freed, 1,
                            turn0=n * NIT, limits=limits,
                            ready=((stored, (n + 1) * 16 * PARTS), (over_stored, (n + 1) * 16)))

            step(0, tables[0])
            step(1, tables[1])
            with pool.Fori(1, steps // 2) as half:
                for q in range(2):
                    step(2 * half + q, tables[q])

        @block.sync
        def _(sp):
            def load(c, s):
                for source, tiles in ((tables[0], ht), (x2, xt)):
                    sp.dma_start(flat(tiles[s][0:PD, :, :]), node_block(source, c, JM)).then_inc(loaded[s], 16)

            def store(c, s, so_far, times):
                sp.wait_ge(mlp.made, so_far)
                for to, tiles in ((h3, ht), (x3, xt)):
                    sp.dma_start(node_block(to, c, JM), flat(tiles[s][0:PD, :, :])).then_inc(moved[s], 16)
                sp.wait_ge(moved[s], times * 32)

            def store_slots(n, to, chunks):
                for c in chunks:
                    sp.wait_ge(g_made, n * NCH + (c + 1))
                    sp.dma_start(slot_rows(slot_tables[to], c), flat(pr.g[:, slot_cols(c), :])).then_inc(stored, 16)

            def store_over(n, to):
                sp.wait_ge(over_made, n + 1)
                sp.dma_start(tables[to][N + SLOTS:N + SLOTS + P, :], pr.over_g[:, :]).then_inc(over_stored, 16)

            def step(n, q):
                last = isinstance(n, int) and n == steps - 1
                if not last:
                    store_slots(n, 1 - q, range(0, 6))
                if not isinstance(n, int) or n > 0:
                    store(2 * n - 1, 1, 2 * n, n)
                    load(2 * n + 1, 1)
                if not last:
                    store_slots(n, 1 - q, range(6, 11))
                store(2 * n, 0, 2 * n + 1, n + 1)
                if not last:
                    load(2 * n + 2, 0)
                    store_slots(n, 1 - q, range(11, NCH))
                    store_over(n, 1 - q)

            for c in range(NCH):
                sp.dma_start(slot_rows(slot_tables[0], c), flat(pr.g[:, slot_cols(c), :])).then_inc(stored, 16)
            sp.dma_start(tables[0][N + SLOTS:N + SLOTS + P, :], pr.over_g[:, :]).then_inc(over_stored, 16)
            sp.wait_ge(cleared, 4)
            for s in range(2):
                load(s, s)
            mlp.load_weights(sp, a)
            step(0, 0)
            step(1, 1)
            with sp.Fori(1, steps // 2 - 1) as half:
                for q in range(2):
                    step(2 * half + q, q)
            step(steps - 2, 0)
            step(steps - 1, 1)
            store(MBLK - 1, 1, MBLK, steps)
            sp.wait_ge(stored, steps * PARTS * 16)
            sp.wait_ge(over_stored, steps * 16)

        @block.tensor
        def _(pe):
            def turn(step):
                for s in range(2):
                    pe.wait_ge(loaded[s], (step + 1) * 32)
                    mlp.tensor_block(pe, 2 * step + s, s)
                pe.wait_ge(run_made, (step + 1) * NCH)
                scan.carries_tensor(pe, ps, step)

            pe.wait_ge(mlp.w_landed, mlp.WEIGHTS)
            turn(0)
            with pe.Fori(1, steps) as step:
                turn(step)
            mlp.tensor_rest(pe)

        @block.scalar
        def _(act):
            act.wait_ge(mlp.w_landed, mlp.WEIGHTS)
            for s in range(2):
                mlp.scalar_block(act, s, s)
            with act.Fori(1, steps) as step:
                for s in range(2):
                    mlp.scalar_block(act, 2 * step + s, s)
            mlp.scalar_rest(act)

        @block.vector
        def _(dve):
            clear_blocks(dve, ht + xt, cleared)
            scan.prepare(dve, Chain(dve, chain0))
            dve.wait_ge(mlp.w_landed, mlp.WEIGHTS)
            ch = Chain(dve, chain, 5 + Scan.LINKS)
            ch2 = Chain(dve, chain2, 4)
            ch3 = Chain(dve, mlp.chain, LN_LINKS)
            G, LAG = mlp.groups, 4

            def nodes(c, step):
                before = not isinstance(step, int) or step > 0
                m = c - LAG
                if m < 0:
                    if before:
                        mlp.add(dve, 2 * step - 1, m + G, 1)
                elif m < 2 * G - LAG:
                    s, g = m // G, m % G
                    if g == 0:
                        dve.wait_ge(loaded[s], (step + 1) * 32)
                        mlp.bias(dve, 2 * step + s, s)
                    mlp.add(dve, 2 * step + s, g, s)
                for end, there, block_c, s in ((LAG - 1, before, 2 * step - 1, 1), (LAG + G - 1, True, 2 * step, 0)):
                    if there and c == end:
                        mlp.centre(dve, ch3, block_c, s)
                    if there and c == end + 1:
                        mlp.var(dve, ch3, block_c)
                    if there and c == end + 2:
                        mlp.scale(dve, ch3, block_c, s)

            def turn(step):
                for c in range(NCH):
                    s, i = c % 2, c // 2
                    at = step * NCH + c
                    ch.turn(at)
                    g = pr.g[:, chunk_cols(c), :]
                    dve.wait_ge(stored, (step + 1) * 16 * PARTS)
                    ch.link(dve.tensor_tensor(pr.total[:, chunk_cols(c), :], pr.total[:, chunk_cols(c), :], g, ALU.add))
                    dve.wait_ge(landed[s], (step * NIT + (i + 1)) * 16 * CH)
                    weight = o.val["weight"][:, chunk_cols(c), :].rearrange("p t o -> p o t")
                    dve.tensor_tensor(buf[:, :, :], gb[s][:, :, 0, :].rearrange("p t f -> p f t"),
                                      weight.to_broadcast([P, D, CH]), ALU.mult).then_inc(freed[s], 1)
                    dve.wait_ge(freed[s], step * NIT + (i + 1))
                    scan.chunk(dve, ch, buf[:, :, :], c, run_made, turn=at)
                    ch.link(dve.tensor_tensor(g, g, buf[:, :, :].rearrange("p f t -> p t f"), ALU.add))
                    dve.tensor_tensor(g, g, spread(col_of(pr.inv, c), P, CH, D), ALU.mult).then_inc(g_made, 1)
                    over = o.over[:, chunk_cols(c)].rearrange("p (o t) -> p o t", o=1).to_broadcast([P, D, CH])
                    ch.link(dve.tensor_tensor(picked[:, :, :], buf[:, :, :], over, ALU.mult))
                    if c == 0:
                        ch.link(dve.tensor_reduce(over_sum[:, :], picked[:, :, :], AX.X, ALU.add))
                        ch.link(dve.tensor_copy(pick[:, :], over_sum[:, :]))
                    else:
                        ch.link(dve.tensor_reduce(pick[:, :], picked[:, :, :], AX.X, ALU.add))
                        ch.link(dve.tensor_tensor(over_sum[:, :], over_sum[:, :], pick[:, :], ALU.add))
                    nodes(c, step)
                    dve.wait_ge(g_made, at + 1)
                ch2.turn(step)
                ch2.link(scan.carries_vector(dve, ps, step))
                dve.wait_ge(over_stored, (step + 1) * 16)
                ch2.link(dve.tensor_tensor(pr.over_total[:, :], pr.over_total[:, :], pr.over_g[:, :], ALU.add))
                ch2.link(dve.tensor_tensor(over_sum[:, :], over_sum[:, :], scan.carry[:, 0:D], ALU.add))
                ch2.link(dve.tensor_tensor(pick[:, :], pr.over_g[:, :], over_sum[:, :], ALU.add))
                dve.tensor_scalar(pr.over_g[:, :], pick[:, :], pr.over_inv[:, :], None, ALU.mult).then_inc(over_made, 1)
                dve.wait_ge(over_made, step + 1)

            turn(0)
            with dve.Fori(1, steps) as step:
                turn(step)
            for g in range(G - LAG, G):
                mlp.add(dve, MBLK - 1, g, 1)
            mlp.centre(dve, ch3, MBLK - 1, 1)
            mlp.var(dve, ch3, MBLK - 1)
            mlp.scale(dve, ch3, MBLK - 1, 1)


def slot_pass(k, a, o, pr, x2_slots, x3, h3, aggs):
    nc = k.nc
    k.phase("slot_pass")
    with ExitStack() as st:
        k.opened = k.sem("opened", st)
        pt, xt, x3t, h3t = ([k.sb(f"{n}{s}", [P, CH, D], F32, st) for s in range(2)] for n in ("pt", "xt", "x3t", "h3t"))
        idx = [k.sb(f"idx{s}", [P, CH], I32, st) for s in range(2)]
        share = k.sb("share", [P, T], F32, st)
        mlp = Perceptron(k, st, CH, NCH, pt, xt, x3t, h3t)
        G = mlp.groups
        over_share = k.sb("over_share", [P, T], F32, st)
        over_p = k.sb("over_p", [P, D], F32, st)
        over_rows = k.sb("over_rows", [P, CH, D], F32, st)
        chain2 = k.sem("chain2", st)
        zeros = k.sb("zeros", [P, 1000], F32, st)
        staged, shared, summed, p_made, zeroed, cleared = (
            k.sem(n, st) for n in ("staged", "shared", "summed", "p_made", "zeroed", "cleared"))
        loaded, sent = ([k.sem(f"{n}{s}", st) for s in range(2)] for n in ("loaded", "sent"))
        block = st.enter_context(nc.Block())

        @block.gpsimd
        def _(pool):
            pool.engine_nop().then_inc(k.opened, 1)
            limit, set_limit = bound_register(pool, k, N - 1)

            def turn(i):
                for s in range(2):
                    wait_for(pool, sent[s], i * 32 * CH)
                    pool.wait_ge(k.opened, 1)
                    pool.tensor_copy(idx[s][:, :], o.last_row[:, chunk_cols(2 * i + s)]).then_inc(staged, 1)
                    pool.wait_ge(staged, 2 * i + (s + 1))
                    pool.wait_ge(mlp.made, 2 * i + (s + 1))
                    set_limit()
                    for t in range(CH):
                        for table, tile in ((x3, mlp.x3t[s]), (h3, mlp.h3t[s])):
                            pool.indirect_dma_start(
                                table, bass.IndirectOffsetOnAxis(ap=idx[s][:, t:t + 1], axis=0),
                                tile[:, t, :], None, bounds_check=limit, oob_is_err=False).then_inc(sent[s], 16)

            turn(0)
            with pool.Fori(1, NIT) as i:
                turn(i)
            for s in range(2):
                pool.wait_ge(sent[s], NIT * 32 * CH)

        @block.sync
        def _(sp):
            mlp.load_weights(sp, a)
            sp.wait_ge(zeroed, 1)
            for s in range(2):
                sp.dma_start(flat(xt[s][:, :, :]), slot_rows(x2_slots, s)).then_inc(loaded[s], 16)
            for table in aggs:
                sp.dma_start(table.rearrange("n f -> (n f)").rearrange("(p r w) -> p r w", p=P, w=1000),
                             zeros[:, :].rearrange("p (o w) -> p o w", o=1).to_broadcast([P, N * D // P // 1000, 1000])
                             ).then_inc(cleared, 16)
            with sp.Fori(0, NIT - 1) as i:
                for s in range(2):
                    sp.wait_ge(mlp.x3_made, (2 * i + (s + 1)) * G)
                    sp.dma_start(flat(xt[s][:, :, :]), slot_rows(x2_slots, 2 * i + (s + 2))).then_inc(loaded[s], 16)
            for s in range(2):
                sp.wait_ge(loaded[s], NIT * 16)
            sp.wait_ge(cleared, 16 * len(aggs))

        @block.tensor
        def _(pe):
            def turn(i):
                for s in range(2):
                    pe.wait_ge(p_made, 2 * i + (s + 1))
                    mlp.tensor_block(pe, 2 * i + s, s)

            pe.wait_ge(mlp.w_landed, mlp.WEIGHTS)
            turn(0)
            with pe.Fori(1, NIT) as i:
                turn(i)
            mlp.tensor_rest(pe)

        @block.scalar
        def _(act):
            act.wait_ge(mlp.w_landed, mlp.WEIGHTS)
            for s in range(2):
                mlp.scalar_block(act, s, s)
            with act.Fori(1, NIT) as i:
                for s in range(2):
                    mlp.scalar_block(act, 2 * i + s, s)
            mlp.scalar_rest(act)

        @block.vector
        def _(dve):
            dve.memset(zeros[:, :], 0.0).then_inc(zeroed, 1)
            dve.wait_ge(mlp.w_landed, mlp.WEIGHTS)
            ch1 = Chain(dve, shared)
            ch1.link(dve.tensor_scalar(share[:, :], pr.root[:, :], 0.09, None, ALU.mult))
            ch1.link(dve.tensor_tensor(over_share[:, :], share[:, :], o.over[:, :], ALU.mult))
            ch1.link(dve.tensor_tensor(share[:, :], share[:, :], over_share[:, :], ALU.subtract))
            ch1.link(dve.tensor_tensor(over_p[:, :], pr.over_total[:, :], pr.over_g[:, :], ALU.add))
            ch2 = Chain(dve, chain2, 2)
            ch = Chain(dve, mlp.chain, LN_LINKS)

            def build(c, s):
                wait_for(dve, mlp.turned, (c - 1) * G)
                dve.tensor_tensor(pt[s][:, :, :], pr.total[:, chunk_cols(c), :], pr.g[:, chunk_cols(c), :],
                                  ALU.add).then_inc(summed, 1)
                dve.wait_ge(summed, c + 1)
                ch2.turn(c)
                ch2.link(dve.tensor_tensor(pt[s][:, :, :], pt[s][:, :, :], spread(col_of(share, c), P, CH, D), ALU.mult))
                ch2.link(dve.tensor_tensor(over_rows[:, :, :], spread(col_of(over_share, c), P, CH, D),
                                           spread(across(over_p, D), P, CH, D), ALU.mult))
                dve.tensor_tensor(pt[s][:, :, :], pt[s][:, :, :], over_rows[:, :, :], ALU.add).then_inc(p_made, 1)

            def chunk(c, i, s, more):
                if more:
                    build(c + 1, 1 - s)
                dve.wait_ge(loaded[s], (i + 1) * 16)
                mlp.bias(dve, c, s)
                wait_for(dve, sent[s], i * 32 * CH)
                for g in range(G):
                    mlp.add(dve, c, g, s)
                mlp.centre(dve, ch, c, s)
                mlp.var(dve, ch, c)
                mlp.scale(dve, ch, c, s)

            build(0, 0)
            for s in range(2):
                chunk(s, 0, s, True)
            with dve.Fori(1, NIT - 1) as i:
                for s in range(2):
                    chunk(2 * i + s, i, s, True)
            chunk(NCH - 2, NIT - 1, 0, True)
            chunk(NCH - 1, NIT - 1, 1, False)


def root_pass(k, h, root, bias, adds, y, relu):
    nc = k.nc
    k.phase("root")
    PAIRS = (J + 1) // 2
    GROUP = 4
    groups = [range(q, min(q + GROUP, PAIRS)) for q in range(0, PAIRS, GROUP)]
    NR = len(groups)
    assert NR % 2 == 0
    with ExitStack() as st:
        ht, yt = ([k.sb(f"{n}{s}", [P, J + 1, D], F32, st) for s in range(2)] for n in ("ht", "yt"))
        at = [[k.sb(f"add{q}_{s}", [P, J + 1, D], F32, st) for s in range(2)] for q in range(len(adds))]
        w = k.sb("w", [P, P], F32, st)
        b = k.sb("b", [P, 1, D], F32, st)
        turned_h = k.sb("turned_h", [P, 2, GROUP, P], F32, st)
        ps_t = [k.pb(f"ps_t{n}", [P, 512], F32, st) for n in range(2)]
        ps_y = [k.pb(f"ps_y{n}", [P, 512], F32, st) for n in range(2)]
        chain, made, cleared, w_clear, w_landed, turned, copied, y_made, y_read = (
            k.sem(n, st) for n in ("chain", "made", "cleared", "w_clear", "w_landed", "turned", "copied", "y_made",
                                   "y_read"))
        loaded, stored = ([k.sem(f"{n}{s}", st) for s in range(2)] for n in ("loaded", "stored"))
        block = st.enter_context(nc.Block())

        @block.sync
        def _(sp):
            sp.wait_ge(w_clear, 1)
            for q in range(2):
                sp.dma_start(w[q * D:(q + 1) * D, q * D:(q + 1) * D], root).then_inc(w_landed, 16)
            sp.dma_start(b[:, 0, :], row(bias).to_broadcast([P, D])).then_inc(w_landed, 16)
            sp.wait_ge(w_landed, 48)
            move_blocks(sp, [(h, ht), *zip(adds, at)], [(y, yt)], loaded, [(turned, NR), (y_read, NR)], made, stored,
                        cleared)

        @block.tensor
        def _(pe):
            def turn_rows(n, g, s):
                wait_for(pe, copied, n + (g - 1))
                for q, pair in enumerate(groups[g]):
                    last = pe.transpose(ps_t[g % 2][:, q * P:(q + 1) * P],
                                        ht[s][:, 2 * pair:2 * pair + 2, :].rearrange("p j f -> p (j f)"), k.ident[:, :])
                last.then_inc(turned, 1)

            def multiply(count, g):
                pe.wait_ge(copied, count + 1)
                wait_for(pe, y_read, count - 1)
                for q in range(len(groups[g])):
                    last = pe.matmul(ps_y[g % 2][:, q * P:(q + 1) * P], turned_h[:, g % 2, q, :], w[:, :],
                                     start=True, stop=True)
                last.then_inc(y_made, 1)

            def turn(i):
                for s in range(2):
                    n = (2 * i + s) * NR
                    pe.wait_ge(loaded[s], (i + 1) * 16 * (1 + len(adds)))
                    for g in range(NR):
                        turn_rows(n, g, s)
                        if not isinstance(i, int) or n + g > 0:
                            multiply(n + (g - 1), (g - 1) % NR)

            pe.wait_ge(w_landed, 48)
            turn(0)
            with pe.Fori(1, NBLK // 2) as i:
                turn(i)
            multiply(NBLK * NR - 1, NR - 1)

        @block.scalar
        def _(act):
            def copy(c):
                for g in range(NR):
                    act.wait_ge(turned, c * NR + g + 1)
                    wait_for(act, y_made, c * NR + (g - 1))
                    wide = len(groups[g]) * P
                    act.activation(turned_h[:, g % 2, 0:len(groups[g]), :].rearrange("p q n -> p (q n)"),
                                   ps_t[g % 2][:, 0:wide], ACT.Copy).then_inc(copied, 1)

            copy(0)
            with act.Fori(1, NBLK) as c:
                copy(c)

        @block.vector
        def _(dve):
            dve.memset(w[:, :], 0.0).then_inc(w_clear, 1)
            clear_blocks(dve, [x for xs in [ht, *at] for x in xs], cleared)
            dve.wait_ge(w_landed, 48)
            ch = Chain(dve, chain, 2 * len(adds))
            def turn(i):
                ch.turn(i)
                for s in range(2):
                    c = 2 * i + s
                    n = c * NR
                    dve.wait_ge(loaded[s], (i + 1) * 16 * (1 + len(adds)))
                    base = at[0][s]
                    ch.link(dve.tensor_tensor(base[:, :, :], base[:, :, :], spread(b[:, :, :], P, J + 1, D), ALU.add))
                    for more in at[1:]:
                        ch.link(dve.tensor_tensor(base[:, :, :], base[:, :, :], more[s][:, :, :], ALU.add))
                    wait_for(dve, stored[s], i * 16)
                    for g in range(NR):
                        dve.wait_ge(y_made, n + g + 1)
                        nodes = slice(2 * groups[g][0], 2 * groups[g][-1] + 2)
                        wide = len(groups[g]) * P
                        dve.tensor_tensor(yt[s][:, nodes, :], ps_y[g % 2][:, 0:wide].rearrange("p (j f) -> p j f", f=D),
                                          base[:, nodes, :], ALU.add).then_inc(y_read, 1)
                    dve.wait_ge(y_read, n + NR)
                    if relu:
                        dve.tensor_scalar(yt[s][:, :, :], yt[s][:, :, :], 0.0, None, ALU.max).then_inc(made, 1)
                    else:
                        dve.tensor_scalar(yt[s][:, 0:1, :], yt[s][:, 0:1, :], 1.0, None, ALU.mult).then_inc(made, 1)

            turn(0)
            with dve.Fori(1, NBLK // 2) as i:
                turn(i)


K5 = 5


class Spline:

    def __init__(self, k, st, o):
        nc = k.nc
        k.phase("spline")
        self.knots = k.sb("knots", [P, T, 2, K5], F32, st)
        with ExitStack() as tmp:
            v = k.sb("v", [P, 2 * T], F32, tmp)
            x = k.sb("x", [P, 2 * T], F32, tmp)
            y = k.sb("y", [P, 2 * T], F32, tmp)
            chain = k.sem("chain", tmp)
            block = tmp.enter_context(nc.Block())

            @block.vector
            def _(dve):
                ch = Chain(dve, chain)
                pseudo = o.val["pseudo"][:, :, :].rearrange("p t d -> p (t d)")
                ch.link(dve.tensor_scalar(x[:, :], pseudo, float(K5 - 1), 0.0, ALU.mult, ALU.max))
                ch.link(dve.tensor_scalar(v[:, :], x[:, :], float(K5 - 1), None, ALU.min))
                for n in range(K5):
                    ch.link(dve.tensor_scalar(x[:, :], v[:, :], float(-n), None, ALU.add))
                    ch.link(dve.scalar_tensor_tensor(out=y[:, :], in0=x[:, :], scalar=-1.0, in1=x[:, :], op0=ALU.mult,
                                                     op1=ALU.max))
                    ch.link(dve.tensor_scalar(x[:, :], y[:, :], -1.0, 1.0, ALU.mult, ALU.add))
                    ch.link(dve.tensor_scalar(self.knots[:, :, :, n].rearrange("p t d -> p (t d)"), x[:, :], 0.0, None,
                                              ALU.max))


def conv(k, o, spline, h, weight, agg):
    with ExitStack() as st:
        k.phase("conv")
        scan = Scan(k, st, "max", o, D, largest=True)
        sender = Sender(k, st, o, scan)
        conv_rows(k, o, spline, h, weight, scan, sender, agg)


def conv_rows(k, o, spline, h, weight, scan, sender, agg):
    nc = k.nc
    k.phase("conv_rows")
    W = K5 * D
    with ExitStack() as st:
        k.opened = k.sem("opened", st)
        gb = [k.sb(f"rows{s}", [P, CH, 1, D], F32, st) for s in range(2)]
        idx = [k.sb(f"idx{s}", [P, 1, CH], I32, st) for s in range(2)]
        w = k.sb("w", [P, 3, W], F32, st)
        z4 = [k.sb(f"z4_{s}", [P, CH, 4, D], F32, st) for s in range(2)]
        z1 = [k.sb(f"z1_{s}", [P, CH, D], F32, st) for s in range(2)]
        zt = k.sb("zt", [P, 2, K5 * P], F32, st)
        prod = k.sb("prod", [P, 2, K5, D], F32, st)
        buf = [k.sb(f"buf{s}", [P, D, CH], F32, st) for s in range(2)]
        ps_z = k.pb("ps_z", [P, 1024], F32, st)
        ps_c = k.pb("ps_c", [P, 512], F32, st)
        ps_m = [k.pb(f"ps_m{n}", [P, 1024], F32, st) for n in range(2)]
        staged, chain0, chain, w_landed, turned, zt_made, m_made, m_read, reduced, run_made = (
            k.sem(n, st) for n in ("staged", "chain0", "chain", "w_landed", "turned", "zt_made", "m_made",
                                   "m_read", "reduced", "run_made"))
        landed = [k.sem(f"landed{s}", st) for s in range(2)]
        z_made = [k.sem(f"z_made{s}", st) for s in range(2)]
        block = st.enter_context(nc.Block())

        @block.gpsimd
        def _(pool):
            pool.engine_nop().then_inc(k.opened, 1)
            gather_and_send(pool, k, h, [o.other], gb, idx, staged, landed, z_made, GROUPS, sender, agg)

        @block.sync
        def _(sp):
            by_knot = weight.rearrange("(k1 k0) i o -> k0 i k1 o", k0=K5)
            for c, q, k0 in ((0, 0, 0), (0, 1, 1), (1, 0, 2), (1, 1, 3), (2, 0, 4), (2, 1, 4)):
                sp.dma_start(w[q * D:(q + 1) * D, c, :].rearrange("p (k o) -> p k o", k=K5),
                             by_knot[k0]).then_inc(w_landed, 16)
            sp.wait_ge(w_landed, 96)

        @block.tensor
        def _(pe):
            def turn_z(n, g, s):
                wait_for(pe, zt_made, n + g)
                for e in range(2):
                    for q in range(2):
                        pe.transpose(ps_z[:, (2 * e + q) * P:(2 * e + q + 1) * P],
                                     z4[s][:, 2 * g + e, 2 * q:2 * q + 2, :].rearrange("p n f -> p (n f)"), k.ident[:, :])
                pe.transpose(ps_z[:, 4 * P:5 * P], z1[s][:, 2 * g:2 * g + 2, :].rearrange("p t f -> p (t f)"),
                             k.ident[:, :]).then_inc(turned, 1)

            def multiply(pair, ring):
                pe.wait_ge(zt_made, pair + 1)
                wait_for(pe, m_read, pair - 1)
                to = [ps_m[ring][:, e * 512:e * 512 + W] for e in range(2)]
                for e in range(2):
                    for q in range(2):
                        pe.matmul(to[e], zt[:, ring, (2 * e + q) * P:(2 * e + q + 1) * P], w[:, q, :],
                                  start=q == 0, stop=False)
                for e in range(2):
                    rows = slice(e * D, (e + 1) * D)
                    last = pe.matmul(to[e], zt[rows, ring, 4 * P:5 * P], w[rows, 2, :], start=False, stop=True)
                last.then_inc(m_made, 1)

            def turn(i):
                for s in range(2):
                    n = (2 * i + s) * GROUPS
                    for g in range(GROUPS):
                        pe.wait_ge(z_made[s], i * GROUPS + (g + 1))
                        turn_z(n, g, s)
                        if not isinstance(i, int) or n + g > 0:
                            multiply(n + g - 1, (s * GROUPS + g + 1) % 2)

            pe.wait_ge(w_landed, 96)
            turn(0)
            with pe.Fori(1, NIT) as i:
                turn(i)
            multiply(NCH * GROUPS - 1, 1)
            pe.wait_ge(run_made, NCH)
            scan.carries_tensor(pe, ps_c)

        @block.scalar
        def _(act):
            def chunk(c, s):
                for g in range(GROUPS):
                    act.wait_ge(turned, c * GROUPS + g + 1)
                    wait_for(act, m_made, c * GROUPS + (g - 1))
                    act.activation(zt[:, (s * GROUPS + g) % 2, :], ps_z[:, 0:K5 * P], ACT.Copy).then_inc(zt_made, 1)

            chunk(0, 0)
            chunk(1, 1)
            with act.Fori(1, NIT) as i:
                for s in range(2):
                    chunk(2 * i + s, s)

        @block.vector
        def _(dve):
            ch0 = Chain(dve, chain0)
            scan.prepare(dve, ch0)
            sender.prepare(dve, ch0)
            sender.start(dve)
            ch = Chain(dve, chain, 2 * Scan.LINKS)

            def build(c, s, g, turn):
                if g == 0:
                    dve.wait_ge(landed[s], turn * 16 * CH)
                    wait_for(dve, turned, (c - 1) * GROUPS)
                    dve.wait_ge(k.opened, 1)
                pair = slice(2 * g, 2 * g + 2)
                first = spline.knots[:, bass.ds(c * CH + 2 * g, 2), 0, :]
                rows = gb[s][:, pair, :, :]
                dve.tensor_tensor(z4[s][:, pair, :, :],
                                  first[:, :, 0:4].rearrange("p t (n o) -> p t n o", o=1).to_broadcast([P, 2, 4, D]),
                                  rows.to_broadcast([P, 2, 4, D]), ALU.mult)
                dve.tensor_tensor(z1[s][:, pair, :], first[:, :, 4:5].to_broadcast([P, 2, D]), rows[:, :, 0, :],
                                  ALU.mult).then_inc(z_made[s], 1)

            def chunk(c, i, s, turn):
                for g in range(GROUPS):
                    n = c * GROUPS + g
                    dve.wait_ge(m_made, n + 1)
                    wait_for(dve, reduced, n)
                    second = spline.knots[:, bass.ds(c * CH + 2 * g, 2), 1, :]
                    dve.tensor_tensor(prod[:, :, :, :],
                                      ps_m[(s * GROUPS + g) % 2][:, :].rearrange("p (e w) -> p e w", e=2)[:, :, 0:W].rearrange(
                                          "p e (n f) -> p e n f", f=D),
                                      second.rearrange("p t (n o) -> p t n o", o=1).to_broadcast([P, 2, K5, D]),
                                      ALU.mult).then_inc(m_read, 1)
                    if turn is not None:
                        build(c + 1, 1 - s, g, turn)
                    dve.wait_ge(m_read, n + 1)
                    dve.tensor_reduce(buf[s][:, :, 2 * g:2 * g + 2].rearrange("p f t -> p t f"),
                                      prod[:, :, :, :].rearrange("p e n f -> p e f n"), AX.X,
                                      ALU.add).then_inc(reduced, 1)
                    if g < Sender.PARTS and (not isinstance(c, int) or c > 0):
                        sender.vector_part(dve, g, c - 1, i - 1 + s, 1 - s, buf[1 - s][:, :, :])
                dve.wait_ge(reduced, (c + 1) * GROUPS)
                scan.chunk(dve, ch, buf[s][:, :, :], c, run_made)

            def turn(i):
                ch.turn(i)
                for s in range(2):
                    chunk(2 * i + s, i, s, i + 1 + s)

            for g in range(GROUPS):
                build(0, 0, g, 1)
            turn(0)
            with dve.Fori(1, NIT - 1) as i:
                turn(i)
            ch.turn(NIT - 1)
            chunk(NCH - 2, NIT - 1, 0, NIT)
            chunk(NCH - 1, NIT - 1, 1, None)
            sender.vector_chunk(dve, NCH - 1, NIT - 1, 1, buf[1][:, :, :])
            sender.vector_end(dve, ps_c)


def gnn_kernel(nc, a, out):
    with ExitStack() as stack:
        k = Core(nc, stack)
        k.phase("all")
        constants(k)
        s, d = "src", "dst"
        k.rec_dram = {o: [nc.dram_tensor(f"rec_{o}{i}", (SLOTS, REC), I32, kind="Internal").ap() for i in range(2)]
                      for o in (s, d)}
        x1, x2 = (nc.dram_tensor(n, (N, D), F32, kind="Internal").ap() for n in ("x1", "x2"))
        place_of = nc.dram_tensor("place_of", (N, 1), I32, kind="Internal").ap()
        tables = [nc.dram_tensor(f"table{n}", (N + SLOTS + P, D), F32, kind="Internal").ap() for n in range(2)]
        agg = [nc.dram_tensor(f"agg{n}", (N, D), F32, kind="Internal").ap() for n in range(2)]
        with ExitStack() as st:
            rec = {o: k.sb(f"rec_{o}", [P, T, REC], I32, st) for o in (s, d)}
            place = {o: k.sb(f"place_{o}", [P, T], I32, st) for o in (s, d)}
            load_records(k, a[s], a[d], [(a["edge_weight"].bitcast(I32).rearrange("(e w) -> e w", w=1), 1)], rec[s])
            load_records(k, a[d], a[s], [(a["edge_attr_2"].bitcast(I32), 2), (a["edge_attr_8"].bitcast(I32), 8)],
                         rec[d])
            sort_step(k, (rec[s], place[s], 0, None))
            sort_step(k, (rec[d], place[d], 0, None), (rec[s], place[s], k.rec_dram[s][0]))
            sort_step(k, (rec[s], place[s], 8, k.rec_dram[s][0]), (rec[d], place[d], k.rec_dram[d][0]))
            sort_step(k, (rec[d], place[d], 8, k.rec_dram[d][0]), (rec[s], place[s], k.rec_dram[s][1]),
                      beside=lambda st, block: copy_rows(k, st, block, a["x"], x1))
            sort_step(k, None, (rec[d], place[d], k.rec_dram[d][1]), beside=lambda st, block: own_rows(k, st, block, place_of))
        by_src = Order(k, "by_src", [("weight", 1)])
        build_order(k, by_src, k.rec_dram[s][1])
        layer0(k, a, by_src, x1)
        by_dst = Order(k, "by_dst", [("pseudo", 2), ("basis", 8)])
        build_order(k, by_dst, k.rec_dram[d][1])
        k.recycle()
        layer1(k, a, by_dst, x1, x2)
        k.recycle()
        x2_slots = nc.dram_tensor("x2_slots", (SLOTS, D), F32, kind="Internal").ap()
        x3, h3, h4 = (nc.dram_tensor(n, (N, D), F32, kind="Internal").ap() for n in ("x3", "h3", "h4"))
        with ExitStack() as st:
            pr = Propagation(k, st)
            locate(k, by_src, pr, place_of, lambda st, block: norm_nodes(k, st, block, x2, [t[0:N, :] for t in tables]))
            start_propagation(k, by_src, pr, x2, x2_slots)
            propagate(k, a, by_src, pr, tables, x2, x3, h3)
            k.recycle()
            slot_pass(k, a, by_src, pr, x2_slots, x3, h3, agg)
        k.recycle()
        spline = Spline(k, stack, by_dst)
        conv(k, by_dst, spline, h3, a["L3_gnn_W1"], agg[0])
        root_pass(k, h3, a["L3_gnn_root1"], a["L3_gnn_bias1"], [agg[0]], h4, True)
        k.recycle()
        conv(k, by_dst, spline, h4, a["L3_gnn_W2"], agg[1])
        root_pass(k, h4, a["L3_gnn_root2"], a["L3_gnn_bias2"], [x3, agg[1]], out, False)


def kernel(**inputs):
    import concourse.bacc as bacc
    from concourse.bass_utils import run_bass_kernel_spmd

    nc = bacc.Bacc("TRN2", target_bir_lowering=False, num_devices=1)
    arrays, args = {}, {}
    for name, value in inputs.items():
        value = np.ascontiguousarray(value)
        arrays[f"in_{name}_dram"] = value
        args[name] = nc.dram_tensor(f"in_{name}_dram", value.shape, mybir.dt.from_np(value.dtype),
                                    kind="ExternalInput").ap()
    out = nc.dram_tensor("out_0_dram", (N, D), F32, kind="ExternalOutput").ap()
    gnn_kernel(nc, args, out)
    return run_bass_kernel_spmd(nc, [arrays], core_ids=[0]).results[0]["out_0_dram"]
```
